# Optimizing a Trainium2 kernel written in Bass

```python
import numpy as np
import jax
import jax.numpy as jnp

def _softmax(x, axis=-1):
    return jax.nn.softmax(x, axis=axis)

def _gelu(x):
    return jax.nn.gelu(x, approximate=True)

def _silu(x):
    return jax.nn.silu(x)

def _sigmoid(x):
    return jax.nn.sigmoid(x)

def _layernorm(x, axis=-1, eps=1e-05):
    m = jnp.mean(x, axis=axis, keepdims=True)
    v = jnp.var(x, axis=axis, keepdims=True)
    return (x - m) / jnp.sqrt(v + eps)

def _scatter_add(tgt, idx, src, axis=0):
    return tgt.at[idx].add(src)

def _segment_sum(src, seg, n):
    return jax.ops.segment_sum(src, seg, n)
kernel_name = 'mk_perceiver_d1_seqx_r4_d00461'

def setup_inputs(seed: int=0):
    np.random.seed(seed)
    _w = jnp.asarray

    def _rec_inputs():
        import jax
        import jax.numpy as jnp
        _rk = jax.random.key(seed)
        x = -0.0002928 + 1 * jax.random.normal(jax.random.fold_in(_rk, 1), (64, 32, 256), jnp.float32)
        _lenS = 32 - jax.random.randint(jax.random.fold_in(_rk, 7), (64,), 0, max(1, 32 // 4) + 1, jnp.int32)
        _lenS2 = 257 - jax.random.randint(jax.random.fold_in(_rk, 8), (64,), 0, max(1, 257 // 4) + 1, jnp.int32)
        _ctx_1024P = jax.random.normal(jax.random.fold_in(_rk, 11), (64, 16, 256), jnp.float32)
        _ctx_1024c = jax.random.dirichlet(jax.random.fold_in(_rk, 511), 0.3 * jnp.ones((16,), jnp.float32), (64, 257))
        _ctx_1024t = jnp.einsum('bsk,bkd->bsd', _ctx_1024c, _ctx_1024P)
        _ctx_1024t = _ctx_1024t * jax.lax.rsqrt(jnp.mean(jnp.square(_ctx_1024t)) + 1e-12) * 0.953939
        ctx_1024 = -1.39393e-06 + 0.999914 * (_ctx_1024t + 0.3 * jax.random.normal(jax.random.fold_in(_rk, 611), (64, 257, 256), jnp.float32))
        return (x, ctx_1024)
    x, ctx_1024 = _rec_inputs()

    def _L0_xattn_setup():
        import jax, jax.numpy as jnp
        import numpy as np
        D_MODEL = 256
        N_HEADS = 16
        HEAD_DIM = D_MODEL // N_HEADS

        def sparsemax(x):
            x = x - jnp.max(x, axis=-1, keepdims=True)
            zs = -jnp.sort(-x, axis=-1)
            L = x.shape[-1]
            rho = jnp.arange(1, L + 1, dtype=x.dtype)
            cssv = jnp.cumsum(zs, axis=-1) - 1.0
            support = zs > cssv / rho
            k = jnp.maximum(jnp.sum(support, axis=-1, keepdims=True), 1)
            tau = jnp.take_along_axis(cssv, k - 1, axis=-1) / k.astype(x.dtype)
            return jnp.clip(x - tau, 0.0)

        def _split_heads(x):
            B, L, _ = x.shape
            return x.reshape(B, L, N_HEADS, HEAD_DIM).transpose(0, 2, 1, 3)
        key = jax.random.key(seed)
        ks = jax.random.split(key, 11)
        B, L = (2, 512)
        s = 0.02
        inp = {'q': jax.random.normal(ks[0], (B, L, D_MODEL), jnp.float32), 'k': jax.random.normal(ks[1], (B, L, D_MODEL), jnp.float32), 'v': jax.random.normal(ks[2], (B, L, D_MODEL), jnp.float32), 'Wq': jax.random.normal(ks[3], (D_MODEL, D_MODEL), jnp.float32) * s, 'bq': jnp.zeros((D_MODEL,), jnp.float32), 'Wk': jax.random.normal(ks[4], (D_MODEL, D_MODEL), jnp.float32) * s, 'bk': jnp.zeros((D_MODEL,), jnp.float32), 'Wv': jax.random.normal(ks[5], (D_MODEL, D_MODEL), jnp.float32) * s, 'bv': jnp.zeros((D_MODEL,), jnp.float32), 'Wo': jax.random.normal(ks[6], (D_MODEL, D_MODEL), jnp.float32) * s, 'bo': jnp.zeros((D_MODEL,), jnp.float32)}
        return inp
    _L0_xattn_all = _L0_xattn_setup()
    _L0_xattn_in = {k: v for k, v in _L0_xattn_all.items() if k in ('Wq', 'bq', 'Wk', 'bk', 'Wv', 'bv', 'Wo', 'bo')}
    del _L0_xattn_all

    def _L0_attn_setup():
        import jax, jax.numpy as jnp
        import numpy as np
        import math
        B, T, N_EMBD, N_HEAD = (8, 256, 256, 16)
        HEAD_DIM = N_EMBD // N_HEAD
        key = jax.random.key(seed)
        k1, k2, k3 = jax.random.split(key, 3)
        x = jax.random.normal(k1, (B, T, N_EMBD), dtype=jnp.float32)
        W_attn = jax.random.normal(k2, (3 * N_EMBD, N_EMBD), dtype=jnp.float32) * 0.02
        b_attn = jnp.zeros((3 * N_EMBD,), dtype=jnp.float32)
        res_scale = 1.0 / math.sqrt(2.0 * 24)
        W_proj = jax.random.normal(k3, (N_EMBD, N_EMBD), dtype=jnp.float32) * (0.02 * res_scale)
        b_proj = jnp.zeros((N_EMBD,), dtype=jnp.float32)
        return {'x': x, 'W_attn': W_attn, 'b_attn': b_attn, 'W_proj': W_proj, 'b_proj': b_proj}
    _L0_attn_all = _L0_attn_setup()
    _L0_attn_in = {k: v for k, v in _L0_attn_all.items() if k in ('W_attn', 'b_attn', 'W_proj', 'b_proj')}
    del _L0_attn_all

    def _L0_ffn_setup():
        import jax, jax.numpy as jnp
        import numpy as np
        B, S, D, E = (2, 512, 256, 8)
        key = jax.random.key(seed)
        ks = jax.random.split(key, 5)
        x = jax.random.normal(ks[0], (B, S, D), dtype=jnp.float32)
        router_w = jax.random.normal(ks[1], (E, D), dtype=jnp.float32) * 0.02
        router_b = jnp.zeros((E,), dtype=jnp.float32)
        expert_w = jax.random.normal(ks[2], (E, D, D), dtype=jnp.float32) * 0.02
        expert_b = jnp.zeros((E, D), dtype=jnp.float32)
        return {'x': x, 'router_w': router_w, 'router_b': router_b, 'expert_w': expert_w, 'expert_b': expert_b}
    _L0_ffn_all = _L0_ffn_setup()
    _L0_ffn_in = {k: v for k, v in _L0_ffn_all.items() if k in ('router_w', 'router_b', 'expert_w', 'expert_b')}
    del _L0_ffn_all
    return {'x': x, 'ctx_1024': ctx_1024, 'L0_xattn_Wq': _L0_xattn_in['Wq'], 'L0_xattn_bq': _L0_xattn_in['bq'], 'L0_xattn_Wk': _L0_xattn_in['Wk'], 'L0_xattn_bk': _L0_xattn_in['bk'], 'L0_xattn_Wv': _L0_xattn_in['Wv'], 'L0_xattn_bv': _L0_xattn_in['bv'], 'L0_xattn_Wo': _L0_xattn_in['Wo'], 'L0_xattn_bo': _L0_xattn_in['bo'], 'L0_attn_W_attn': _L0_attn_in['W_attn'], 'L0_attn_b_attn': _L0_attn_in['b_attn'], 'L0_attn_W_proj': _L0_attn_in['W_proj'], 'L0_attn_b_proj': _L0_attn_in['b_proj'], 'L0_ffn_router_w': _L0_ffn_in['router_w'], 'L0_ffn_router_b': _L0_ffn_in['router_b'], 'L0_ffn_expert_w': _L0_ffn_in['expert_w'], 'L0_ffn_expert_b': _L0_ffn_in['expert_b']}

def reference(x, ctx_1024, L0_xattn_Wq, L0_xattn_bq, L0_xattn_Wk, L0_xattn_bk, L0_xattn_Wv, L0_xattn_bv, L0_xattn_Wo, L0_xattn_bo, L0_attn_W_attn, L0_attn_b_attn, L0_attn_W_proj, L0_attn_b_proj, L0_ffn_router_w, L0_ffn_router_b, L0_ffn_expert_w, L0_ffn_expert_b):
    import jax
    import jax.numpy as jnp

    def _L0_xattn_ref(q, k, v, Wq, bq, Wk, bk, Wv, bv, Wo, bo):
        import jax, jax.numpy as jnp
        import numpy as np
        D_MODEL = 256
        N_HEADS = 16
        HEAD_DIM = D_MODEL // N_HEADS

        def sparsemax(x):
            x = x - jnp.max(x, axis=-1, keepdims=True)
            zs = -jnp.sort(-x, axis=-1)
            L = x.shape[-1]
            rho = jnp.arange(1, L + 1, dtype=x.dtype)
            cssv = jnp.cumsum(zs, axis=-1) - 1.0
            support = zs > cssv / rho
            k = jnp.maximum(jnp.sum(support, axis=-1, keepdims=True), 1)
            tau = jnp.take_along_axis(cssv, k - 1, axis=-1) / k.astype(x.dtype)
            return jnp.clip(x - tau, 0.0)

        def _split_heads(x):
            B, L, _ = x.shape
            return x.reshape(B, L, N_HEADS, HEAD_DIM).transpose(0, 2, 1, 3)
        qh = _split_heads(q @ Wq + bq)
        kh = _split_heads(k @ Wk + bk)
        vh = _split_heads(v @ Wv + bv)
        scale = HEAD_DIM ** (-0.5)
        scores = jnp.einsum('bhqd,bhkd->bhqk', qh, kh) * scale
        attn = sparsemax(scores)
        out = jnp.einsum('bhqk,bhkd->bhqd', attn, vh)
        B, L = (q.shape[0], q.shape[1])
        out = out.transpose(0, 2, 1, 3).reshape(B, L, D_MODEL)
        return out @ Wo + bo

    def _L0_attn_ref(x, W_attn, b_attn, W_proj, b_proj):
        import jax, jax.numpy as jnp
        import numpy as np
        import math
        B, T, N_EMBD, N_HEAD = (8, 256, 256, 16)
        HEAD_DIM = N_EMBD // N_HEAD
        Bsz, Tlen, C = x.shape
        nh, hd = (N_HEAD, HEAD_DIM)
        qkv = jnp.einsum('btc,oc->bto', x, W_attn) + b_attn
        q, k, v = jnp.split(qkv, 3, axis=2)
        q = q.reshape(Bsz, Tlen, nh, hd).transpose(0, 2, 1, 3)
        k = k.reshape(Bsz, Tlen, nh, hd).transpose(0, 2, 1, 3)
        v = v.reshape(Bsz, Tlen, nh, hd).transpose(0, 2, 1, 3)
        scale = 1.0 / math.sqrt(hd)
        att = jnp.einsum('bhqd,bhkd->bhqk', q, k) * scale
        causal = jnp.tril(jnp.ones((Tlen, Tlen), dtype=bool))
        att = jnp.where(causal, att, -jnp.inf)
        att = jax.nn.softmax(att, axis=-1)
        out = jnp.einsum('bhqk,bhkd->bhqd', att, v)
        out = out.transpose(0, 2, 1, 3).reshape(Bsz, Tlen, C)
        return jnp.einsum('btc,oc->bto', out, W_proj) + b_proj

    def _L0_ffn_ref(x, router_w, router_b, expert_w, expert_b):
        import jax, jax.numpy as jnp
        import numpy as np
        B, S, D, E = (2, 512, 256, 8)
        logits = jnp.einsum('bsd,ed->bse', x, router_w) + router_b
        probs = jax.nn.softmax(logits, axis=-1)
        weights = jnp.max(probs, axis=-1)
        top1 = jnp.argmax(probs, axis=-1)
        y_all = jnp.einsum('bsd,eod->bseo', x, expert_w) + expert_b
        y = jnp.take_along_axis(y_all, top1[:, :, None, None], axis=2)[:, :, 0, :]
        out = y * weights[:, :, None]
        return out
    x = x + _L0_xattn_ref(_layernorm(x, axis=-1), ctx_1024, ctx_1024, L0_xattn_Wq, L0_xattn_bq, L0_xattn_Wk, L0_xattn_bk, L0_xattn_Wv, L0_xattn_bv, L0_xattn_Wo, L0_xattn_bo)
    x = x + _L0_attn_ref(_layernorm(x, axis=-1), L0_attn_W_attn, L0_attn_b_attn, L0_attn_W_proj, L0_attn_b_proj)
    x = x + _L0_ffn_ref(_layernorm(x, axis=-1), L0_ffn_router_w, L0_ffn_router_b, L0_ffn_expert_w, L0_ffn_expert_b)
    return x

_drawn_inputs = setup_inputs


def setup_inputs(seed=0):
    import zlib

    import numpy as np

    out = dict(_drawn_inputs(seed))
    spreads = {'L0_xattn_bq': (0.0, 0.309),
     'L0_xattn_bk': (0.0, 0.8),
     'L0_xattn_bv': (0.0, 0.1),
     'L0_xattn_bo': (0.0, 0.1),
     'L0_attn_b_attn': (0.0, 0.8),
     'L0_attn_b_proj': (0.0, 0.1),
     'L0_ffn_router_b': (0.0, 0.1),
     'L0_ffn_expert_b': (0.0, 0.391)}
    factors = {'L0_attn_W_attn': 8.0, 'L0_attn_W_proj': 6.02}
    for name, (base, spread) in spreads.items():
        noise = np.random.default_rng([zlib.crc32(name.encode()), seed]).standard_normal(out[name].shape)
        drawn = base * np.exp(spread * noise) if base else spread * noise
        out[name] = jnp.asarray(drawn.astype(out[name].dtype))
    for name, factor in factors.items():
        out[name] = (out[name] * factor).astype(out[name].dtype)
    return out
```

```python
from contextlib import ExitStack

import concourse.bass as bass
from concourse import mybir

F32 = mybir.dt.float32
BF16 = mybir.dt.bfloat16
I32 = mybir.dt.int32
ALU = mybir.AluOpType
ACT = mybir.ActivationFunctionType
AX = mybir.AxisListType

P = 128
B, LQ, D = 64, 32, 256
LK = 257
LM = 256
H, DH = 16, 16
E = 8
NC = D // P
G = 4
NG = B // G
T = 4
ROWS = G * T
W = LK + 1
SCALE = 0.25
EPS = 1e-5
SHIFT = 8.0
ROUND = 1.5 * 2.0 ** 23
TOL = 2e-5
GUESS = (-0.0292, -0.0017, -0.1859, 0.264)
JUNK = 4
SLOW_STEPS = 40


class Tile:

    def __init__(self, i, c, per=4):
        self.i, self.c, self.per = i, c, per
        self.n, self.half = i * per + c, i * (per // 2) + c // 2

    def plus(self, d):
        return Tile(self.i, self.c + d, self.per)

    def from_two(self):
        return not (isinstance(self.n, int) and self.c < 2)


def normalise(nc, block, x_sb, ident, x_nt, sbuf, psum, sem):
    stats = sbuf("ln_stats", [P, NG, 6])
    mv = sbuf("ln_mv", [P, NG, 2])
    var, inv, root = sbuf("ln_var", [P, NG]), sbuf("ln_inv", [P, NG]), sbuf("ln_root", [P, NG])
    x_n = sbuf("ln_x", [P, 2, D])
    turned_ps = psum("ln_ps", [P, 2, 512])
    stats_made, inv_made, root_made = sem("ln_stats_made"), sem("ln_inv_made"), sem("ln_root_made")
    normed, turned, kept = sem("ln_normed"), sem("ln_turned"), sem("ln_kept")
    dve_ln = sem("dve_ln")

    def vector(dve):
        v = nc.vector
        for g in range(NG):
            ins = v.bn_stats(stats[:, g, :], x_sb[:, g, :])
        ins.then_inc(dve_ln, 1)
        dve.wait_ge(dve_ln, 1)
        for g in range(NG):
            ins = v.bn_aggr(mv[:, g, :], stats[:, g, :])
        ins.then_inc(dve_ln, 1)
        dve.wait_ge(dve_ln, 2)
        v.tensor_scalar(var[:, :], mv[:, :, 1], EPS, None, ALU.add).then_inc(dve_ln, 1)
        dve.wait_ge(dve_ln, 3)
        v.reciprocal(inv[:, :], var[:, :]).then_inc(inv_made, 1)
        dve.wait_ge(root_made, 1)
        dve.wait_ge(inv_made, 1)
        v.tensor_tensor(inv[:, :], root[:, :], root[:, :], ALU.mult).then_inc(dve_ln, 1)
        dve.wait_ge(dve_ln, 4)
        v.tensor_tensor(inv[:, :], inv[:, :], var[:, :], ALU.mult).then_inc(dve_ln, 1)
        dve.wait_ge(dve_ln, 5)
        v.tensor_scalar(inv[:, :], inv[:, :], -0.5, 1.5, ALU.mult, ALU.add).then_inc(dve_ln, 1)
        dve.wait_ge(dve_ln, 6)
        v.tensor_tensor(root[:, :], root[:, :], inv[:, :], ALU.mult).then_inc(dve_ln, 1)
        dve.wait_ge(dve_ln, 7)
        for g in range(NG):
            if g >= 2:
                dve.wait_ge(turned, g - 1)
            v.tensor_scalar(x_n[:, g % 2, :], x_sb[:, g, :], mv[:, g, 0:1], root[:, g:g + 1], ALU.subtract, ALU.mult
                            ).then_inc(normed, 1)

    def scalar(act):
        act.wait_ge(inv_made, 1)
        nc.scalar.activation(root[:, :], inv[:, :], ACT.Sqrt).then_inc(root_made, 1)
        for g in range(NG):
            act.wait_ge(turned, g + 1)
            nc.scalar.activation(x_nt[:, :, g * P:(g + 1) * P], turned_ps[:, g % 2, 0:2 * P].rearrange("p (c n) -> p c n", c=NC),
                                 ACT.Copy).then_inc(kept, 1)

    def tensor(pe):
        for g in range(NG):
            pe.wait_ge(normed, g + 1)
            if g >= 2:
                pe.wait_ge(kept, g - 1)
            for c in range(NC):
                mm = nc.tensor.transpose(turned_ps[:, g % 2, c * P:(c + 1) * P], x_n[:, g % 2, c * P:(c + 1) * P], ident[:, :])
            mm.then_inc(turned, 1)
    return vector, scalar, tensor, kept


def queries(nc, a, x_sb, ident, quad_mask, wk, wv, wo, bk, q_t, vl_dram, row):
    with ExitStack() as ctx:
        sb = lambda name, shape, dt=F32: ctx.enter_context(nc.sbuf_tensor(name, shape, dt))
        sem = lambda name: ctx.enter_context(nc.semaphore(name))
        ps = lambda name, shape: ctx.enter_context(nc.psum_tensor(name, shape, F32))
        wq = sb("wq", [P, NC, D])
        bq, bq_s, bv = sb("bq", [P, NC]), sb("bq_s", [P, NC]), sb("bv", [P, NC])
        bv_b = sb("bv_b", [P, NC, P])
        bo = sb("bo", [1, D])
        ones = sb("ones", [1, P])
        last = sb("last", [P, NC, B])
        x_nt = sb("x_nt", [P, NC, B * LQ])
        vl_wide = sb("vl_wide", [B, T, D])
        q_ps = ps("q_ps", [P, 2, 512])
        row_ps = ps("row_ps", [P, 512])
        last_ps = ps("last_ps", [B, 512])
        x_in, w_in, c_in = sem("x_in"), sem("w_in"), sem("c_in")
        q_made, q_kept = sem("q_made"), sem("q_kept")
        prepared, last_made, row_made, row_added = sem("prepared"), sem("last_made"), sem("row_made"), sem("row_added")
        widened, vl_out = sem("widened"), sem("vl_out")

        with nc.Block() as block:
            ln_vector, ln_scalar, ln_tensor, ln_kept = normalise(nc, block, x_sb, ident, x_nt, sb, ps, sem)

            @block.sync
            def _(sp):
                sp.dma_start(x_sb[:, :, :], a["x"]).then_inc(x_in, 16)
                sp.dma_start(ident[:, :], a["ident"]).then_inc(c_in, 16)
                sp.dma_start(quad_mask[:, :], a["quad_mask"]).then_inc(c_in, 16)
                for t, name in ((wq, "wq"), (wk, "wk"), (wv, "wv"), (wo, "wo"), (bq, "bq"), (bk, "bk"), (bv, "bv"),
                                (bo, "bo"), (last, "ctx_last")):
                    sp.dma_start(t[:], a[name]).then_inc(w_in, 16)
                sp.wait_ge(widened, 1)
                sp.dma_start(vl_dram, vl_wide[:, :, :]).then_inc(vl_out, 16)
                sp.wait_ge(vl_out, 16)
                sp.wait_ge(c_in, 32)

            @block.gpsimd
            def _(pool):
                nc.gpsimd.memset(vl_wide[:, :, :], 0.0).then_inc(prepared, 1)
                nc.gpsimd.memset(ones[:, :], 1.0).then_inc(prepared, 1)

            @block.vector
            def _(dve):
                dve.wait_ge(x_in, 16)
                ln_vector(dve)
                dve.wait_ge(w_in, 9 * 16)
                nc.vector.tensor_scalar(bq_s[:, :], bq[:, :], SCALE, None, ALU.mult).then_inc(prepared, 1)
                for c in range(NC):
                    ins = nc.vector.tensor_copy(bv_b[:, c, :], bv[:, c:c + 1].to_broadcast([P, P]))
                ins.then_inc(prepared, 1)
                dve.wait_ge(prepared, 4)
                dve.wait_ge(last_made, 1)
                for t in range(T):
                    ins = nc.vector.tensor_copy(vl_wide[:, t, 64 * t:64 * t + 64], last_ps[:, 64 * t:64 * t + 64])
                ins.then_inc(widened, 1)
                dve.wait_ge(row_made, 1)
                nc.vector.tensor_copy(row[:, :], row_ps[:, 0:D]).then_inc(row_added, 1)
                dve.wait_ge(row_added, 1)
                nc.vector.tensor_tensor(x_sb[:, :, :], x_sb[:, :, :], row[:, :].unsqueeze(1).to_broadcast([P, NG, D]),
                                        ALU.add).then_inc(row_added, 1)
                dve.wait_ge(row_added, 2)

            @block.scalar
            def _(act):
                ln_scalar(act)
                act.wait_ge(prepared, 4)
                for k in range(8):
                    act.wait_ge(q_made, k + 1)
                    m, n = k % 2, k // 2
                    nc.scalar.activation(q_t[:, m, n * 512:(n + 1) * 512], q_ps[:, k % 2, :], ACT.Identity,
                                         bias=bq_s[:, m:m + 1], scale=SCALE).then_inc(q_kept, 1)

            @block.tensor
            def _(pe):
                pe.wait_ge(c_in, 32)
                ln_tensor(pe)
                pe.wait_ge(w_in, 9 * 16)
                for c in range(NC):
                    mm = nc.tensor.matmul(last_ps[:, 0:D], last[:, c, :], wv[:, c, :], start=(c == 0), stop=(c == NC - 1))
                mm.then_inc(last_made, 1)
                pe.wait_ge(prepared, 4)
                for c in range(NC):
                    nc.tensor.matmul(row_ps[:, 0:D], bv_b[:, c, :], wo[:, c, :], start=(c == 0), stop=False)
                nc.tensor.matmul(row_ps[:, 0:D], ones[:, :], bo[:, :], start=False, stop=True).then_inc(row_made, 1)
                pe.wait_ge(ln_kept, NG)
                for k in range(8):
                    m, n = k % 2, k // 2
                    if k >= 2:
                        pe.wait_ge(q_kept, k - 1)
                    for c in range(NC):
                        mm = nc.tensor.matmul(q_ps[:, k % 2, :], wq[:, c, m * P:(m + 1) * P], x_nt[:, c, n * 512:(n + 1) * 512],
                                              start=(c == 0), stop=(c == NC - 1))
                    mm.then_inc(q_made, 1)


def build(nc, a, out):
    with ExitStack() as kernel_ctx:
        keep = lambda name, shape, dt=F32: kernel_ctx.enter_context(nc.sbuf_tensor(name, shape, dt))
        x_sb = keep("x_sb", [P, NG, D])
        ident = keep("ident", [P, P])
        quad_mask = keep("quad_mask", [P, T])
        ok = keep("ok", [P, ROWS])
        flag = keep("flag", [1, 1], I32)
        cross_attention(nc, a, x_sb, ident, quad_mask, ok, flag)
        attention_and_experts(nc, a, x_sb, ident, quad_mask, out)


def cross_attention(nc, a, x_sb, ident, quad_mask, ok, flag):
    with ExitStack() as ctx:
        sb = lambda name, shape, dt=F32: ctx.enter_context(nc.sbuf_tensor(name, shape, dt))
        sem = lambda name: ctx.enter_context(nc.semaphore(name))
        wk = sb("wk", [P, NC, D])
        wv = sb("wv", [P, NC, D])
        wo = sb("wo", [P, NC, D])
        bk = sb("bk", [P, NC])
        q_t = sb("q_t", [P, NC, B * LQ])
        vl_dram = nc.dram_tensor("last_values", [B, T, D], F32, kind="Internal").ap()
        row = sb("row", [P, D])
        queries(nc, a, x_sb, ident, quad_mask, wk, wv, wo, bk, q_t, vl_dram, row)
        fast_cross_attention(nc, a, x_sb, ident, quad_mask, ok, wk, wv, wo, bk, q_t, vl_dram)
        raise_flag(nc, ident, ok, flag)
        general_cross_attention(nc, a, x_sb, ident, quad_mask, flag, wk, wv, wo, bk, q_t, vl_dram, row)


def fast_cross_attention(nc, a, x_sb, ident, quad_mask, ok, wk, wv, wo, bk, q_t, vl_dram):
    with ExitStack() as ctx:
        sb = lambda name, shape, dt=F32: ctx.enter_context(nc.sbuf_tensor(name, shape, dt))
        sem = lambda name: ctx.enter_context(nc.semaphore(name))

        ctx_sb = sb("ctx_sb", [P, 2, G, NC, LK])
        k_t = sb("k_t", [P, 2, NC, W])
        q_bd = sb("q_bd", [P, 2, NC, P])
        v_sb = sb("v_sb", [P, 4, G, 2, D])
        s_sb = sb("s_sb", [P, 4, G, T, W])
        sh_sb = sb("sh_sb", [P, 2, G, T, W])
        a_t = sb("a_t", [P, 2, 2, T * P])
        al_t = sb("al_t", [T, 2, P])
        vl = sb("vl", [T, 2, G, D])
        o_sb = sb("o_sb", [P, 2, NC * P])
        om = sb("om", [P, 2, NC, T, LQ])
        pair_sum = sb("pair_sum", [P, NC, 2, LQ])
        y_sb = sb("y_sb", [P, D])
        o_t = sb("o_t", [P, 2, NC, P])
        junk_v = sb("junk_v", [P, JUNK, LK], BF16)
        junk_a = sb("junk_a", [P, JUNK, LK], BF16)
        small = lambda name, n=1, dt=F32: sb(name, [P, n, ROWS], dt)
        top = sb("top", [P, ROWS, 8])
        top_sum, above, per_mean, lin = small("top_sum"), small("above"), small("per_mean"), small("lin")
        tau = small("tau")
        low = small("low")
        total, ratio, inv = small("total"), small("ratio"), small("inv")
        count = small("count")
        step_ = small("step_")
        tau4, neg4 = small("tau4"), small("neg4")
        f4, g4, inv4, d4 = small("f4"), small("g4"), small("inv4"), small("d4")
        neg5 = small("neg5", 2)
        weight_sum = small("weight_sum", 2)
        off = small("off")

        ps = lambda name, shape: ctx.enter_context(nc.psum_tensor(name, shape, F32))
        k_ps = ps("k_ps", [P, 2, 512])
        v_ps = ps("v_ps", [P, 512])
        s_ps = ps("s_ps", [P, 2, 512])
        t_ps = ps("t_ps", [P, 1024])
        o_ps = ps("o_ps", [P, 512])

        ctx_in = [sem("ctx_in0"), sem("ctx_in1")]
        vl_in = [sem("vl_in0"), sem("vl_in1")]
        k_made, k_kept = sem("k_made"), sem("k_kept")
        v_made, v_kept = sem("v_made"), sem("v_kept")
        s_made, s_kept, sh_kept = sem("s_made"), sem("s_kept"), sem("sh_kept")
        bd_made = sem("bd_made")
        tau4_made, f4_made, tau5_made = sem("tau4_made"), sem("f4_made"), sem("tau5_made")
        weights_made, a_turned, a_kept = sem("weights_made"), sem("a_turned"), sem("a_kept")
        o_made, o_copied, o_masked = sem("o_made"), sem("o_copied"), sem("o_masked")
        o_paired, o_kept = sem("o_paired"), sem("o_kept")
        y_made, y_copied, y_kept = sem("y_made"), sem("y_copied"), sem("y_kept")
        top_made, dve_first, dve_waited = sem("top_made"), sem("dve_first"), sem("dve_waited")
        dve_newton, dve_guess, dve_out = sem("dve_newton"), sem("dve_guess"), sem("dve_out")

        def steps(e, step):
            step(Tile(0, -1), True, False, False)
            step(Tile(0, 0), True, True, False)
            step(Tile(0, 1), True, True, True)
            with e.Fori(0, (NG - 4) // 4) as i:
                for c in range(2, 6):
                    step(Tile(i, c), True, True, True)
            step(Tile(0, NG - 2), True, True, True)
            step(Tile(0, NG - 1), False, True, True)
            step(Tile(0, NG), False, False, True)

        with nc.Block() as block:
            @block.sync
            def _(sp):
                def load_ctx(g):
                    sp.dma_start(ctx_sb[:, g.c % 2], a["ctx_t"][bass.ds(g.n, 1)].rearrange("o p b c l -> (o p) b c l")
                                 ).then_inc(ctx_in[g.c % 2], 16)

                def load_vl(g):
                    with nc.allow_non_contiguous_dma(reason="one row of 1 KiB for each quad"):
                        sp.dma_start(vl[:, g.c % 2], vl_dram[bass.ds(g.n * G, G)].rearrange("b t n -> t b n")
                                     ).then_inc(vl_in[g.c % 2], 16)

                load_ctx(Tile(0, 0))
                load_ctx(Tile(0, 1))
                load_vl(Tile(0, 0))
                load_vl(Tile(0, 1))
                with sp.Fori(0, (NG - 4) // 4) as i:
                    for c in range(2, 6):
                        g = Tile(i, c)
                        sp.wait_ge(v_made, (g.n - 1) * G)
                        load_ctx(g)
                        sp.wait_ge(o_made, (g.n - 1) * G)
                        load_vl(g)
                for c in range(NG - 2, NG):
                    g = Tile(0, c)
                    sp.wait_ge(v_made, (g.n - 1) * G)
                    load_ctx(g)
                    sp.wait_ge(o_made, (g.n - 1) * G)
                    load_vl(g)

            @block.gpsimd
            def _(pool):
                def block_diagonal(n, par, first):
                    if not first:
                        pool.wait_ge(s_made, n * 2 - 2)
                    qv = q_t[:, :, bass.ds(n * LQ, LQ)].unsqueeze(2).to_broadcast([P, NC, T, LQ])
                    mv = quad_mask[:, :].unsqueeze(1).unsqueeze(3).to_broadcast([P, NC, T, LQ])
                    nc.gpsimd.tensor_tensor(q_bd[:, par].rearrange("p c (j q) -> p c j q", j=T), qv, mv,
                                            ALU.mult).then_inc(bd_made, 1)

                def gather_output(g, b):
                    n = g.n * G + b
                    pool.wait_ge(o_copied, n + 1)
                    mv = quad_mask[:, :].unsqueeze(1).unsqueeze(3).to_broadcast([P, NC, T, LQ])
                    nc.gpsimd.tensor_tensor(om[:, b % 2], o_sb[:, b % 2].rearrange("p (c j q) -> p c j q", c=NC, j=T), mv,
                                            ALU.mult).then_inc(o_masked, 1)
                    pool.wait_ge(o_masked, n + 1)
                    nc.gpsimd.tensor_tensor(pair_sum[:, :, :, :], om[:, b % 2, :, 0:2, :], om[:, b % 2, :, 2:4, :],
                                            ALU.add).then_inc(o_paired, 1)
                    pool.wait_ge(o_paired, n + 1)
                    if b == 0 and not (g.c < 2 and isinstance(g.n, int)):
                        pool.wait_ge(y_made, g.n - 1)
                    nc.gpsimd.tensor_tensor(o_t[:, g.c % 2, :, b * LQ:(b + 1) * LQ], pair_sum[:, :, 0, :], pair_sum[:, :, 1, :],
                                            ALU.add).then_inc(o_kept, 1)
                    pool.wait_ge(o_kept, n + 1)

                def residual(g):
                    pool.wait_ge(y_copied, g.n + 1)
                    xt = x_sb[:, bass.ds(g.n, 1), :].rearrange("p o d -> p (o d)")
                    nc.gpsimd.tensor_tensor(xt, y_sb[:, :], xt, ALU.add).then_inc(y_kept, 1)

                def step(k, loads, search, outputs):
                    nxt, last = k.plus(1), k.plus(-1)
                    for b in range(G):
                        if loads:
                            block_diagonal(nxt.n * G + b, b % 2, nxt.c == 0 and b < 2)
                        if outputs:
                            gather_output(last, b)
                    if outputs:
                        residual(last)
                steps(pool, step)

            @block.tensor
            def _(pe):
                def keys(g, b):
                    n = g.n * G + b
                    if b == 0:
                        pe.wait_ge(ctx_in[g.c % 2], (g.half + 1) * 16)
                    for m in range(NC):
                        if not (g.c == 0 and b == 0):
                            pe.wait_ge(k_kept, n * 2 + (m - 1))
                        for c in range(NC):
                            mm = nc.tensor.matmul(k_ps[:, m, 0:LK], wk[:, c, m * P:(m + 1) * P],
                                                  ctx_sb[:, g.c % 2, b, c, :], start=(c == 0), stop=(c == NC - 1))
                        mm.then_inc(k_made, 1)

                def values(g, b):
                    n = g.n * G + b
                    if not (g.c == 0 and b == 0):
                        pe.wait_ge(v_kept, n)
                    for j in range(2):
                        for c in range(NC):
                            mm = nc.tensor.matmul(v_ps[:, j * D:(j + 1) * D], ctx_sb[:, g.c % 2, b, c, j * P:(j + 1) * P],
                                                  wv[:, c, :], start=(c == 0), stop=(c == NC - 1))
                    mm.then_inc(v_made, 1)

                def scores(g, b, pair):
                    n = g.n * G + b
                    pe.wait_ge(k_kept, n * 2 + 2)
                    pe.wait_ge(bd_made, n + 1)
                    if not (g.c == 0 and b == 0 and pair == 0):
                        pe.wait_ge(sh_kept, n * 2 + pair)
                    for u in range(2):
                        h = slice(64 * u, 64 * u + 64)
                        mm = nc.tensor.matmul(s_ps[:, u, 0:W], q_bd[h, b % 2, pair, :], k_t[h, b % 2, pair, :],
                                              start=True, stop=True)
                    mm.then_inc(s_made, 1)

                def turn(g, b):
                    n = g.n * G + b
                    pe.wait_ge(weights_made, n + 1)
                    if not (g.c == 0 and b == 0):
                        pe.wait_ge(a_kept, n)
                        pe.wait_ge(o_copied, n)
                    if b == 0 and not g.c == 0:
                        pe.wait_ge(y_copied, g.n)
                    for t in range(T):
                        for j in range(2):
                            nc.tensor.transpose(t_ps[:, (j * T + t) * P:(j * T + t + 1) * P],
                                                s_sb[:, g.c % 4, b, t, j * P:(j + 1) * P], ident[:, :])
                    nc.tensor.transpose(o_ps[0:T, D:D + P], s_sb[:, g.c % 4, b, :, LM], ident[:, :]
                                        ).then_inc(a_turned, 1)

                def output(g, b):
                    n = g.n * G + b
                    pe.wait_ge(a_kept, n + 1)
                    pe.wait_ge(v_kept, n + 1)
                    if b == 0:
                        pe.wait_ge(vl_in[g.c % 2], (g.half + 1) * 16)
                    for c in range(NC):
                        cols = slice(c * P, (c + 1) * P)
                        nc.tensor.matmul(o_ps[:, cols], vl[:, g.c % 2, b, cols], al_t[:, b % 2, :],
                                         start=True, stop=False, skip_group_check=True)
                        for t in (2 * c, 2 * c + 1):
                            for j in range(2):
                                mm = nc.tensor.matmul(
                                    o_ps[64 * (t % 2):64 * (t % 2) + 64, cols], v_sb[:, g.c % 4, b, j, 64 * t:64 * t + 64],
                                    a_t[:, b % 2, j, t * P:(t + 1) * P], start=False, stop=(j == 1), skip_group_check=True)
                    mm.then_inc(o_made, 1)

                def project(g):
                    pe.wait_ge(o_kept, g.n * G + G)
                    pe.wait_ge(o_copied, g.n * G + G)
                    for c in range(NC):
                        mm = nc.tensor.matmul(o_ps[:, D:2 * D], o_t[:, g.c % 2, c, :], wo[:, c, :],
                                              start=(c == 0), stop=(c == NC - 1))
                    mm.then_inc(y_made, 1)

                def step(k, loads, search, outputs):
                    nxt, last = k.plus(1), k.plus(-1)
                    for b in range(G):
                        if loads:
                            keys(nxt, b)
                            if b:
                                scores(nxt, b - 1, 1)
                        if outputs:
                            turn(last, b)
                        if loads:
                            values(nxt, b)
                        if outputs:
                            output(last, b)
                        if loads:
                            scores(nxt, b, 0)
                    if loads:
                        scores(nxt, G - 1, 1)
                    if outputs:
                        project(last)
                steps(pe, step)

            @block.scalar
            def _(act):
                def keep_keys(g, b):
                    n = g.n * G + b
                    for m in range(NC):
                        act.wait_ge(k_made, n * 2 + (m + 1))
                        if not (g.c == 0 and b < 2):
                            act.wait_ge(s_made, n * 2 - 2)
                        nc.scalar.activation(k_t[:, b % 2, m, 0:LK], k_ps[:, m, 0:LK], ACT.Identity, bias=bk[:, m:m + 1],
                                             accum_out=k_t[:, b % 2, m, LK:W]).then_inc(k_kept, 1)

                def keep_values(g, b):
                    n = g.n * G + b
                    act.wait_ge(v_made, n + 1)
                    if b == 0 and not (g.c < 4 and isinstance(g.n, int)):
                        act.wait_ge(o_made, g.n * G - 12)
                    nc.scalar.activation(v_sb[:, g.c % 4, b].rearrange("p j n -> p (j n)"), v_ps[:, :], ACT.Copy
                                         ).then_inc(v_kept, 1)

                def keep_scores(g, b, pair):
                    n = g.n * G + b
                    act.wait_ge(s_made, n * 2 + (pair + 1))
                    nc.scalar.activation(s_sb[:, g.c % 4, b, 2 * pair:2 * pair + 2, :], s_ps[:, :, 0:W], ACT.Copy
                                         ).then_inc(s_kept, 1)
                    nc.scalar.activation(sh_sb[:, g.c % 2, b, 2 * pair:2 * pair + 2, :], s_ps[:, :, 0:W], ACT.Copy,
                                         bias=SHIFT).then_inc(sh_kept, 1)

                def exact_excess(g):
                    act.wait_ge(tau4_made, g.n + 1)
                    for r in range(ROWS):
                        if r >= JUNK:
                            act.wait_ge(f4_made, g.n * ROWS + (r - JUNK + 1))
                        nc.scalar.activation(junk_a[:, r % JUNK, :], s_sb[:, g.c % 4, r // T, r % T, 0:LK], ACT.Relu,
                                             bias=neg4[:, 0, r:r + 1], accum_out=f4[:, 0, r:r + 1]).then_inc(f4_made, 1)

                def weights(g, b):
                    if b == 0:
                        act.wait_ge(tau5_made, g.n + 1)
                    for t in range(T):
                        row, r = s_sb[:, g.c % 4, b, t, 0:LK], b * T + t
                        ins = nc.scalar.activation(row, row, ACT.Relu, bias=neg5[:, g.c % 2, r:r + 1],
                                                   accum_out=weight_sum[:, g.c % 2, r:r + 1])
                    ins.then_inc(weights_made, 1)

                def keep_turned(g, b):
                    n = g.n * G + b
                    act.wait_ge(a_turned, n + 1)
                    if not (g.c == 0 and b < 2):
                        act.wait_ge(o_made, n - 1)
                    nc.scalar.activation(al_t[:, b % 2, :], o_ps[0:T, D:D + P], ACT.Copy)
                    nc.scalar.activation(a_t[:, b % 2].rearrange("p j n -> p (j n)"), t_ps[:, :], ACT.Copy
                                         ).then_inc(a_kept, 1)

                def keep_output(g, b):
                    n = g.n * G + b
                    act.wait_ge(o_made, n + 1)
                    if not (g.c == 0 and b < 2):
                        act.wait_ge(o_masked, n - 1)
                    nc.scalar.activation(o_sb[:, b % 2, :], o_ps[:, 0:D], ACT.Copy).then_inc(o_copied, 1)

                def keep_projected(g):
                    act.wait_ge(y_made, g.n + 1)
                    if not g.c == 0:
                        act.wait_ge(y_kept, g.n)
                    nc.scalar.activation(y_sb[:, :], o_ps[:, D:2 * D], ACT.Copy).then_inc(y_copied, 1)

                def step(k, loads, search, outputs):
                    nxt, last = k.plus(1), k.plus(-1)
                    if outputs:
                        weights(last, 0)
                    for b in range(G):
                        if loads:
                            keep_keys(nxt, b)
                            if b:
                                keep_scores(nxt, b - 1, 1)
                        if outputs:
                            keep_turned(last, b)
                        if loads:
                            keep_values(nxt, b)
                        if outputs:
                            if b < G - 1:
                                weights(last, b + 1)
                            keep_output(last, b)
                        if loads:
                            keep_scores(nxt, b, 0)
                    if loads:
                        keep_scores(nxt, G - 1, 1)
                    if outputs:
                        keep_projected(last)
                    if search:
                        exact_excess(k)
                steps(act, step)

            @block.vector
            def _(dve):
                class Chain:

                    def __init__(self, semaphore, per):
                        self.sem, self.per = semaphore, per

                    def start(self, g):
                        self.g, self.n = g, 0

                    def __call__(self, ins):
                        self.n += 1
                        ins.then_inc(self.sem, 1)
                        dve.wait_ge(self.sem, self.g.n * self.per + self.n)

                    def post(self, ins):
                        self.n += 1
                        ins.then_inc(self.sem, 1)

                    def settle(self, open_=0):
                        dve.wait_ge(self.sem, self.g.n * self.per + (self.n - open_))

                    def end(self):
                        assert self.n == self.per, self.n

                newton, guess, result = Chain(dve_newton, 35 + 4 * (ROWS - 1)), Chain(dve_guess, 9), Chain(dve_out, 3)
                v = nc.vector

                def largest(g, b):
                    dve.wait_ge(s_kept, (g.n * G + b) * 2 + 2)
                    dve.sem_inc(dve_waited, 1)
                    for t in range(T):
                        ins = v.max(top[:, b * T + t, :], s_sb[:, g.c % 4, b, t, 0:LK])
                    return ins

                def first_guess(g):
                    guess.start(g)
                    eighth, largest_ = top[:, :, 7], top[:, :, 0]
                    sums = s_sb[:, g.c % 4, :, :, LK].rearrange("p b t -> p (b t)")
                    guess(v.tensor_reduce(top_sum[:, 0, :], top[:, :, :], AX.X, ALU.add))
                    guess(v.scalar_tensor_tensor(above[:, 0, :], eighth, -8.0, top_sum[:, 0, :], ALU.mult, ALU.add))
                    guess(v.tensor_scalar(low[:, 0, :], top_sum[:, 0, :], 8 * SHIFT - 1, 0.125, ALU.add, ALU.mult))
                    guess(v.scalar_tensor_tensor(low[:, 0, :], largest_, SHIFT - 1, low[:, 0, :], ALU.add, ALU.max))
                    guess(v.scalar_tensor_tensor(per_mean[:, 0, :].rearrange("p (b t) -> p b t", t=T), s_sb[:, g.c % 4, :, :, LK], -1.0 / LK,
                                                 eighth.rearrange("p (b t) -> p b t", t=T), ALU.mult, ALU.add))
                    guess(v.tensor_scalar(lin[:, 0, :], per_mean[:, 0, :], GUESS[3], GUESS[1], ALU.mult, ALU.add))
                    guess(v.tensor_tensor(lin[:, 0, :], lin[:, 0, :], above[:, 0, :], ALU.mult))
                    guess(v.scalar_tensor_tensor(lin[:, 0, :], per_mean[:, 0, :], GUESS[2], lin[:, 0, :], ALU.mult, ALU.add))
                    guess(v.scalar_tensor_tensor(tau[:, 0, :], lin[:, 0, :], GUESS[0] + SHIFT, eighth, ALU.add, ALU.add))
                    guess.end()

                def sums_above(g, t):
                    for r in range(ROWS):
                        row = sh_sb[:, g.c % 2, r // T, r % T, 0:LK]
                        if r >= JUNK:
                            newton.settle(JUNK - 1)
                        newton.post(v.scalar_tensor_tensor(junk_v[:, r % JUNK, :], row, t[:, 0, r:r + 1], row, ALU.is_gt,
                                                           ALU.mult, accum_out=total[:, 0, r:r + 1]))
                    newton.settle()

                def newton_round(t, fast):
                    newton(v.reciprocal(inv[:, 0, :], t[:, 0, :]))
                    newton(v.tensor_tensor(ratio[:, 0, :], total[:, 0, :], inv[:, 0, :], ALU.mult))
                    newton(v.tensor_scalar(count[:, 0, :], ratio[:, 0, :], -0.45, ROUND, ALU.add, ALU.add))
                    newton(v.tensor_scalar(count[:, 0, :], count[:, 0, :], -ROUND, 1.0, ALU.add, ALU.max))
                    newton(v.reciprocal(inv[:, 0, :], count[:, 0, :]))
                    newton(v.scalar_tensor_tensor(ratio[:, 0, :], total[:, 0, :], -1.0, inv[:, 0, :], ALU.add, ALU.mult))
                    newton(v.tensor_tensor(low[:, 0, :], low[:, 0, :], ratio[:, 0, :], ALU.max))
                    if fast:
                        newton(v.tensor_tensor(step_[:, 0, :], ratio[:, 0, :], tau[:, 0, :], ALU.subtract))
                        newton(v.scalar_tensor_tensor(inv[:, 0, :], step_[:, 0, :], 0.25, count[:, 0, :], ALU.mult, ALU.mult))
                        newton(v.tensor_tensor(inv[:, 0, :], inv[:, 0, :], step_[:, 0, :], ALU.mult))
                        newton(v.tensor_tensor(inv[:, 0, :], inv[:, 0, :], ratio[:, 0, :], ALU.add))
                        newton(v.tensor_tensor(tau[:, 0, :], inv[:, 0, :], low[:, 0, :], ALU.max))

                def check_sums(g):
                    dve.wait_ge(weights_made, g.n * G + G)
                    result.start(g)
                    result(v.tensor_scalar(off[:, 0, :], weight_sum[:, g.c % 2, :], 1.0, None, ALU.subtract))
                    result(v.tensor_tensor(off[:, 0, :], off[:, 0, :], off[:, 0, :], ALU.mult))
                    result(v.scalar_tensor_tensor(ok[:, :], off[:, 0, :], TOL * TOL, ok[:, :], ALU.is_le, ALU.mult))

                def step(k, loads, search, outputs):
                    nxt, last = k.plus(1), k.plus(-1)
                    if search:
                        newton.start(k)
                        dve.wait_ge(sh_kept, (k.n + 1) * (2 * G))
                        newton(v.tensor_tensor(tau[:, 0, :], tau[:, 0, :], low[:, 0, :], ALU.max))
                        sums_above(k, tau)
                        newton_round(tau, True)
                    if search:
                        sums_above(k, tau)
                        newton_round(tau, False)
                    if loads:
                        largest(nxt, 0)
                    if search:
                        sums_above(k, low)
                        newton_round(low, False)
                        newton(v.tensor_scalar(neg4[:, 0, :], low[:, 0, :], -1.0, SHIFT, ALU.mult, ALU.add))
                        v.tensor_scalar(tau4[:, 0, :], neg4[:, 0, :], -1.0, None, ALU.mult).then_inc(tau4_made, 1)
                        dve.wait_ge(tau4_made, k.n + 1)
                    if loads:
                        largest(nxt, 1)
                    if search:
                        for r in range(ROWS):
                            if r >= JUNK:
                                newton.settle(JUNK - 1)
                            newton.post(v.tensor_scalar(junk_v[:, r % JUNK, :], s_sb[:, k.c % 4, r // T, r % T, 0:LK],
                                                        tau4[:, 0, r:r + 1], None, ALU.is_gt, ALU.add,
                                                        accum_out=g4[:, 0, r:r + 1]))
                        newton.settle()
                    if loads:
                        largest(nxt, 2)
                    if loads:
                        largest(nxt, 3).then_inc(top_made, 1)
                        dve.wait_ge(top_made, nxt.n + 1)
                    if search:
                        newton(v.tensor_scalar(inv4[:, 0, :], g4[:, 0, :], 1.0, None, ALU.max))
                        newton(v.reciprocal(inv4[:, 0, :], inv4[:, 0, :]))
                        dve.wait_ge(f4_made, (k.n + 1) * ROWS)
                        newton(v.scalar_tensor_tensor(d4[:, 0, :], f4[:, 0, :], -1.0, inv4[:, 0, :], ALU.add, ALU.mult))
                        newton.end()
                        v.tensor_tensor(neg5[:, k.c % 2, :], neg4[:, 0, :], d4[:, 0, :], ALU.subtract).then_inc(tau5_made, 1)
                    if loads:
                        first_guess(nxt)
                    if outputs:
                        check_sums(last)
                v.memset(ok[:, :], 1.0).then_inc(dve_first, 1)
                dve.wait_ge(dve_first, 1)
                steps(dve, step)


def raise_flag(nc, ident, ok, flag):
    with ExitStack() as ctx:
        sb = lambda name, shape, dt=F32: ctx.enter_context(nc.sbuf_tensor(name, shape, dt))
        sem = lambda name: ctx.enter_context(nc.semaphore(name))
        least, least_all = sb("least", [P, 1]), sb("least_all", [1, 1])
        turned = ctx.enter_context(nc.psum_tensor("flag_ps", [P, 512], F32))
        least_made, flag_turned, flag_made = sem("least_made"), sem("flag_turned"), sem("flag_made")
        with nc.Block() as block:
            @block.vector
            def _(dve):
                nc.vector.tensor_reduce(least[:, :], ok[:, :], AX.X, ALU.min).then_inc(least_made, 1)
                dve.wait_ge(flag_turned, 1)
                nc.vector.tensor_reduce(least_all[:, :], turned[0:1, 0:P], AX.X, ALU.min).then_inc(flag_made, 1)
                dve.wait_ge(flag_made, 1)
                nc.vector.tensor_copy(flag[:, :], least_all[:, :]).then_inc(flag_made, 1)
                dve.wait_ge(flag_made, 2)

            @block.tensor
            def _(pe):
                pe.wait_ge(least_made, 1)
                nc.tensor.transpose(turned[0:1, 0:P], least[:, :], ident[:, :]).then_inc(flag_turned, 1)
                pe.wait_ge(flag_turned, 1)


def general_cross_attention(nc, a, x_sb, ident, quad_mask, flag, wk, wv, wo, bk, q_t, vl_dram, row):
    with ExitStack() as ctx:
        sb = lambda name, shape, dt=F32: ctx.enter_context(nc.sbuf_tensor(name, shape, dt))
        sem = lambda name: ctx.enter_context(nc.semaphore(name))
        ps = lambda name, shape: ctx.enter_context(nc.psum_tensor(name, shape, F32))
        ctx_sb = sb("g_ctx", [P, G, NC, LK])
        vl = sb("g_vl", [T, G, D])
        k_t = sb("g_k", [P, NC, LK])
        q_bd = sb("g_bd", [P, NC, P])
        v_sb = sb("g_v", [P, 2, D])
        s_sb = sb("g_s", [P, T, LK])
        zeros = sb("g_zeros", [P, LK])
        junk = sb("g_junk", [P, 2, T, LK])
        low, excess, count, inv, neg = (sb(f"g_{n}", [P, T]) for n in ("low", "excess", "count", "inv", "neg"))
        a_t = sb("g_at", [P, 2, T * P])
        al_t = sb("g_alt", [T, P])
        om = sb("g_om", [P, NC, T, LQ])
        o_t = sb("g_ot", [P, NC, P])
        kv_ps = ps("g_kvps", [P, 2, 512])
        s_ps = ps("g_sps", [P, T, 512])
        t_ps = s_ps[:, 0:2, :]
        o_ps = ps("g_ops", [P, 512])
        y_ps = ps("g_yps", [P, 512])
        zeroed, row_in, row_added, loaded, vl_loaded = (sem(f"g_{n}") for n in (
            "zeroed", "row_in", "row_added", "loaded", "vl_loaded"))
        k_made, k_kept, bd_made, s_made, s_kept = (sem(f"g_{n}") for n in ("k_made", "k_kept", "bd_made", "s_made", "s_kept"))
        dve_waited = sem("g_waited")
        v_made, v_kept, newton, stepped, w_made, turned, a_kept = (sem(f"g_{n}") for n in (
            "v_made", "v_kept", "newton", "stepped", "w_made", "turned", "a_kept"))
        o_made, o_masked, o_kept, y_made, y_kept = (sem(f"g_{n}") for n in ("o_made", "o_masked", "o_kept", "y_made", "y_kept"))
        START, EACH = 3, 4

        with nc.Block() as block:
            def needed(e):
                return e.If(e.value_load(flag[0:1, 0:1], min_val=0, max_val=1) < 1)

            @block.sync
            def _(sp):
                with needed(sp):
                    sp.dma_start(x_sb[:, :, :], a["x"]).then_inc(row_in, 16)
                    with sp.Fori(0, NG) as g:
                        sp.wait_ge(v_made, g * G)
                        sp.dma_start(ctx_sb[:, :, :, :], a["ctx_t"][bass.ds(g, 1)].rearrange("o p b c l -> (o p) b c l")
                                     ).then_inc(loaded, 16)
                        sp.wait_ge(o_made, g * G)
                        with nc.allow_non_contiguous_dma(reason="one row of 1 KiB for each quad"):
                            sp.dma_start(vl[:, :, :], vl_dram[bass.ds(g * G, G)].rearrange("b t n -> t b n")
                                         ).then_inc(vl_loaded, 16)
                sp.nop()

            @block.gpsimd
            def _(pool):
                with needed(pool):
                    with pool.Fori(0, B) as n:
                        pool.wait_ge(s_made, n)
                        qv = q_t[:, :, bass.ds(n * LQ, LQ)].unsqueeze(2).to_broadcast([P, NC, T, LQ])
                        mv = quad_mask[:, :].unsqueeze(1).unsqueeze(3).to_broadcast([P, NC, T, LQ])
                        nc.gpsimd.tensor_tensor(q_bd[:, :, :].rearrange("p c (j q) -> p c j q", j=T), qv, mv, ALU.mult
                                                ).then_inc(bd_made, 1)
                pool.nop()

            @block.tensor
            def _(pe):
                with needed(pe):
                    with pe.Fori(0, NG) as g:
                        pe.wait_ge(loaded, g * 16 + 16)
                        pe.wait_ge(vl_loaded, g * 16 + 16)
                        for b in range(G):
                            n = g * G + b
                            pe.wait_ge(v_kept, n)
                            for m in range(NC):
                                for c in range(NC):
                                    mm = nc.tensor.matmul(kv_ps[:, m, 0:LK], wk[:, c, m * P:(m + 1) * P], ctx_sb[:, b, c, :],
                                                          start=(c == 0), stop=(c == NC - 1))
                            mm.then_inc(k_made, 1)
                            pe.wait_ge(k_kept, n + 1)
                            pe.wait_ge(bd_made, n + 1)
                            pe.wait_ge(a_kept, n)
                            for t in range(T):
                                h = slice(64 * (t % 2), 64 * (t % 2) + 64)
                                mm = nc.tensor.matmul(s_ps[:, t, 0:LK], q_bd[h, t // 2, :], k_t[h, t // 2, :],
                                                      start=True, stop=True)
                            mm.then_inc(s_made, 1)
                            for j in range(2):
                                for c in range(NC):
                                    mm = nc.tensor.matmul(kv_ps[:, j, 0:D], ctx_sb[:, b, c, j * P:(j + 1) * P], wv[:, c, :],
                                                          start=(c == 0), stop=(c == NC - 1))
                            mm.then_inc(v_made, 1)
                            pe.wait_ge(w_made, n + 1)
                            pe.wait_ge(s_kept, n + 1)
                            pe.wait_ge(o_kept, n)
                            for t in range(T):
                                for j in range(2):
                                    nc.tensor.transpose(t_ps[:, j, t * P:(t + 1) * P], s_sb[:, t, j * P:(j + 1) * P], ident[:, :])
                            nc.tensor.transpose(o_ps[0:T, D:D + P], s_sb[:, :, LM], ident[:, :]).then_inc(turned, 1)
                            pe.wait_ge(a_kept, n + 1)
                            pe.wait_ge(v_kept, n + 1)
                            for c in range(NC):
                                cols = slice(c * P, (c + 1) * P)
                                nc.tensor.matmul(o_ps[:, cols], vl[:, b, cols], al_t[:, :], start=True, stop=False,
                                                 skip_group_check=True)
                                for t in (2 * c, 2 * c + 1):
                                    for j in range(2):
                                        mm = nc.tensor.matmul(
                                            o_ps[64 * (t % 2):64 * (t % 2) + 64, cols], v_sb[:, j, 64 * t:64 * t + 64],
                                            a_t[:, j, t * P:(t + 1) * P], start=False, stop=(j == 1), skip_group_check=True)
                            mm.then_inc(o_made, 1)
                        pe.wait_ge(o_kept, g * G + G)
                        pe.wait_ge(y_kept, g)
                        for c in range(NC):
                            mm = nc.tensor.matmul(y_ps[:, 0:D], o_t[:, c, :], wo[:, c, :], start=(c == 0), stop=(c == NC - 1))
                        mm.then_inc(y_made, 1)
                pe.nop()

            @block.scalar
            def _(act):
                with needed(act):
                    with act.Fori(0, B) as n:
                        act.wait_ge(k_made, n + 1)
                        for m in range(NC):
                            ins = nc.scalar.activation(k_t[:, m, :], kv_ps[:, m, 0:LK], ACT.Identity, bias=bk[:, m:m + 1])
                        ins.then_inc(k_kept, 1)
                        act.wait_ge(s_made, n + 1)
                        nc.scalar.activation(s_sb[:, :, :], s_ps[:, :, 0:LK], ACT.Copy).then_inc(s_kept, 1)
                        act.wait_ge(v_made, n + 1)
                        nc.scalar.activation(v_sb[:, :, :], kv_ps[:, :, 0:D], ACT.Copy).then_inc(v_kept, 1)
                        act.wait_ge(turned, n + 1)
                        nc.scalar.activation(al_t[:, :], o_ps[0:T, D:D + P], ACT.Copy)
                        nc.scalar.activation(a_t[:, :, :], t_ps, ACT.Copy).then_inc(a_kept, 1)
                act.nop()

            @block.vector
            def _(dve):
                v = nc.vector
                with needed(dve):
                    v.memset(zeros[:, :], 0.0).then_inc(zeroed, 1)
                    dve.wait_ge(zeroed, 1)
                    dve.wait_ge(row_in, 16)
                    v.tensor_tensor(x_sb[:, :, :], x_sb[:, :, :], row[:, :].unsqueeze(1).to_broadcast([P, NG, D]), ALU.add
                                    ).then_inc(row_added, 1)
                    dve.wait_ge(row_added, 1)
                    with dve.Fori(0, NG) as g:
                        for b in range(G):
                            n = g * G + b
                            done = n * (START + EACH * SLOW_STEPS)
                            dve.wait_ge(s_kept, n + 1)
                            v.tensor_reduce(low[:, :], s_sb[:, :, :], AX.X, ALU.max).then_inc(newton, 1)
                            dve.wait_ge(newton, done + 1)
                            v.tensor_scalar(low[:, :], low[:, :], -1.0, None, ALU.add).then_inc(newton, 1)
                            dve.wait_ge(newton, done + 2)
                            dve.sem_inc(dve_waited, 1)
                            with dve.Fori(0, SLOW_STEPS) as k:
                                at = done + k * EACH + 2
                                for t in range(T):
                                    v.scalar_tensor_tensor(junk[:, 0, t, :], s_sb[:, t, :], low[:, t:t + 1], zeros[:, :],
                                                           ALU.subtract, ALU.max, accum_out=excess[:, t:t + 1])
                                    ins = v.tensor_scalar(junk[:, 1, t, :], s_sb[:, t, :], low[:, t:t + 1], None, ALU.is_gt,
                                                          ALU.add, accum_out=count[:, t:t + 1])
                                ins.then_inc(newton, 1)
                                dve.wait_ge(newton, at + 1)
                                v.tensor_scalar(count[:, :], count[:, :], 1.0, None, ALU.max).then_inc(newton, 1)
                                dve.wait_ge(newton, at + 2)
                                v.reciprocal(inv[:, :], count[:, :]).then_inc(newton, 1)
                                dve.wait_ge(newton, at + 3)
                                v.scalar_tensor_tensor(inv[:, :], excess[:, :], -1.0, inv[:, :], ALU.add, ALU.mult
                                                       ).then_inc(newton, 1)
                                dve.wait_ge(newton, at + 4)
                                v.scalar_tensor_tensor(low[:, :], inv[:, :], 0.0, low[:, :], ALU.max, ALU.add
                                                       ).then_inc(stepped, 1)
                                dve.wait_ge(stepped, n * SLOW_STEPS + k + 1)
                            v.tensor_scalar(neg[:, :], low[:, :], -1.0, None, ALU.mult).then_inc(newton, 1)
                            dve.wait_ge(newton, done + START + EACH * SLOW_STEPS)
                            for t in range(T):
                                ins = v.tensor_scalar(s_sb[:, t, :], s_sb[:, t, :], neg[:, t:t + 1], 0.0, ALU.add, ALU.max)
                            ins.then_inc(w_made, 1)
                            dve.wait_ge(o_made, n + 1)
                            ov = o_ps[:, 0:D].rearrange("p (c j q) -> p c j q", c=NC, j=T)
                            mv = quad_mask[:, :].unsqueeze(1).unsqueeze(3).to_broadcast([P, NC, T, LQ])
                            v.tensor_tensor(om[:, :, :, :], ov, mv, ALU.mult).then_inc(o_masked, 1)
                            dve.wait_ge(o_masked, n + 1)
                            v.tensor_reduce(o_t[:, :, b * LQ:(b + 1) * LQ], om[:, :, :, :].rearrange("p c j q -> p c q j"),
                                            AX.X, ALU.add).then_inc(o_kept, 1)
                            dve.wait_ge(o_kept, n + 1)
                        dve.wait_ge(y_made, g + 1)
                        xt = x_sb[:, bass.ds(g, 1), :].rearrange("p o d -> p (o d)")
                        v.tensor_tensor(xt, y_ps[:, 0:D], xt, ALU.add).then_inc(y_kept, 1)
                        dve.wait_ge(y_kept, g + 1)
                dve.nop()


def attention_and_experts(nc, a, x_sb, ident, quad_mask, out):
    with ExitStack() as ctx:
        sb = lambda name, shape, dt=F32: ctx.enter_context(nc.sbuf_tensor(name, shape, dt))
        sem = lambda name: ctx.enter_context(nc.semaphore(name))
        ps = lambda name, shape: ctx.enter_context(nc.psum_tensor(name, shape, F32))
        w_qkv = sb("w_qkv", [P, NC, 3 * D])
        w_proj = sb("w_proj", [P, NC, D])
        b_qk, b_qs, b_v = sb("b_qk", [P, 4]), sb("b_qs", [P, NC]), sb("b_v", [P, NC])
        b_vb = sb("b_vb", [P, NC, P])
        b_proj = sb("b_proj", [1, D])
        w_exp = sb("w_exp", [P, NC, E * D])
        b_exp = sb("b_exp", [E, D])
        w_rt, b_rt = sb("w_rt", [P, NC, E]), sb("b_rt", [1, E])
        causal = sb("causal", [P, LQ])
        rank = sb("rank", [P, E])
        ones = sb("s_ones", [1, P])
        power = sb("power", [P, NG])
        row = sb("s_row", [P, D])

        stats, mv = sb("stats1", [P, NG, 6]), sb("mv1", [P, NG, 2])
        var1, root1, half1 = sb("var1", [P, NG]), sb("root1", [P, NG]), sb("half1", [P, NG])
        xn1, xt1 = sb("xn1", [P, 2, D]), sb("xt1", [P, 2, NC, P])
        q_t, k_t = sb("s_q", [P, 2, NC, P]), sb("s_k", [P, 2, NC, P])
        v_sb = sb("s_v", [P, 2, G, D])
        batch_mask = sb("batch_mask", [P, G])
        q_bd = sb("s_bd", [P, 2, NC, G, T * LQ])
        s_sb = sb("s_s", [P, 2, T * G, LQ])
        top, den, inv = sb("s_top", [P, T * G]), sb("s_den", [P, T * G]), sb("s_inv", [P, T * G])
        p_t = sb("s_pt", [P, 2, T, P])
        o_sb = sb("s_o", [P, NC, G, T * LQ])
        om = sb("s_om", [P, NC * G, T, LQ])
        o_pair = sb("s_opair", [P, NC * G, 2, LQ])
        o_t = sb("s_ot", [P, 2, NC, P])
        xr = sb("xr", [P, 2, D])
        x2 = sb("x2", [P, 2, D])
        st2, mv2, var2, root2, half2 = sb("st2", [P, 6]), sb("mv2", [P, 2]), sb("var2", [P, 1]), sb("root2", [P, 1]), sb("half2", [P, 1])
        xn2, xt2 = sb("xn2", [P, 2, D]), sb("xt2", [P, 2, NC, P])
        r_top, r_exp, r_den, r_w = sb("r_top", [P, 1]), sb("r_exp", [P, E]), sb("r_den", [P, 1]), sb("r_w", [P, 1])
        r_max, r_sel, r_best, gate = sb("r_max", [P, 1]), sb("r_sel", [P, E]), sb("r_best", [P, 1]), sb("gate", [P, 2, E])
        gate_t = sb("gate_t", [E, P])
        acc = sb("acc", [P, 2, D])

        a_ps = ps("a_ps", [P, 512])
        qk_ps = ps("qk_ps", [P, 512])
        s_ps = ps("ss_ps", [P, 2, 512])
        c_ps = ps("c_ps", [P, 512])
        o_ps = ps("so_ps", [P, 512])
        e_ps = ps("e_ps", [P, 2, 512])

        w_in, e_in, consts, biases, row_made = sem("s_win"), sem("s_ein"), sem("s_consts"), sem("s_biases"), sem("s_rowmade")
        ln1, var1_made, root1_made = sem("ln1"), sem("var1_made"), sem("root1_made")
        dve_waited = sem("s_waited")
        normed1, turned1, kept1 = sem("normed1"), sem("turned1"), sem("kept1")
        qk_made, qk_kept, v_made, v_kept, bd_made = (sem(f"s_{n}") for n in ("qk_made", "qk_kept", "v_made", "v_kept", "bd_made"))
        s_made, masked, softmax, exp_made, probs_made = (sem(f"s_{n}") for n in ("s_made", "masked", "softmax", "exp_made", "probs_made"))
        p_turned, p_kept, o_made, o_copied = (sem(f"s_{n}") for n in ("p_turned", "p_kept", "o_made", "o_copied"))
        o_masked, o_paired, o_kept = (sem(f"s_{n}") for n in ("o_masked", "o_paired", "o_kept"))
        xr_made, y_made, x2_made = sem("xr_made"), sem("s_y_made"), sem("x2_made")
        dve_second, dve_route, dve_total, var2_made, root2_made, normed2, turned2, kept2 = (sem(n) for n in (
            "dve_second", "dve_route", "dve_total", "var2_made", "root2_made", "normed2", "turned2", "kept2"))
        l_made, r_top_made, r_exp_made, gate_made, gate_turned, gate_kept, eb_made, eb_taken = (sem(n) for n in (
            "l_made", "r_top_made", "r_exp_made", "gate_made", "gate_turned", "gate_kept", "eb_made", "eb_taken"))
        e_made, e_taken, stored = sem("e_made"), sem("e_taken"), [sem("stored0"), sem("stored1")]

        def steps(e, step):
            peeled = lambda c: step(Tile(0, c, 2), *(0 <= c + d < NG for d in (2, 1, 0, -1, -2)))
            for c in range(-2, 4):
                peeled(c)
            with e.Fori(0, (NG - 6) // 2) as i:
                for c in (4, 5):
                    step(Tile(i, c, 2), True, True, True, True, True)
            for c in range(NG - 2, NG + 2):
                peeled(c)

        def head_mask(n):
            return quad_mask[:, :].unsqueeze(1).unsqueeze(3).to_broadcast([P, n, T, LQ])

        with nc.Block() as block:
            @block.sync
            def _(sp):
                for t, name in ((w_qkv, "w_qkv"), (w_proj, "w_proj"), (b_qk, "b_qk"), (b_v, "b_v2"), (b_proj, "b_proj"),
                                (b_exp, "b_exp"), (w_rt, "w_rt"), (b_rt, "b_rt"), (causal, "causal"), (rank, "rank"), (batch_mask, "batch_mask")):
                    sp.dma_start(t[:], a[name]).then_inc(w_in, 16)
                sp.dma_start(w_exp[:, :, :], a["w_exp"]).then_inc(e_in, 16)

                def store(g, par):
                    sp.wait_ge(e_taken, g * 4 + 4)
                    sp.dma_start(out[:, bass.ds(g, 1), :].rearrange("p o d -> p (o d)"), acc[:, par, :]).then_inc(stored[par], 16)
                with sp.Fori(0, NG // 2) as i:
                    store(i * 2, 0)
                    store(i * 2 + 1, 1)
                sp.wait_ge(stored[0], NG // 2 * 16)
                sp.wait_ge(stored[1], NG // 2 * 16)

            @block.gpsimd
            def _(pool):
                nc.gpsimd.memset(ones[:, :], 1.0).then_inc(consts, 1)
                nc.gpsimd.memset(power[:, :], -0.5).then_inc(consts, 1)
                pool.wait_ge(consts, 2)
                pool.wait_ge(var1_made, 1)
                nc.gpsimd.tensor_tensor(root1[:, :], var1[:, :], power[:, :], ALU.pow).then_inc(root1_made, 1)

                def root_of(g):
                    pool.wait_ge(var2_made, g.n + 1)
                    nc.gpsimd.tensor_tensor(root2[:, :], var2[:, :], power[:, 0:1], ALU.pow).then_inc(root2_made, 1)

                def block_diagonal(g):
                    pool.wait_ge(qk_kept, g.n + 1)
                    if g.from_two():
                        pool.wait_ge(s_made, g.n - 1)
                    for c in range(NC):
                        qv = q_t[:, g.c % 2, c, :].rearrange("p (b q) -> p b q", b=G).unsqueeze(2).to_broadcast([P, G, T, LQ])
                        ins = nc.gpsimd.tensor_tensor(q_bd[:, g.c % 2, c].rearrange("p b (j q) -> p b j q", j=T), qv,
                                                      head_mask(G), ALU.mult)
                    ins.then_inc(bd_made, 1)

                def residual_input(g):
                    if g.from_two():
                        pool.wait_ge(x2_made, g.n - 1)
                    else:
                        pool.wait_ge(row_made, 2)
                    xt = x_sb[:, bass.ds(g.n, 1), :].rearrange("p o d -> p (o d)")
                    nc.gpsimd.tensor_tensor(xr[:, g.c % 2, :], xt, row[:, :], ALU.add).then_inc(xr_made, 1)

                def gather_output(g, c):
                    n = g.n * 2 + c
                    half = slice(c * G, (c + 1) * G)
                    pool.wait_ge(o_copied, n + 1)
                    nc.gpsimd.tensor_tensor(om[:, half, :, :], o_sb[:, c].rearrange("p b (j q) -> p b j q", j=T),
                                            head_mask(G), ALU.mult).then_inc(o_masked, 1)
                    pool.wait_ge(o_masked, n + 1)
                    nc.gpsimd.tensor_tensor(o_pair[:, half, :, :], om[:, half, 0:2, :], om[:, half, 2:4, :], ALU.add
                                            ).then_inc(o_paired, 1)
                    pool.wait_ge(o_paired, n + 1)
                    if c == 0 and g.from_two():
                        pool.wait_ge(y_made, g.n - 1)
                    nc.gpsimd.tensor_tensor(o_t[:, g.c % 2, c].rearrange("p (b q) -> p b q", b=G), o_pair[:, half, 0, :],
                                            o_pair[:, half, 1, :], ALU.add).then_inc(o_kept, 1)
                    pool.wait_ge(o_kept, n + 1)

                def step(k, prepares, projects, attends, leads, ends):
                    if attends:
                        residual_input(k)
                    if leads:
                        root_of(k.plus(-1))
                    if projects:
                        block_diagonal(k.plus(1))
                    if attends:
                        gather_output(k, 0)
                        gather_output(k, 1)
                steps(pool, step)

            @block.tensor
            def _(pe):
                pe.wait_ge(w_in, 11 * 16)
                pe.wait_ge(consts, 2)
                pe.wait_ge(biases, 1)
                for c in range(NC):
                    nc.tensor.matmul(c_ps[:, 0:D], b_vb[:, c, :], w_proj[:, c, :], start=(c == 0), stop=False)
                nc.tensor.matmul(c_ps[:, 0:D], ones[:, :], b_proj[:, :], start=False, stop=True).then_inc(row_made, 1)

                def turn_first(g):
                    pe.wait_ge(normed1, g.n + 1)
                    if g.c:
                        pe.wait_ge(v_kept, g.n)
                    for c in range(NC):
                        mm = nc.tensor.transpose(a_ps[:, c * P:(c + 1) * P], xn1[:, g.c % 2, c * P:(c + 1) * P], ident[:, :])
                    mm.then_inc(turned1, 1)

                def project_in(g):
                    pe.wait_ge(kept1, g.n + 1)
                    if g.c:
                        pe.wait_ge(qk_kept, g.n)
                    for m in range(4):
                        for c in range(NC):
                            mm = nc.tensor.matmul(qk_ps[:, m * P:(m + 1) * P], w_qkv[:, c, m * P:(m + 1) * P], xt1[:, g.c % 2, c, :],
                                                  start=(c == 0), stop=(c == NC - 1))
                    mm.then_inc(qk_made, 1)
                    for c in range(NC):
                        mm = nc.tensor.matmul(a_ps[:, D:2 * D], xt1[:, g.c % 2, c, :], w_qkv[:, c, 2 * D:3 * D],
                                              start=(c == 0), stop=(c == NC - 1))
                    mm.then_inc(v_made, 1)

                def scores(g):
                    pe.wait_ge(bd_made, g.n + 1)
                    pe.wait_ge(qk_kept, g.n + 1)
                    if g.c:
                        pe.wait_ge(p_kept, g.n)
                    for t in range(T):
                        h = slice(64 * (t % 2), 64 * (t % 2) + 64)
                        for b in range(G):
                            at = (t // 2 * G + b) * LQ
                            mm = nc.tensor.matmul(s_ps[:, t % 2, at:at + LQ], q_bd[h, g.c % 2, t // 2, b, :],
                                                  k_t[h, g.c % 2, t // 2, b * LQ:(b + 1) * LQ], start=True, stop=True)
                    mm.then_inc(s_made, 1)

                def turn_probs(g):
                    pe.wait_ge(probs_made, g.n + 1)
                    for t in range(T):
                        mm = nc.tensor.transpose(s_ps[:, t % 2, t // 2 * P:(t // 2 + 1) * P],
                                                 s_sb[:, g.c % 2, t * G:(t + 1) * G, :].rearrange("p b k -> p (b k)"), ident[:, :])
                    mm.then_inc(p_turned, 1)

                def attend(g, c):
                    pe.wait_ge(p_kept, g.n + 1)
                    pe.wait_ge(v_kept, g.n + 1)
                    if g.c or c:
                        pe.wait_ge(o_copied, g.n * 2 + c)
                    for t in (2 * c, 2 * c + 1):
                        for b in range(G):
                            mm = nc.tensor.matmul(o_ps[64 * (t % 2):64 * (t % 2) + 64, b * P:(b + 1) * P],
                                                  v_sb[:, g.c % 2, b, 64 * t:64 * t + 64], p_t[:, g.c % 2, t, :],
                                                  start=True, stop=True)
                    mm.then_inc(o_made, 1)

                def project_out(g):
                    pe.wait_ge(o_kept, g.n * 2 + 2)
                    pe.wait_ge(row_made, 2)
                    if g.c:
                        pe.wait_ge(r_exp_made, g.n)
                    for c in range(NC):
                        mm = nc.tensor.matmul(c_ps[:, 0:D], o_t[:, g.c % 2, c, :], w_proj[:, c, :], start=(c == 0), stop=(c == NC - 1))
                    mm.then_inc(y_made, 1)

                def turn_second(g):
                    pe.wait_ge(normed2, g.n + 1)
                    if g.c:
                        pe.wait_ge(eb_taken, g.n)
                    for c in range(NC):
                        mm = nc.tensor.transpose(c_ps[:, D + c * P:D + (c + 1) * P], xn2[:, g.c % 2, c * P:(c + 1) * P], ident[:, :])
                    mm.then_inc(turned2, 1)

                def route(g):
                    pe.wait_ge(kept2, g.n + 1)
                    for c in range(NC):
                        nc.tensor.matmul(c_ps[:, D:D + E], xt2[:, g.c % 2, c, :], w_rt[:, c, :], start=(c == 0), stop=False)
                    nc.tensor.matmul(c_ps[:, D:D + E], ones[:, :], b_rt[:, :], start=False, stop=True).then_inc(l_made, 1)

                def turn_gates(g, leads):
                    if leads:
                        pe.wait_ge(x2_made, g.n + 2)
                    else:
                        pe.wait_ge(r_exp_made, g.n + 1)
                    pe.wait_ge(gate_made, g.n + 1)
                    nc.tensor.transpose(c_ps[0:E, D:D + P], gate[:, g.c % 2, :], ident[:, :]).then_inc(gate_turned, 1)

                def gate_biases(g):
                    pe.wait_ge(gate_kept, g.n + 1)
                    nc.tensor.matmul(c_ps[:, 0:D], gate_t[:, :], b_exp[:, :], start=True, stop=True).then_inc(eb_made, 1)

                def experts(g, p):
                    if g.c < 2:
                        pe.wait_ge(e_in, 16)
                    if not (g.c == 0 and p < 2):
                        pe.wait_ge(e_taken, g.n * 4 + (p - 1))
                    for c in range(NC):
                        mm = nc.tensor.matmul(e_ps[:, p % 2, :], xt2[:, g.c % 2, c, :], w_exp[:, c, p * 512:(p + 1) * 512],
                                              start=(c == 0), stop=(c == NC - 1))
                    mm.then_inc(e_made, 1)

                def step(k, prepares, projects, attends, leads, ends):
                    nxt, last, done = k.plus(1), k.plus(-1), k.plus(-2)
                    if attends:
                        scores(k)
                    if projects:
                        turn_first(nxt)
                    if ends:
                        experts(done, 0)
                    if leads:
                        project_out(last)
                    if ends:
                        experts(done, 1)
                    if projects:
                        project_in(nxt)
                    if ends:
                        turn_gates(done, leads)
                    if attends:
                        turn_probs(k)
                    if ends:
                        gate_biases(done)
                        experts(done, 2)
                    if attends:
                        attend(k, 0)
                    if leads:
                        turn_second(last)
                    if ends:
                        experts(done, 3)
                    if attends:
                        attend(k, 1)
                    if leads:
                        route(last)
                steps(pe, step)

            @block.scalar
            def _(act):
                act.wait_ge(biases, 2)

                def keep_output(g, c):
                    act.wait_ge(o_made, g.n * 2 + (c + 1))
                    if g.c:
                        act.wait_ge(o_masked, g.n * 2 + (c - 1))
                    nc.scalar.activation(o_sb[:, c].rearrange("p b n -> p (b n)"), o_ps[:, :], ACT.Copy).then_inc(o_copied, 1)

                def keep_projections(g):
                    act.wait_ge(qk_made, g.n + 1)
                    if g.from_two():
                        act.wait_ge(bd_made, g.n - 1)
                        act.wait_ge(s_made, g.n - 1)
                    for m in range(NC):
                        nc.scalar.activation(q_t[:, g.c % 2, m, :], qk_ps[:, m * P:(m + 1) * P], ACT.Identity,
                                             bias=b_qs[:, m:m + 1], scale=SCALE)
                        ins = nc.scalar.activation(k_t[:, g.c % 2, m, :], qk_ps[:, D + m * P:D + (m + 1) * P], ACT.Identity,
                                                   bias=b_qk[:, 2 + m:3 + m])
                    ins.then_inc(qk_kept, 1)

                def keep_values(g):
                    act.wait_ge(v_made, g.n + 1)
                    if g.from_two():
                        act.wait_ge(o_made, g.n * 2 - 2)
                    for b in range(G):
                        ins = nc.scalar.activation(v_sb[:, g.c % 2, b, :], a_ps[:, D:2 * D], ACT.Copy,
                                                   scale=batch_mask[:, b:b + 1])
                    ins.then_inc(v_kept, 1)

                def step(k, prepares, projects, attends, leads, ends):
                    nxt, last, done = k.plus(1), k.plus(-1), k.plus(-2)
                    if projects:
                        act.wait_ge(turned1, nxt.n + 1)
                        nc.scalar.activation(xt1[:, nxt.c % 2].rearrange("p c n -> p (c n)"), a_ps[:, 0:D], ACT.Copy).then_inc(kept1, 1)
                    if attends:
                        act.wait_ge(masked, k.n + 1)
                        sv = s_sb[:, k.c % 2].rearrange("p r k -> p (r k)")
                        nc.scalar.activation(sv, sv, ACT.Exp).then_inc(exp_made, 1)
                    if projects:
                        keep_projections(nxt)
                    if ends:
                        act.wait_ge(gate_turned, done.n + 1)
                        nc.scalar.activation(gate_t[:, :], c_ps[0:E, D:D + P], ACT.Copy).then_inc(gate_kept, 1)
                    if attends:
                        act.wait_ge(p_turned, k.n + 1)
                        for u in range(2):
                            ins = nc.scalar.activation(p_t[:, k.c % 2, u::2, :],
                                                       s_ps[:, u, 0:2 * P].rearrange("p (t n) -> p t n", t=2), ACT.Copy)
                        ins.then_inc(p_kept, 1)
                    if projects:
                        keep_values(nxt)
                    if attends:
                        keep_output(k, 0)
                    if leads:
                        act.wait_ge(turned2, last.n + 1)
                        nc.scalar.activation(xt2[:, last.c % 2].rearrange("p c n -> p (c n)"), c_ps[:, D:2 * D], ACT.Copy
                                             ).then_inc(kept2, 1)
                    if attends:
                        keep_output(k, 1)
                    if leads:
                        act.wait_ge(r_top_made, last.n + 1)
                        nc.scalar.activation(r_exp[:, :], c_ps[:, D:D + E], ACT.Exp, bias=r_top[:, :], accum_out=r_den[:, :]
                                             ).then_inc(r_exp_made, 1)
                steps(act, step)

            @block.vector
            def _(dve):
                v = nc.vector
                for g in range(NG):
                    ins = v.bn_stats(stats[:, g, :], x_sb[:, g, :])
                ins.then_inc(ln1, 1)
                dve.wait_ge(ln1, 1)
                for g in range(NG):
                    ins = v.bn_aggr(mv[:, g, :], stats[:, g, :])
                ins.then_inc(ln1, 1)
                dve.wait_ge(ln1, 2)
                v.tensor_scalar(var1[:, :], mv[:, :, 1], EPS, None, ALU.add).then_inc(var1_made, 1)
                dve.wait_ge(w_in, 11 * 16)
                for c in range(NC):
                    ins = v.tensor_copy(b_vb[:, c, :], b_v[:, c:c + 1].to_broadcast([P, P]))
                ins.then_inc(biases, 1)
                v.tensor_scalar(b_qs[:, :], b_qk[:, 0:2], SCALE, None, ALU.mult).then_inc(biases, 1)
                dve.wait_ge(var1_made, 1)
                dve.wait_ge(root1_made, 1)
                v.tensor_tensor(half1[:, :], root1[:, :], root1[:, :], ALU.mult).then_inc(ln1, 1)
                dve.wait_ge(ln1, 3)
                v.tensor_tensor(half1[:, :], half1[:, :], var1[:, :], ALU.mult).then_inc(ln1, 1)
                dve.wait_ge(ln1, 4)
                v.tensor_scalar(half1[:, :], half1[:, :], -0.5, 1.5, ALU.mult, ALU.add).then_inc(ln1, 1)
                dve.wait_ge(ln1, 5)
                v.tensor_tensor(root1[:, :], root1[:, :], half1[:, :], ALU.mult).then_inc(ln1, 1)
                dve.wait_ge(ln1, 6)
                dve.wait_ge(row_made, 1)
                v.tensor_copy(row[:, :], c_ps[:, 0:D]).then_inc(row_made, 1)

                class Chain:

                    def __init__(self, semaphore, per):
                        self.sem, self.per = semaphore, per

                    def start(self, g):
                        self.g, self.n = g, 0

                    def __call__(self, ins):
                        self.n += 1
                        ins.then_inc(self.sem, 1)
                        dve.wait_ge(self.sem, self.g.n * self.per + self.n)

                    def end(self):
                        assert self.n == self.per, self.n

                soft, second, route, total = Chain(softmax, 4), Chain(dve_second, 6), Chain(dve_route, 4), Chain(dve_total, 4)

                def normalise_first(g):
                    if g.from_two():
                        dve.wait_ge(turned1, g.n - 1)
                    if isinstance(g.n, int):
                        xt, mean, root = x_sb[:, g.n, :], mv[:, g.n, 0:1], root1[:, g.n:g.n + 1]
                    else:
                        xt = x_sb[:, bass.ds(g.n, 1), :].rearrange("p o d -> p (o d)")
                        mean = mv[:, bass.ds(g.n, 1), 0:1].rearrange("p o d -> p (o d)")
                        root = root1[:, bass.ds(g.n, 1)]
                    v.tensor_scalar(xn1[:, g.c % 2, :], xt, mean, root, ALU.subtract, ALU.mult).then_inc(normed1, 1)

                def residual(g):
                    second.start(g)
                    x2t = x2[:, g.c % 2, :]
                    dve.wait_ge(y_made, g.n + 1)
                    dve.wait_ge(xr_made, g.n + 1)
                    v.tensor_tensor(x2t, c_ps[:, 0:D], xr[:, g.c % 2, :], ALU.add).then_inc(x2_made, 1)
                    dve.wait_ge(x2_made, g.n + 1)
                    second(v.bn_stats(st2[:, :], x2t))
                    dve.sem_inc(dve_waited, 1)
                    second(v.bn_aggr(mv2[:, :], st2[:, :]))
                    v.tensor_scalar(var2[:, :], mv2[:, 1:2], EPS, None, ALU.add).then_inc(var2_made, 1)
                    dve.wait_ge(var2_made, g.n + 1)

                def normalise_second(g):
                    dve.wait_ge(root2_made, g.n + 1)
                    second(v.tensor_tensor(half2[:, :], root2[:, :], root2[:, :], ALU.mult))
                    second(v.tensor_tensor(half2[:, :], half2[:, :], var2[:, :], ALU.mult))
                    second(v.tensor_scalar(half2[:, :], half2[:, :], -0.5, 1.5, ALU.mult, ALU.add))
                    second(v.tensor_tensor(half2[:, :], half2[:, :], root2[:, :], ALU.mult))
                    second.end()
                    if g.from_two():
                        dve.wait_ge(turned2, g.n - 1)
                    v.tensor_scalar(xn2[:, g.c % 2, :], x2[:, g.c % 2, :], mv2[:, 0:1], half2[:, 0:1], ALU.subtract, ALU.mult
                                    ).then_inc(normed2, 1)

                def mask_scores(g):
                    soft.start(g)
                    dve.wait_ge(s_made, g.n + 1)
                    sv = s_sb[:, g.c % 2]
                    for u in range(2):
                        for w in range(2):
                            t = 2 * w + u
                            ins = v.tensor_tensor(sv[:, t * G:(t + 1) * G, :],
                                                  s_ps[:, u, w * P:(w + 1) * P].rearrange("p (b k) -> p b k", k=LQ),
                                                  causal[:, :].unsqueeze(1).to_broadcast([P, G, LQ]), ALU.add)
                    soft(ins)
                    soft(v.tensor_reduce(top[:, :], sv, AX.X, ALU.max))
                    v.tensor_tensor(sv, sv, top[:, :].unsqueeze(2).to_broadcast([P, T * G, LQ]), ALU.subtract).then_inc(masked, 1)

                def normalise_probs(g):
                    dve.wait_ge(exp_made, g.n + 1)
                    sv = s_sb[:, g.c % 2]
                    soft(v.tensor_reduce(den[:, :], sv, AX.X, ALU.add))
                    soft(v.reciprocal(inv[:, :], den[:, :]))
                    v.tensor_tensor(sv, sv, inv[:, :].unsqueeze(2).to_broadcast([P, T * G, LQ]), ALU.mult).then_inc(probs_made, 1)

                def likeliest(g):
                    dve.wait_ge(l_made, g.n + 1)
                    v.tensor_reduce(r_top[:, :], c_ps[:, D:D + E], AX.X, ALU.max, negate=True).then_inc(r_top_made, 1)

                def gates(g):
                    route.start(g)
                    dve.wait_ge(r_exp_made, g.n + 1)
                    route(v.reciprocal(r_w[:, :], r_den[:, :]))
                    route(v.tensor_reduce(r_max[:, :], r_exp[:, :], AX.X, ALU.max))
                    route(v.scalar_tensor_tensor(r_sel[:, :], r_exp[:, :], r_max[:, 0:1], rank[:, :], ALU.is_ge, ALU.mult))
                    route(v.tensor_reduce(r_best[:, :], r_sel[:, :], AX.X, ALU.max))
                    if g.from_two():
                        dve.wait_ge(gate_turned, g.n - 1)
                    v.tensor_scalar(gate[:, g.c % 2, :], r_sel[:, :], r_best[:, 0:1], r_w[:, 0:1], ALU.is_ge, ALU.mult
                                    ).then_inc(gate_made, 1)
                    dve.wait_ge(gate_made, g.n + 1)
                    route.end()

                def combine(g, p):
                    at = acc[:, g.c % 2, :]
                    if p == 0:
                        total.start(g)
                        if g.from_two():
                            dve.wait_ge(stored[g.c % 2], g.half * 16)
                    dve.wait_ge(e_made, g.n * 4 + (p + 1))
                    for e in (2 * p, 2 * p + 1):
                        ins = v.scalar_tensor_tensor(at, e_ps[:, p % 2, (e % 2) * D:(e % 2 + 1) * D], gate[:, g.c % 2, e:e + 1],
                                                     x2[:, g.c % 2, :] if e == 0 else at, ALU.mult, ALU.add)
                        if e % 2 == 0:
                            total(ins)
                    ins.then_inc(e_taken, 1)
                    dve.wait_ge(e_taken, g.n * 4 + (p + 1))

                def add_biases(g):
                    dve.wait_ge(eb_made, g.n + 1)
                    at = acc[:, g.c % 2, :]
                    v.tensor_tensor(at, c_ps[:, 0:D], at, ALU.add).then_inc(eb_taken, 1)
                    dve.wait_ge(eb_taken, g.n + 1)

                def step(k, prepares, projects, attends, leads, ends):
                    last, done = k.plus(-1), k.plus(-2)
                    if attends:
                        mask_scores(k)
                    if ends:
                        gates(done)
                        combine(done, 0)
                    if attends:
                        normalise_probs(k)
                    if leads:
                        residual(last)
                    if ends:
                        combine(done, 1)
                    if leads:
                        normalise_second(last)
                    if ends:
                        add_biases(done)
                        combine(done, 2)
                    if prepares:
                        normalise_first(k.plus(2))
                    if ends:
                        combine(done, 3)
                        total.end()
                    if leads:
                        likeliest(last)
                steps(dve, step)


def kernel(**inputs):
    import numpy as np
    import concourse.bacc as bacc
    from concourse.bass_utils import run_bass_kernel_spmd

    arrays = lay_out(**inputs)
    nc = bacc.Bacc("TRN2", target_bir_lowering=False, num_devices=1, dynamic_dma_scratch_size=1024)
    aps = {n: nc.dram_tensor(f"in_{n}", v.shape, F32, kind="ExternalInput").ap() for n, v in arrays.items()}
    out = nc.dram_tensor("out_x", (P, NG, D), F32, kind="ExternalOutput").ap()
    build(nc, aps, out)
    r = run_bass_kernel_spmd(nc, [{f"in_{n}": v for n, v in arrays.items()}], core_ids=[0])
    got = r.results[0]["out_x"]
    return np.ascontiguousarray(got.transpose(1, 0, 2)).reshape(B, LQ, D)


def lay_out(**inputs):
    import numpy as np

    i = {k: np.asarray(v) for k, v in inputs.items()}
    chunks = lambda w: w.reshape(NC, P, -1).transpose(1, 0, 2)
    column = lambda v: v.reshape(-1, P).T
    c = i["ctx_1024"]
    ctx_t = c.transpose(0, 2, 1).reshape(NG, G, NC, P, LK).transpose(0, 3, 1, 2, 4)
    channel = np.arange(P)
    arrays = {
        "x": i["x"].reshape(NG, P, D).transpose(1, 0, 2),
        "ctx_t": ctx_t,
        "ctx_last": c[:, LM, :].T.reshape(NC, P, B).transpose(1, 0, 2),
        "wq": chunks(i["L0_xattn_Wq"]), "wk": chunks(i["L0_xattn_Wk"]), "wv": chunks(i["L0_xattn_Wv"]),
        "wo": chunks(i["L0_xattn_Wo"]),
        "bq": column(i["L0_xattn_bq"]), "bk": column(i["L0_xattn_bk"]), "bv": column(i["L0_xattn_bv"]),
        "bo": i["L0_xattn_bo"].reshape(1, D),
        "w_qkv": chunks(i["L0_attn_W_attn"].T), "w_proj": chunks(i["L0_attn_W_proj"].T),
        "b_qk": column(i["L0_attn_b_attn"][:2 * D]), "b_v2": column(i["L0_attn_b_attn"][2 * D:]),
        "b_proj": i["L0_attn_b_proj"].reshape(1, D),
        "w_exp": chunks(i["L0_ffn_expert_w"].transpose(2, 0, 1).reshape(D, E * D)), "b_exp": i["L0_ffn_expert_b"],
        "w_rt": chunks(i["L0_ffn_router_w"].T), "b_rt": i["L0_ffn_router_b"].reshape(1, E),
        "causal": np.where(np.arange(LQ)[None, :] <= (channel % LQ)[:, None], 0.0, -1e30).astype(np.float32),
        "batch_mask": (channel[:, None] // LQ == np.arange(G)[None, :]).astype(np.float32),
        "rank": np.tile(E - np.arange(E, dtype=np.float32), (P, 1)),
        "ident": np.eye(P, dtype=np.float32),
        "quad_mask": (channel[:, None] % 64 // DH == np.arange(T)[None, :]).astype(np.float32),
    }
    return {n: np.ascontiguousarray(v) for n, v in arrays.items()}
```

```python
from contextlib import ExitStack

import concourse.bass as bass
from concourse import mybir

F32 = mybir.dt.float32
BF16 = mybir.dt.bfloat16
I32 = mybir.dt.int32
ALU = mybir.AluOpType
ACT = mybir.ActivationFunctionType
AX = mybir.AxisListType

P = 128
B, LQ, D = 64, 32, 256
LK = 257
LM = 256
H, DH = 16, 16
E = 8
NC = D // P
G = 4
NG = B // G
T = 4
ROWS = G * T
W = LK + 1
SCALE = 0.25
EPS = 1e-5
SHIFT = 8.0
ROUND = 1.5 * 2.0 ** 23
TOL = 2e-5
GUESS = (-0.0292, -0.0017, -0.1859, 0.264)
ACT_ROWS = (range(4), range(4, 7), range(7, 10))
DVE_ROWS = range(10, 16)
JUNK = 4
SLOW_STEPS = 40


class Tile:

    def __init__(self, i, c, per=4):
        self.i, self.c, self.per = i, c, per
        self.n, self.half = i * per + c, i * (per // 2) + c // 2

    def plus(self, d):
        return Tile(self.i, self.c + d, self.per)

    def from_two(self):
        return not (isinstance(self.n, int) and self.c < 2)


def normalise(nc, block, x_sb, ident, x_nt, sbuf, psum, sem):
    stats = sbuf("ln_stats", [P, NG, 6])
    mv = sbuf("ln_mv", [P, NG, 2])
    var, inv, root = sbuf("ln_var", [P, NG]), sbuf("ln_inv", [P, NG]), sbuf("ln_root", [P, NG])
    x_n = sbuf("ln_x", [P, 2, D])
    turned_ps = psum("ln_ps", [P, 2, 512])
    stats_made, inv_made, root_made = sem("ln_stats_made"), sem("ln_inv_made"), sem("ln_root_made")
    normed, turned, kept = sem("ln_normed"), sem("ln_turned"), sem("ln_kept")
    dve_ln = sem("dve_ln")

    def vector(dve):
        v = nc.vector
        for g in range(NG):
            ins = v.bn_stats(stats[:, g, :], x_sb[:, g, :])
        ins.then_inc(dve_ln, 1)
        dve.wait_ge(dve_ln, 1)
        for g in range(NG):
            ins = v.bn_aggr(mv[:, g, :], stats[:, g, :])
        ins.then_inc(dve_ln, 1)
        dve.wait_ge(dve_ln, 2)
        v.tensor_scalar(var[:, :], mv[:, :, 1], EPS, None, ALU.add).then_inc(dve_ln, 1)
        dve.wait_ge(dve_ln, 3)
        v.reciprocal(inv[:, :], var[:, :]).then_inc(inv_made, 1)
        dve.wait_ge(root_made, 1)
        dve.wait_ge(inv_made, 1)
        v.tensor_tensor(inv[:, :], root[:, :], root[:, :], ALU.mult).then_inc(dve_ln, 1)
        dve.wait_ge(dve_ln, 4)
        v.tensor_tensor(inv[:, :], inv[:, :], var[:, :], ALU.mult).then_inc(dve_ln, 1)
        dve.wait_ge(dve_ln, 5)
        v.tensor_scalar(inv[:, :], inv[:, :], -0.5, 1.5, ALU.mult, ALU.add).then_inc(dve_ln, 1)
        dve.wait_ge(dve_ln, 6)
        v.tensor_tensor(root[:, :], root[:, :], inv[:, :], ALU.mult).then_inc(dve_ln, 1)
        dve.wait_ge(dve_ln, 7)
        for g in range(NG):
            if g >= 2:
                dve.wait_ge(turned, g - 1)
            v.tensor_scalar(x_n[:, g % 2, :], x_sb[:, g, :], mv[:, g, 0:1], root[:, g:g + 1], ALU.subtract, ALU.mult
                            ).then_inc(normed, 1)

    def scalar(act):
        act.wait_ge(inv_made, 1)
        nc.scalar.activation(root[:, :], inv[:, :], ACT.Sqrt).then_inc(root_made, 1)
        for g in range(NG):
            act.wait_ge(turned, g + 1)
            nc.scalar.activation(x_nt[:, :, g * P:(g + 1) * P], turned_ps[:, g % 2, 0:2 * P].rearrange("p (c n) -> p c n", c=NC),
                                 ACT.Copy).then_inc(kept, 1)

    def tensor(pe):
        for g in range(NG):
            pe.wait_ge(normed, g + 1)
            if g >= 2:
                pe.wait_ge(kept, g - 1)
            for c in range(NC):
                mm = nc.tensor.transpose(turned_ps[:, g % 2, c * P:(c + 1) * P], x_n[:, g % 2, c * P:(c + 1) * P], ident[:, :])
            mm.then_inc(turned, 1)
    return vector, scalar, tensor, kept


def queries(nc, a, x_sb, ident, quad_mask, wk, wv, wo, bk, q_t, vl_dram, row):
    with ExitStack() as ctx:
        sb = lambda name, shape, dt=F32: ctx.enter_context(nc.sbuf_tensor(name, shape, dt))
        sem = lambda name: ctx.enter_context(nc.semaphore(name))
        ps = lambda name, shape: ctx.enter_context(nc.psum_tensor(name, shape, F32))
        wq = sb("wq", [P, NC, D])
        bq, bq_s, bv = sb("bq", [P, NC]), sb("bq_s", [P, NC]), sb("bv", [P, NC])
        bv_b = sb("bv_b", [P, NC, P])
        bo = sb("bo", [1, D])
        ones = sb("ones", [1, P])
        last = sb("last", [P, NC, B])
        x_nt = sb("x_nt", [P, NC, B * LQ])
        vl_wide = sb("vl_wide", [B, T, D])
        q_ps = ps("q_ps", [P, 2, 512])
        row_ps = ps("row_ps", [P, 512])
        last_ps = ps("last_ps", [B, 512])
        x_in, w_in, c_in = sem("x_in"), sem("w_in"), sem("c_in")
        q_made, q_kept = sem("q_made"), sem("q_kept")
        prepared, last_made, row_made, row_added = sem("prepared"), sem("last_made"), sem("row_made"), sem("row_added")
        widened, vl_out = sem("widened"), sem("vl_out")

        with nc.Block() as block:
            ln_vector, ln_scalar, ln_tensor, ln_kept = normalise(nc, block, x_sb, ident, x_nt, sb, ps, sem)

            @block.sync
            def _(sp):
                sp.dma_start(x_sb[:, :, :], a["x"]).then_inc(x_in, 16)
                sp.dma_start(ident[:, :], a["ident"]).then_inc(c_in, 16)
                sp.dma_start(quad_mask[:, :], a["quad_mask"]).then_inc(c_in, 16)
                for t, name in ((wq, "wq"), (wk, "wk"), (wv, "wv"), (wo, "wo"), (bq, "bq"), (bk, "bk"), (bv, "bv"),
                                (bo, "bo"), (last, "ctx_last")):
                    sp.dma_start(t[:], a[name]).then_inc(w_in, 16)
                sp.wait_ge(widened, 1)
                sp.dma_start(vl_dram, vl_wide[:, :, :]).then_inc(vl_out, 16)
                sp.wait_ge(vl_out, 16)
                sp.wait_ge(c_in, 32)

            @block.gpsimd
            def _(pool):
                nc.gpsimd.memset(vl_wide[:, :, :], 0.0).then_inc(prepared, 1)
                nc.gpsimd.memset(ones[:, :], 1.0).then_inc(prepared, 1)

            @block.vector
            def _(dve):
                dve.wait_ge(x_in, 16)
                ln_vector(dve)
                dve.wait_ge(w_in, 9 * 16)
                nc.vector.tensor_scalar(bq_s[:, :], bq[:, :], SCALE, None, ALU.mult).then_inc(prepared, 1)
                for c in range(NC):
                    ins = nc.vector.tensor_copy(bv_b[:, c, :], bv[:, c:c + 1].to_broadcast([P, P]))
                ins.then_inc(prepared, 1)
                dve.wait_ge(prepared, 4)
                dve.wait_ge(last_made, 1)
                for t in range(T):
                    ins = nc.vector.tensor_copy(vl_wide[:, t, 64 * t:64 * t + 64], last_ps[:, 64 * t:64 * t + 64])
                ins.then_inc(widened, 1)
                dve.wait_ge(row_made, 1)
                nc.vector.tensor_copy(row[:, :], row_ps[:, 0:D]).then_inc(row_added, 1)
                dve.wait_ge(row_added, 1)
                nc.vector.tensor_tensor(x_sb[:, :, :], x_sb[:, :, :], row[:, :].unsqueeze(1).to_broadcast([P, NG, D]),
                                        ALU.add).then_inc(row_added, 1)
                dve.wait_ge(row_added, 2)

            @block.scalar
            def _(act):
                ln_scalar(act)
                act.wait_ge(prepared, 4)
                for k in range(8):
                    act.wait_ge(q_made, k + 1)
                    m, n = k % 2, k // 2
                    nc.scalar.activation(q_t[:, m, n * 512:(n + 1) * 512], q_ps[:, k % 2, :], ACT.Identity,
                                         bias=bq_s[:, m:m + 1], scale=SCALE).then_inc(q_kept, 1)

            @block.tensor
            def _(pe):
                pe.wait_ge(c_in, 32)
                ln_tensor(pe)
                pe.wait_ge(w_in, 9 * 16)
                for c in range(NC):
                    mm = nc.tensor.matmul(last_ps[:, 0:D], last[:, c, :], wv[:, c, :], start=(c == 0), stop=(c == NC - 1))
                mm.then_inc(last_made, 1)
                pe.wait_ge(prepared, 4)
                for c in range(NC):
                    nc.tensor.matmul(row_ps[:, 0:D], bv_b[:, c, :], wo[:, c, :], start=(c == 0), stop=False)
                nc.tensor.matmul(row_ps[:, 0:D], ones[:, :], bo[:, :], start=False, stop=True).then_inc(row_made, 1)
                pe.wait_ge(ln_kept, NG)
                for k in range(8):
                    m, n = k % 2, k // 2
                    if k >= 2:
                        pe.wait_ge(q_kept, k - 1)
                    for c in range(NC):
                        mm = nc.tensor.matmul(q_ps[:, k % 2, :], wq[:, c, m * P:(m + 1) * P], x_nt[:, c, n * 512:(n + 1) * 512],
                                              start=(c == 0), stop=(c == NC - 1))
                    mm.then_inc(q_made, 1)


def build(nc, a, out):
    with ExitStack() as kernel_ctx:
        keep = lambda name, shape, dt=F32: kernel_ctx.enter_context(nc.sbuf_tensor(name, shape, dt))
        x_sb = keep("x_sb", [P, NG, D])
        ident = keep("ident", [P, P])
        quad_mask = keep("quad_mask", [P, T])
        miss = keep("miss", [P, ROWS])
        flag = keep("flag", [1, 1], I32)
        cross_attention(nc, a, x_sb, ident, quad_mask, miss, flag)
        attention_and_experts(nc, a, x_sb, ident, quad_mask, out)


def cross_attention(nc, a, x_sb, ident, quad_mask, miss, flag):
    with ExitStack() as ctx:
        sb = lambda name, shape, dt=F32: ctx.enter_context(nc.sbuf_tensor(name, shape, dt))
        sem = lambda name: ctx.enter_context(nc.semaphore(name))
        wk = sb("wk", [P, NC, D])
        wv = sb("wv", [P, NC, D])
        wo = sb("wo", [P, NC, D])
        bk = sb("bk", [P, NC])
        q_t = sb("q_t", [P, NC, B * LQ])
        vl_dram = nc.dram_tensor("last_values", [B, T, D], F32, kind="Internal").ap()
        row = sb("row", [P, D])
        queries(nc, a, x_sb, ident, quad_mask, wk, wv, wo, bk, q_t, vl_dram, row)
        fast_cross_attention(nc, a, x_sb, ident, quad_mask, miss, wk, wv, wo, bk, q_t, vl_dram)
        raise_flag(nc, ident, miss, flag)
        general_cross_attention(nc, a, x_sb, ident, quad_mask, flag, wk, wv, wo, bk, q_t, vl_dram, row)


def fast_cross_attention(nc, a, x_sb, ident, quad_mask, miss, wk, wv, wo, bk, q_t, vl_dram):
    with ExitStack() as ctx:
        sb = lambda name, shape, dt=F32: ctx.enter_context(nc.sbuf_tensor(name, shape, dt))
        sem = lambda name: ctx.enter_context(nc.semaphore(name))

        ctx_sb = sb("ctx_sb", [P, 2, G, NC, LK])
        k_t = sb("k_t", [P, 2, NC, W])
        q_bd = sb("q_bd", [P, 2, NC, P])
        v_sb = sb("v_sb", [P, 4, G, 2, D])
        s_sb = sb("s_sb", [P, 4, G, T, W])
        sh_sb = sb("sh_sb", [P, 2, G, T, W])
        a_t = sb("a_t", [P, 2, 2, T * P])
        al_t = sb("al_t", [T, 2, P])
        vl = sb("vl", [T, 2, G, D])
        om = sb("om", [P, 2, NC, T, LQ])
        pair_sum = sb("pair_sum", [P, NC, 2, LQ])
        o_sb = sb("o_sb", [P, 2, NC * P])
        y_sb = sb("y_sb", [P, D])
        o_t = sb("o_t", [P, 2, NC, P])
        junk_v = sb("junk_v", [P, JUNK, LK], BF16)
        junk_x = sb("junk_x", [P, 2, LK], BF16)
        zero, one = sb("zero", [P, 1]), sb("one", [P, 1])
        junk_a = sb("junk_a", [P, JUNK, LK], BF16)
        small = lambda name, n=1, dt=F32: sb(name, [P, n, ROWS], dt)
        top = sb("top", [P, ROWS, 8])
        top_sum, above, per_mean, lin = small("top_sum"), small("above"), small("per_mean"), small("lin")
        tau = small("tau")
        low = small("low")
        total, ratio, inv = small("total"), small("ratio"), small("inv")
        count = small("count")
        step_ = small("step_")
        neg4, inv4 = small("neg4", 2), small("inv4", 2)
        f4, d4 = small("f4"), small("d4")
        neg5 = small("neg5", 2)
        weight_sum = small("weight_sum", 2)
        off = small("off")

        ps = lambda name, shape: ctx.enter_context(nc.psum_tensor(name, shape, F32))
        k_ps = ps("k_ps", [P, 2, 512])
        v_ps = ps("v_ps", [P, 512])
        s_ps = ps("s_ps", [P, 2, 512])
        t_ps = ps("t_ps", [P, 1024])
        o_ps = ps("o_ps", [P, 512])

        ctx_in = [sem("ctx_in0"), sem("ctx_in1")]
        vl_in = [sem("vl_in0"), sem("vl_in1")]
        k_made, k_kept = sem("k_made"), sem("k_kept")
        v_made, v_kept = sem("v_made"), sem("v_kept")
        s_made, s_kept, sh_kept = sem("s_made"), sem("s_kept"), sem("sh_kept")
        bd_made = sem("bd_made")
        tau4_made, f4_made, tau5_made = sem("tau4_made"), sem("f4_made"), sem("tau5_made")
        weights_made, a_turned, a_kept = sem("weights_made"), sem("a_turned"), sem("a_kept")
        o_made, o_copied, o_masked = sem("o_made"), sem("o_copied"), sem("o_masked")
        o_paired, o_kept = sem("o_paired"), sem("o_kept")
        y_made, y_copied, y_kept = sem("y_made"), sem("y_copied"), sem("y_kept")
        top_made, dve_first, d4_made = sem("top_made"), sem("dve_first"), sem("d4_made")
        pool_first = sem("pool_first")
        dve_waited = sem("dve_waited")
        dve_newton, dve_guess, dve_exact, checked = (sem(n) for n in ("dve_newton", "dve_guess", "dve_exact", "checked"))

        def steps(e, step):
            peeled = lambda c: step(Tile(0, c), *(0 <= c + d < NG for d in (1, 0, -1, -2, -3)))
            for c in range(-1, 3):
                peeled(c)
            with e.Fori(0, (NG - 4) // 4) as i:
                for c in range(3, 7):
                    step(Tile(i, c), True, True, True, True, True)
            for c in range(NG - 1, NG + 3):
                peeled(c)

        with nc.Block() as block:
            @block.sync
            def _(sp):
                def load_ctx(g):
                    sp.dma_start(ctx_sb[:, g.c % 2], a["ctx_t"][bass.ds(g.n, 1)].rearrange("o p b c l -> (o p) b c l")
                                 ).then_inc(ctx_in[g.c % 2], 16)

                def load_vl(g):
                    with nc.allow_non_contiguous_dma(reason="one row of 1 KiB for each quad"):
                        sp.dma_start(vl[:, g.c % 2], vl_dram[bass.ds(g.n * G, G)].rearrange("b t n -> t b n")
                                     ).then_inc(vl_in[g.c % 2], 16)

                def reload_ctx(g):
                    sp.wait_ge(v_made, (g.n - 1) * G)
                    load_ctx(g)

                def reload_vl(g):
                    sp.wait_ge(o_made, (g.n - 1) * G)
                    load_vl(g)

                for c in range(2):
                    load_ctx(Tile(0, c))
                    load_vl(Tile(0, c))
                for c in range(2, 5):
                    reload_ctx(Tile(0, c))
                with sp.Fori(0, (NG - 6) // 2) as i:
                    for c in (5, 6):
                        reload_ctx(Tile(i, c, 2))
                        reload_vl(Tile(i, c - 3, 2))
                reload_ctx(Tile(0, NG - 1))
                for c in range(NG - 4, NG):
                    reload_vl(Tile(0, c))

            @block.gpsimd
            def _(pool):
                def block_diagonal(n, par, first):
                    if not first:
                        pool.wait_ge(s_made, n * 2 - 2)
                    qv = q_t[:, :, bass.ds(n * LQ, LQ)].unsqueeze(2).to_broadcast([P, NC, T, LQ])
                    mv = quad_mask[:, :].unsqueeze(1).unsqueeze(3).to_broadcast([P, NC, T, LQ])
                    nc.gpsimd.tensor_tensor(q_bd[:, par].rearrange("p c (j q) -> p c j q", j=T), qv, mv,
                                            ALU.mult).then_inc(bd_made, 1)

                def gather_output(g, b):
                    n = g.n * G + b
                    pool.wait_ge(o_copied, n + 1)
                    mv = quad_mask[:, :].unsqueeze(1).unsqueeze(3).to_broadcast([P, NC, T, LQ])
                    nc.gpsimd.tensor_tensor(om[:, b % 2], o_sb[:, b % 2].rearrange("p (c j q) -> p c j q", c=NC, j=T), mv,
                                            ALU.mult).then_inc(o_masked, 1)
                    pool.wait_ge(o_masked, n + 1)
                    nc.gpsimd.tensor_tensor(pair_sum[:, :, :, :], om[:, b % 2, :, 0:2, :], om[:, b % 2, :, 2:4, :],
                                            ALU.add).then_inc(o_paired, 1)
                    pool.wait_ge(o_paired, n + 1)
                    if b == 0 and not (g.c < 2 and isinstance(g.n, int)):
                        pool.wait_ge(y_made, g.n - 1)
                    nc.gpsimd.tensor_tensor(o_t[:, g.c % 2, :, b * LQ:(b + 1) * LQ], pair_sum[:, :, 0, :], pair_sum[:, :, 1, :],
                                            ALU.add).then_inc(o_kept, 1)
                    pool.wait_ge(o_kept, n + 1)

                def residual(g):
                    pool.wait_ge(y_copied, g.n + 1)
                    xt = x_sb[:, bass.ds(g.n, 1), :].rearrange("p o d -> p (o d)")
                    nc.gpsimd.tensor_tensor(xt, y_sb[:, :], xt, ALU.add).then_inc(y_kept, 1)

                def refine(g):
                    pool.wait_ge(f4_made, (g.n + 1) * DVE_ROWS[0])
                    pool.wait_ge(dve_exact, (g.n + 1) * len(DVE_ROWS))
                    pool.wait_ge(tau4_made, g.n + 1)
                    nc.gpsimd.tensor_tensor(d4[:, 0, :], f4[:, 0, :], one[:, 0:1].to_broadcast([P, ROWS]), ALU.subtract
                                            ).then_inc(d4_made, 1)
                    pool.wait_ge(d4_made, g.n * 2 + 1)
                    nc.gpsimd.tensor_tensor(d4[:, 0, :], d4[:, 0, :], inv4[:, g.c % 2, :], ALU.mult).then_inc(d4_made, 1)
                    pool.wait_ge(d4_made, g.n * 2 + 2)
                    if g.from_two():
                        pool.wait_ge(weights_made, (g.n - 1) * G)
                    nc.gpsimd.tensor_tensor(neg5[:, g.c % 2, :], neg4[:, g.c % 2, :], d4[:, 0, :], ALU.subtract).then_inc(tau5_made, 1)

                def check_sums(g):
                    at = g.n * 3
                    pool.wait_ge(weights_made, g.n * G + G)
                    nc.gpsimd.tensor_tensor(off[:, 0, :], weight_sum[:, g.c % 2, :], one[:, 0:1].to_broadcast([P, ROWS]), ALU.subtract
                                            ).then_inc(checked, 1)
                    pool.wait_ge(checked, at + 1)
                    nc.gpsimd.tensor_tensor(off[:, 0, :], off[:, 0, :], off[:, 0, :], ALU.mult).then_inc(checked, 1)
                    pool.wait_ge(checked, at + 2)
                    nc.gpsimd.tensor_tensor(miss[:, :], off[:, 0, :], miss[:, :], ALU.add).then_inc(checked, 1)
                    pool.wait_ge(checked, at + 3)

                def step(k, loads, search, refines, outputs, projects):
                    nxt, last, old = k.plus(1), k.plus(-1), k.plus(-2)
                    for b in range(G):
                        if loads:
                            block_diagonal(nxt.n * G + b, b % 2, nxt.c == 0 and b < 2)
                        if outputs:
                            gather_output(old, b)
                        if b == 0 and projects:
                            residual(k.plus(-3))
                        if b == 2 and refines:
                            refine(last)
                        if b == 3 and outputs:
                            check_sums(old)
                nc.gpsimd.memset(miss[:, :], 0.0)
                nc.gpsimd.memset(one[:, :], 1.0).then_inc(pool_first, 1)
                pool.wait_ge(pool_first, 1)
                steps(pool, step)

            @block.tensor
            def _(pe):
                def keys(g, b):
                    n = g.n * G + b
                    if b == 0:
                        pe.wait_ge(ctx_in[g.c % 2], (g.half + 1) * 16)
                    for m in range(NC):
                        if not (g.c == 0 and b == 0):
                            pe.wait_ge(k_kept, n * 2 + (m - 1))
                        for c in range(NC):
                            mm = nc.tensor.matmul(k_ps[:, m, 0:LK], wk[:, c, m * P:(m + 1) * P],
                                                  ctx_sb[:, g.c % 2, b, c, :], start=(c == 0), stop=(c == NC - 1))
                        mm.then_inc(k_made, 1)

                def values(g, b):
                    n = g.n * G + b
                    if not (g.c == 0 and b == 0):
                        pe.wait_ge(v_kept, n)
                    for j in range(2):
                        for c in range(NC):
                            mm = nc.tensor.matmul(v_ps[:, j * D:(j + 1) * D], ctx_sb[:, g.c % 2, b, c, j * P:(j + 1) * P],
                                                  wv[:, c, :], start=(c == 0), stop=(c == NC - 1))
                    mm.then_inc(v_made, 1)

                def scores(g, b, pair):
                    n = g.n * G + b
                    pe.wait_ge(k_kept, n * 2 + 2)
                    pe.wait_ge(bd_made, n + 1)
                    if not (g.c == 0 and b == 0 and pair == 0):
                        pe.wait_ge(sh_kept, n * 2 + pair)
                    for u in range(2):
                        h = slice(64 * u, 64 * u + 64)
                        mm = nc.tensor.matmul(s_ps[:, u, 0:W], q_bd[h, b % 2, pair, :], k_t[h, b % 2, pair, :],
                                              start=True, stop=True)
                    mm.then_inc(s_made, 1)

                def turn(g, b):
                    n = g.n * G + b
                    pe.wait_ge(weights_made, n + 1)
                    if not (g.c == 0 and b == 0):
                        pe.wait_ge(a_kept, n)
                        pe.wait_ge(o_copied, n)
                    if b == 1 and not g.c == 0:
                        pe.wait_ge(y_copied, g.n)
                    for t in range(T):
                        for j in range(2):
                            nc.tensor.transpose(t_ps[:, (j * T + t) * P:(j * T + t + 1) * P],
                                                s_sb[:, g.c % 4, b, t, j * P:(j + 1) * P], ident[:, :])
                    nc.tensor.transpose(o_ps[0:T, D:D + P], s_sb[:, g.c % 4, b, :, LM], ident[:, :]
                                        ).then_inc(a_turned, 1)

                def output(g, b):
                    n = g.n * G + b
                    pe.wait_ge(a_kept, n + 1)
                    pe.wait_ge(v_kept, n + 1)
                    if b == 0:
                        pe.wait_ge(vl_in[g.c % 2], (g.half + 1) * 16)
                    for c in range(NC):
                        cols = slice(c * P, (c + 1) * P)
                        nc.tensor.matmul(o_ps[:, cols], vl[:, g.c % 2, b, cols], al_t[:, b % 2, :],
                                         start=True, stop=False, skip_group_check=True)
                        for t in (2 * c, 2 * c + 1):
                            for j in range(2):
                                mm = nc.tensor.matmul(
                                    o_ps[64 * (t % 2):64 * (t % 2) + 64, cols], v_sb[:, g.c % 4, b, j, 64 * t:64 * t + 64],
                                    a_t[:, b % 2, j, t * P:(t + 1) * P], start=False, stop=(j == 1), skip_group_check=True)
                    mm.then_inc(o_made, 1)

                def project(g, outputs):
                    pe.wait_ge(o_kept, g.n * G + G)
                    pe.wait_ge(o_copied, g.n * G + G)
                    if outputs:
                        pe.wait_ge(a_kept, g.n * G + G + 1)
                    for c in range(NC):
                        mm = nc.tensor.matmul(o_ps[:, D:2 * D], o_t[:, g.c % 2, c, :], wo[:, c, :],
                                              start=(c == 0), stop=(c == NC - 1))
                    mm.then_inc(y_made, 1)

                def step(k, loads, search, refines, outputs, projects):
                    nxt, old = k.plus(1), k.plus(-2)
                    for b in range(G):
                        if loads:
                            keys(nxt, b)
                        if b and loads:
                            scores(nxt, b - 1, 1)
                        if b == 0 and search:
                            scores(k, G - 1, 1)
                        if outputs:
                            turn(old, b)
                        if loads:
                            values(nxt, b)
                        if b == 0 and projects:
                            project(k.plus(-3), outputs)
                        if outputs:
                            output(old, b)
                        if loads:
                            scores(nxt, b, 0)
                steps(pe, step)

            @block.scalar
            def _(act):
                def keep_keys(g, b):
                    n = g.n * G + b
                    for m in range(NC):
                        act.wait_ge(k_made, n * 2 + (m + 1))
                        if not (g.c == 0 and b < 2):
                            act.wait_ge(s_made, n * 2 - 2)
                        nc.scalar.activation(k_t[:, b % 2, m, 0:LK], k_ps[:, m, 0:LK], ACT.Identity, bias=bk[:, m:m + 1],
                                             accum_out=k_t[:, b % 2, m, LK:W]).then_inc(k_kept, 1)

                def keep_values(g, b):
                    n = g.n * G + b
                    act.wait_ge(v_made, n + 1)
                    if b == 0 and not (g.c < 4 and isinstance(g.n, int)):
                        act.wait_ge(o_made, g.n * G - 12)
                    nc.scalar.activation(v_sb[:, g.c % 4, b].rearrange("p j n -> p (j n)"), v_ps[:, :], ACT.Copy
                                         ).then_inc(v_kept, 1)

                def keep_output(g, b):
                    n = g.n * G + b
                    act.wait_ge(o_made, n + 1)
                    if not (g.c == 0 and b < 2):
                        act.wait_ge(o_masked, n - 1)
                    nc.scalar.activation(o_sb[:, b % 2, :], o_ps[:, 0:D], ACT.Copy).then_inc(o_copied, 1)

                def keep_projected(g, outputs):
                    act.wait_ge(y_made, g.n + 1)
                    if outputs:
                        act.wait_ge(o_made, g.n * G + G + 1)
                    if not g.c == 0:
                        act.wait_ge(y_kept, g.n)
                    nc.scalar.activation(y_sb[:, :], o_ps[:, D:2 * D], ACT.Copy).then_inc(y_copied, 1)

                def keep_scores(g, b, pair):
                    n = g.n * G + b
                    act.wait_ge(s_made, n * 2 + (pair + 1))
                    if b == 0 and pair == 0 and g.from_two():
                        act.wait_ge(tau4_made, g.n - 1)
                    nc.scalar.activation(s_sb[:, g.c % 4, b, 2 * pair:2 * pair + 2, :], s_ps[:, :, 0:W], ACT.Copy
                                         ).then_inc(s_kept, 1)
                    nc.scalar.activation(sh_sb[:, g.c % 2, b, 2 * pair:2 * pair + 2, :], s_ps[:, :, 0:W], ACT.Copy,
                                         bias=SHIFT).then_inc(sh_kept, 1)

                len_act = DVE_ROWS[0]

                def exact_excess(g, rows):
                    for r in rows:
                        if r == 0:
                            act.wait_ge(tau4_made, g.n + 1)
                        if r >= JUNK:
                            act.wait_ge(f4_made, g.n * len_act + (r - JUNK + 1))
                        nc.scalar.activation(junk_a[:, r % JUNK, :], s_sb[:, g.c % 4, r // T, r % T, 0:LK], ACT.Relu,
                                             bias=neg4[:, g.c % 2, r:r + 1], accum_out=f4[:, 0, r:r + 1]).then_inc(f4_made, 1)

                def weights(g, b):
                    if b == 0:
                        act.wait_ge(tau5_made, g.n + 1)
                    for t in range(T):
                        row, r = s_sb[:, g.c % 4, b, t, 0:LK], b * T + t
                        ins = nc.scalar.activation(row, row, ACT.Relu, bias=neg5[:, g.c % 2, r:r + 1],
                                                   accum_out=weight_sum[:, g.c % 2, r:r + 1])
                    ins.then_inc(weights_made, 1)

                def keep_turned(g, b):
                    n = g.n * G + b
                    act.wait_ge(a_turned, n + 1)
                    if not (g.c == 0 and b < 2):
                        act.wait_ge(o_made, n - 1)
                    nc.scalar.activation(al_t[:, b % 2, :], o_ps[0:T, D:D + P], ACT.Copy)
                    nc.scalar.activation(a_t[:, b % 2].rearrange("p j n -> p (j n)"), t_ps[:, :], ACT.Copy
                                         ).then_inc(a_kept, 1)

                def step(k, loads, search, refines, outputs, projects):
                    nxt, last, old = k.plus(1), k.plus(-1), k.plus(-2)
                    for b in range(G):
                        if loads:
                            keep_keys(nxt, b)
                        if outputs:
                            keep_turned(old, b)
                        if b and loads:
                            keep_scores(nxt, b - 1, 1)
                        if b == 0 and search:
                            keep_scores(k, G - 1, 1)
                        if outputs:
                            if b < G - 1:
                                weights(old, b + 1)
                            keep_output(old, b)
                        if b == 0 and projects:
                            keep_projected(k.plus(-3), outputs)
                        if loads:
                            keep_values(nxt, b)
                            keep_scores(nxt, b, 0)
                        if refines and b < 3:
                            exact_excess(last, ACT_ROWS[b])
                        if refines and b == G - 1:
                            weights(last, 0)
                steps(act, step)

            @block.vector
            def _(dve):
                class Chain:

                    def __init__(self, semaphore, per):
                        self.sem, self.per = semaphore, per

                    def start(self, g):
                        self.g, self.n = g, 0

                    def __call__(self, ins, meanwhile=None):
                        self.n += 1
                        ins.then_inc(self.sem, 1)
                        if meanwhile:
                            meanwhile()
                        dve.wait_ge(self.sem, self.g.n * self.per + self.n)

                    def post(self, ins):
                        self.n += 1
                        ins.then_inc(self.sem, 1)

                    def settle(self, open_=0):
                        dve.wait_ge(self.sem, self.g.n * self.per + (self.n - open_))

                    def end(self):
                        assert self.n == self.per, self.n

                newton, guess, exact = Chain(dve_newton, 3 * ROWS + 30), Chain(dve_guess, 9), Chain(dve_exact, len(DVE_ROWS))
                v = nc.vector

                def largest(g, rows):
                    for r in rows:
                        if r % T == 0:
                            dve.wait_ge(s_kept, (g.n * G + r // T) * 2 + 2)
                            dve.sem_inc(dve_waited, 1)
                        ins = v.max(top[:, r, :], s_sb[:, g.c % 4, r // T, r % T, 0:LK])
                        if r == ROWS - 1:
                            ins.then_inc(top_made, 1)

                def first_guess(g):
                    guess.start(g)
                    eighth, largest_ = top[:, :, 7], top[:, :, 0]
                    guess.post(v.tensor_reduce(top_sum[:, 0, :], top[:, :, :], AX.X, ALU.add))
                    guess.post(v.scalar_tensor_tensor(per_mean[:, 0, :].rearrange("p (b t) -> p b t", t=T), s_sb[:, g.c % 4, :, :, LK], -1.0 / LK,
                                                      eighth.rearrange("p (b t) -> p b t", t=T), ALU.mult, ALU.add))
                    guess.settle(1)
                    guess.post(v.scalar_tensor_tensor(above[:, 0, :], eighth, -8.0, top_sum[:, 0, :], ALU.mult, ALU.add))
                    guess.settle(1)
                    guess.post(v.tensor_scalar(lin[:, 0, :], per_mean[:, 0, :], GUESS[3], GUESS[1], ALU.mult, ALU.add))
                    guess.post(v.tensor_scalar(low[:, 0, :], top_sum[:, 0, :], 8 * SHIFT - 1, 0.125, ALU.add, ALU.mult))
                    guess.settle(1)
                    guess.post(v.tensor_tensor(above[:, 0, :], lin[:, 0, :], above[:, 0, :], ALU.mult))
                    guess.settle(1)
                    guess.post(v.scalar_tensor_tensor(low[:, 0, :], largest_, SHIFT - 1, low[:, 0, :], ALU.add, ALU.max))
                    guess.settle(1)
                    guess.post(v.scalar_tensor_tensor(lin[:, 0, :], per_mean[:, 0, :], GUESS[2], above[:, 0, :], ALU.mult, ALU.add))
                    guess.settle()
                    guess(v.scalar_tensor_tensor(tau[:, 0, :], lin[:, 0, :], GUESS[0] + SHIFT, eighth, ALU.add, ALU.add))
                    guess.end()

                def sums_above(g, t):
                    for r in range(ROWS):
                        row = sh_sb[:, g.c % 2, r // T, r % T, 0:LK]
                        if r >= JUNK:
                            newton.settle(JUNK - 1)
                        newton.post(v.scalar_tensor_tensor(junk_v[:, r % JUNK, :], row, t[:, 0, r:r + 1], row, ALU.is_gt,
                                                           ALU.mult, accum_out=total[:, 0, r:r + 1]))
                    newton.settle()

                def newton_round(t, fast, inverse, meanwhile):
                    other = lambda j: lambda: meanwhile(j)
                    newton(v.reciprocal(inv[:, 0, :], t[:, 0, :]), other(0))
                    newton(v.tensor_tensor(ratio[:, 0, :], total[:, 0, :], inv[:, 0, :], ALU.mult), other(1))
                    newton(v.tensor_scalar(count[:, 0, :], ratio[:, 0, :], -0.45, ROUND, ALU.add, ALU.add), other(2))
                    newton(v.tensor_scalar(count[:, 0, :], count[:, 0, :], -ROUND, 1.0, ALU.add, ALU.max), other(3))
                    newton(v.reciprocal(inverse, count[:, 0, :]), other(4))
                    newton(v.scalar_tensor_tensor(ratio[:, 0, :], total[:, 0, :], -1.0, inverse, ALU.add, ALU.mult), other(5))
                    if fast:
                        newton.post(v.tensor_tensor(step_[:, 0, :], ratio[:, 0, :], tau[:, 0, :], ALU.subtract))
                        newton.post(v.tensor_tensor(low[:, 0, :], low[:, 0, :], ratio[:, 0, :], ALU.max))
                        meanwhile(6)
                        newton.settle(1)
                        newton(v.scalar_tensor_tensor(inv[:, 0, :], step_[:, 0, :], 0.25, count[:, 0, :], ALU.mult, ALU.mult), other(7))
                        newton(v.tensor_tensor(inv[:, 0, :], inv[:, 0, :], step_[:, 0, :], ALU.mult), other(8))
                        newton(v.tensor_tensor(tau[:, 0, :], inv[:, 0, :], ratio[:, 0, :], ALU.add), other(9))
                    else:
                        newton(v.tensor_tensor(low[:, 0, :], low[:, 0, :], ratio[:, 0, :], ALU.max), other(6))

                def exact_excess(g, rows):
                    for r in rows:
                        if r == DVE_ROWS[0]:
                            exact.start(g)
                            dve.wait_ge(tau4_made, g.n + 1)
                            if not g.c == 0:
                                dve.wait_ge(tau5_made, g.n)
                        if r >= DVE_ROWS[0] + 2:
                            exact.settle(1)
                        exact.post(v.scalar_tensor_tensor(junk_x[:, r % 2, :], s_sb[:, g.c % 4, r // T, r % T, 0:LK],
                                                          neg4[:, g.c % 2, r:r + 1], zero[:, 0:1].to_broadcast([P, LK]), ALU.add,
                                                          ALU.max, accum_out=f4[:, 0, r:r + 1]))

                def step(k, loads, search, refines, outputs, projects):
                    nxt, last, old = k.plus(1), k.plus(-1), k.plus(-2)
                    if search:
                        largest(k, range(3 * T, ROWS))
                        dve.wait_ge(top_made, k.n + 1)
                        first_guess(k)
                        newton.start(k)
                        dve.wait_ge(sh_kept, (k.n + 1) * (2 * G))
                        newton(v.tensor_tensor(tau[:, 0, :], tau[:, 0, :], low[:, 0, :], ALU.max))
                        sums_above(k, tau)
                        newton_round(tau, True, inv[:, 0, :], lambda j: exact_excess(last, DVE_ROWS[j:j + 1]) if refines else None)
                        sums_above(k, tau)
                        newton_round(tau, True, inv[:, 0, :], lambda j: largest(nxt, (j,)) if loads and j < T else None)
                        sums_above(k, low)
                    else:
                        if refines:
                            exact_excess(last, DVE_ROWS)
                        if loads:
                            largest(nxt, range(T))
                    if search:
                        newton_round(low, False, inv4[:, k.c % 2, :], lambda j: largest(nxt, (T + j,)) if loads and j < T else None)
                        v.tensor_scalar(neg4[:, k.c % 2, :], low[:, 0, :], -1.0, SHIFT, ALU.mult, ALU.add).then_inc(tau4_made, 1)
                        newton.end()
                    elif loads:
                        largest(nxt, range(T, 2 * T))
                    if loads:
                        largest(nxt, range(2 * T, 3 * T))
                v.memset(zero[:, :], 0.0).then_inc(dve_first, 1)
                dve.wait_ge(dve_first, 1)
                steps(dve, step)


def raise_flag(nc, ident, miss, flag):
    with ExitStack() as ctx:
        sb = lambda name, shape, dt=F32: ctx.enter_context(nc.sbuf_tensor(name, shape, dt))
        sem = lambda name: ctx.enter_context(nc.semaphore(name))
        ok, ok_made = sb("ok", [P, ROWS]), sem("ok_made")
        least, least_all = sb("least", [P, 1]), sb("least_all", [1, 1])
        turned = ctx.enter_context(nc.psum_tensor("flag_ps", [P, 512], F32))
        least_made, flag_turned, flag_made = sem("least_made"), sem("flag_turned"), sem("flag_made")
        with nc.Block() as block:
            @block.vector
            def _(dve):
                nc.vector.tensor_scalar(ok[:, :], miss[:, :], TOL * TOL, None, ALU.is_le).then_inc(ok_made, 1)
                dve.wait_ge(ok_made, 1)
                nc.vector.tensor_reduce(least[:, :], ok[:, :], AX.X, ALU.min).then_inc(least_made, 1)
                dve.wait_ge(flag_turned, 1)
                nc.vector.tensor_reduce(least_all[:, :], turned[0:1, 0:P], AX.X, ALU.min).then_inc(flag_made, 1)
                dve.wait_ge(flag_made, 1)
                nc.vector.tensor_copy(flag[:, :], least_all[:, :]).then_inc(flag_made, 1)
                dve.wait_ge(flag_made, 2)

            @block.tensor
            def _(pe):
                pe.wait_ge(least_made, 1)
                nc.tensor.transpose(turned[0:1, 0:P], least[:, :], ident[:, :]).then_inc(flag_turned, 1)
                pe.wait_ge(flag_turned, 1)


def general_cross_attention(nc, a, x_sb, ident, quad_mask, flag, wk, wv, wo, bk, q_t, vl_dram, row):
    with ExitStack() as ctx:
        sb = lambda name, shape, dt=F32: ctx.enter_context(nc.sbuf_tensor(name, shape, dt))
        sem = lambda name: ctx.enter_context(nc.semaphore(name))
        ps = lambda name, shape: ctx.enter_context(nc.psum_tensor(name, shape, F32))
        ctx_sb = sb("g_ctx", [P, G, NC, LK])
        vl = sb("g_vl", [T, G, D])
        k_t = sb("g_k", [P, NC, LK])
        q_bd = sb("g_bd", [P, NC, P])
        v_sb = sb("g_v", [P, 2, D])
        s_sb = sb("g_s", [P, T, LK])
        zeros = sb("g_zeros", [P, LK])
        junk = sb("g_junk", [P, 2, T, LK])
        low, excess, count, inv, neg = (sb(f"g_{n}", [P, T]) for n in ("low", "excess", "count", "inv", "neg"))
        a_t = sb("g_at", [P, 2, T * P])
        al_t = sb("g_alt", [T, P])
        om = sb("g_om", [P, NC, T, LQ])
        o_t = sb("g_ot", [P, NC, P])
        kv_ps = ps("g_kvps", [P, 2, 512])
        s_ps = ps("g_sps", [P, T, 512])
        t_ps = s_ps[:, 0:2, :]
        o_ps = ps("g_ops", [P, 512])
        y_ps = ps("g_yps", [P, 512])
        zeroed, row_in, row_added, loaded, vl_loaded = (sem(f"g_{n}") for n in (
            "zeroed", "row_in", "row_added", "loaded", "vl_loaded"))
        k_made, k_kept, bd_made, s_made, s_kept = (sem(f"g_{n}") for n in ("k_made", "k_kept", "bd_made", "s_made", "s_kept"))
        dve_waited = sem("g_waited")
        v_made, v_kept, newton, stepped, w_made, turned, a_kept = (sem(f"g_{n}") for n in (
            "v_made", "v_kept", "newton", "stepped", "w_made", "turned", "a_kept"))
        o_made, o_masked, o_kept, y_made, y_kept = (sem(f"g_{n}") for n in ("o_made", "o_masked", "o_kept", "y_made", "y_kept"))
        START, EACH = 3, 4

        with nc.Block() as block:
            def needed(e):
                return e.If(e.value_load(flag[0:1, 0:1], min_val=0, max_val=1) < 1)

            @block.sync
            def _(sp):
                with needed(sp):
                    sp.dma_start(x_sb[:, :, :], a["x"]).then_inc(row_in, 16)
                    with sp.Fori(0, NG) as g:
                        sp.wait_ge(v_made, g * G)
                        sp.dma_start(ctx_sb[:, :, :, :], a["ctx_t"][bass.ds(g, 1)].rearrange("o p b c l -> (o p) b c l")
                                     ).then_inc(loaded, 16)
                        sp.wait_ge(o_made, g * G)
                        with nc.allow_non_contiguous_dma(reason="one row of 1 KiB for each quad"):
                            sp.dma_start(vl[:, :, :], vl_dram[bass.ds(g * G, G)].rearrange("b t n -> t b n")
                                         ).then_inc(vl_loaded, 16)
                sp.nop()

            @block.gpsimd
            def _(pool):
                with needed(pool):
                    with pool.Fori(0, B) as n:
                        pool.wait_ge(s_made, n)
                        qv = q_t[:, :, bass.ds(n * LQ, LQ)].unsqueeze(2).to_broadcast([P, NC, T, LQ])
                        mv = quad_mask[:, :].unsqueeze(1).unsqueeze(3).to_broadcast([P, NC, T, LQ])
                        nc.gpsimd.tensor_tensor(q_bd[:, :, :].rearrange("p c (j q) -> p c j q", j=T), qv, mv, ALU.mult
                                                ).then_inc(bd_made, 1)
                pool.nop()

            @block.tensor
            def _(pe):
                with needed(pe):
                    with pe.Fori(0, NG) as g:
                        pe.wait_ge(loaded, g * 16 + 16)
                        pe.wait_ge(vl_loaded, g * 16 + 16)
                        for b in range(G):
                            n = g * G + b
                            pe.wait_ge(v_kept, n)
                            for m in range(NC):
                                for c in range(NC):
                                    mm = nc.tensor.matmul(kv_ps[:, m, 0:LK], wk[:, c, m * P:(m + 1) * P], ctx_sb[:, b, c, :],
                                                          start=(c == 0), stop=(c == NC - 1))
                            mm.then_inc(k_made, 1)
                            pe.wait_ge(k_kept, n + 1)
                            pe.wait_ge(bd_made, n + 1)
                            pe.wait_ge(a_kept, n)
                            for t in range(T):
                                h = slice(64 * (t % 2), 64 * (t % 2) + 64)
                                mm = nc.tensor.matmul(s_ps[:, t, 0:LK], q_bd[h, t // 2, :], k_t[h, t // 2, :],
                                                      start=True, stop=True)
                            mm.then_inc(s_made, 1)
                            for j in range(2):
                                for c in range(NC):
                                    mm = nc.tensor.matmul(kv_ps[:, j, 0:D], ctx_sb[:, b, c, j * P:(j + 1) * P], wv[:, c, :],
                                                          start=(c == 0), stop=(c == NC - 1))
                            mm.then_inc(v_made, 1)
                            pe.wait_ge(w_made, n + 1)
                            pe.wait_ge(s_kept, n + 1)
                            pe.wait_ge(o_kept, n)
                            for t in range(T):
                                for j in range(2):
                                    nc.tensor.transpose(t_ps[:, j, t * P:(t + 1) * P], s_sb[:, t, j * P:(j + 1) * P], ident[:, :])
                            nc.tensor.transpose(o_ps[0:T, D:D + P], s_sb[:, :, LM], ident[:, :]).then_inc(turned, 1)
                            pe.wait_ge(a_kept, n + 1)
                            pe.wait_ge(v_kept, n + 1)
                            for c in range(NC):
                                cols = slice(c * P, (c + 1) * P)
                                nc.tensor.matmul(o_ps[:, cols], vl[:, b, cols], al_t[:, :], start=True, stop=False,
                                                 skip_group_check=True)
                                for t in (2 * c, 2 * c + 1):
                                    for j in range(2):
                                        mm = nc.tensor.matmul(
                                            o_ps[64 * (t % 2):64 * (t % 2) + 64, cols], v_sb[:, j, 64 * t:64 * t + 64],
                                            a_t[:, j, t * P:(t + 1) * P], start=False, stop=(j == 1), skip_group_check=True)
                            mm.then_inc(o_made, 1)
                        pe.wait_ge(o_kept, g * G + G)
                        pe.wait_ge(y_kept, g)
                        for c in range(NC):
                            mm = nc.tensor.matmul(y_ps[:, 0:D], o_t[:, c, :], wo[:, c, :], start=(c == 0), stop=(c == NC - 1))
                        mm.then_inc(y_made, 1)
                pe.nop()

            @block.scalar
            def _(act):
                with needed(act):
                    with act.Fori(0, B) as n:
                        act.wait_ge(k_made, n + 1)
                        for m in range(NC):
                            ins = nc.scalar.activation(k_t[:, m, :], kv_ps[:, m, 0:LK], ACT.Identity, bias=bk[:, m:m + 1])
                        ins.then_inc(k_kept, 1)
                        act.wait_ge(s_made, n + 1)
                        nc.scalar.activation(s_sb[:, :, :], s_ps[:, :, 0:LK], ACT.Copy).then_inc(s_kept, 1)
                        act.wait_ge(v_made, n + 1)
                        nc.scalar.activation(v_sb[:, :, :], kv_ps[:, :, 0:D], ACT.Copy).then_inc(v_kept, 1)
                        act.wait_ge(turned, n + 1)
                        nc.scalar.activation(al_t[:, :], o_ps[0:T, D:D + P], ACT.Copy)
                        nc.scalar.activation(a_t[:, :, :], t_ps, ACT.Copy).then_inc(a_kept, 1)
                act.nop()

            @block.vector
            def _(dve):
                v = nc.vector
                with needed(dve):
                    v.memset(zeros[:, :], 0.0).then_inc(zeroed, 1)
                    dve.wait_ge(zeroed, 1)
                    dve.wait_ge(row_in, 16)
                    v.tensor_tensor(x_sb[:, :, :], x_sb[:, :, :], row[:, :].unsqueeze(1).to_broadcast([P, NG, D]), ALU.add
                                    ).then_inc(row_added, 1)
                    dve.wait_ge(row_added, 1)
                    with dve.Fori(0, NG) as g:
                        for b in range(G):
                            n = g * G + b
                            done = n * (START + EACH * SLOW_STEPS)
                            dve.wait_ge(s_kept, n + 1)
                            v.tensor_reduce(low[:, :], s_sb[:, :, :], AX.X, ALU.max).then_inc(newton, 1)
                            dve.wait_ge(newton, done + 1)
                            v.tensor_scalar(low[:, :], low[:, :], -1.0, None, ALU.add).then_inc(newton, 1)
                            dve.wait_ge(newton, done + 2)
                            dve.sem_inc(dve_waited, 1)
                            with dve.Fori(0, SLOW_STEPS) as k:
                                at = done + k * EACH + 2
                                for t in range(T):
                                    v.scalar_tensor_tensor(junk[:, 0, t, :], s_sb[:, t, :], low[:, t:t + 1], zeros[:, :],
                                                           ALU.subtract, ALU.max, accum_out=excess[:, t:t + 1])
                                    ins = v.tensor_scalar(junk[:, 1, t, :], s_sb[:, t, :], low[:, t:t + 1], None, ALU.is_gt,
                                                          ALU.add, accum_out=count[:, t:t + 1])
                                ins.then_inc(newton, 1)
                                dve.wait_ge(newton, at + 1)
                                v.tensor_scalar(count[:, :], count[:, :], 1.0, None, ALU.max).then_inc(newton, 1)
                                dve.wait_ge(newton, at + 2)
                                v.reciprocal(inv[:, :], count[:, :]).then_inc(newton, 1)
                                dve.wait_ge(newton, at + 3)
                                v.scalar_tensor_tensor(inv[:, :], excess[:, :], -1.0, inv[:, :], ALU.add, ALU.mult
                                                       ).then_inc(newton, 1)
                                dve.wait_ge(newton, at + 4)
                                v.scalar_tensor_tensor(low[:, :], inv[:, :], 0.0, low[:, :], ALU.max, ALU.add
                                                       ).then_inc(stepped, 1)
                                dve.wait_ge(stepped, n * SLOW_STEPS + k + 1)
                            v.tensor_scalar(neg[:, :], low[:, :], -1.0, None, ALU.mult).then_inc(newton, 1)
                            dve.wait_ge(newton, done + START + EACH * SLOW_STEPS)
                            for t in range(T):
                                ins = v.tensor_scalar(s_sb[:, t, :], s_sb[:, t, :], neg[:, t:t + 1], 0.0, ALU.add, ALU.max)
                            ins.then_inc(w_made, 1)
                            dve.wait_ge(o_made, n + 1)
                            ov = o_ps[:, 0:D].rearrange("p (c j q) -> p c j q", c=NC, j=T)
                            mv = quad_mask[:, :].unsqueeze(1).unsqueeze(3).to_broadcast([P, NC, T, LQ])
                            v.tensor_tensor(om[:, :, :, :], ov, mv, ALU.mult).then_inc(o_masked, 1)
                            dve.wait_ge(o_masked, n + 1)
                            v.tensor_reduce(o_t[:, :, b * LQ:(b + 1) * LQ], om[:, :, :, :].rearrange("p c j q -> p c q j"),
                                            AX.X, ALU.add).then_inc(o_kept, 1)
                            dve.wait_ge(o_kept, n + 1)
                        dve.wait_ge(y_made, g + 1)
                        xt = x_sb[:, bass.ds(g, 1), :].rearrange("p o d -> p (o d)")
                        v.tensor_tensor(xt, y_ps[:, 0:D], xt, ALU.add).then_inc(y_kept, 1)
                        dve.wait_ge(y_kept, g + 1)
                dve.nop()


def attention_and_experts(nc, a, x_sb, ident, quad_mask, out):
    with ExitStack() as ctx:
        sb = lambda name, shape, dt=F32: ctx.enter_context(nc.sbuf_tensor(name, shape, dt))
        sem = lambda name: ctx.enter_context(nc.semaphore(name))
        ps = lambda name, shape: ctx.enter_context(nc.psum_tensor(name, shape, F32))
        w_qkv = sb("w_qkv", [P, NC, 3 * D])
        w_proj = sb("w_proj", [P, NC, D])
        b_qk, b_qs, b_v = sb("b_qk", [P, 4]), sb("b_qs", [P, NC]), sb("b_v", [P, NC])
        b_vb = sb("b_vb", [P, NC, P])
        b_proj = sb("b_proj", [1, D])
        w_exp = sb("w_exp", [P, NC, E * D])
        b_exp = sb("b_exp", [E, D])
        w_rt, b_rt = sb("w_rt", [P, NC, E]), sb("b_rt", [1, E])
        causal = sb("causal", [P, LQ])
        rank = sb("rank", [P, E])
        ones = sb("s_ones", [1, P])
        power = sb("power", [P, NG])
        row = sb("s_row", [P, D])

        stats, mv = sb("stats1", [P, NG, 6]), sb("mv1", [P, NG, 2])
        var1, root1, half1 = sb("var1", [P, NG]), sb("root1", [P, NG]), sb("half1", [P, NG])
        xn1, xt1 = sb("xn1", [P, 2, D]), sb("xt1", [P, 2, NC, P])
        q_t, k_t = sb("s_q", [P, 2, NC, P]), sb("s_k", [P, 2, NC, P])
        v_sb = sb("s_v", [P, 2, G, D])
        batch_mask = sb("batch_mask", [P, G])
        q_bd = sb("s_bd", [P, 2, NC, G, T * LQ])
        s_sb = sb("s_s", [P, 2, T * G, LQ])
        top, den, inv = sb("s_top", [P, T * G]), sb("s_den", [P, T * G]), sb("s_inv", [P, T * G])
        p_t = sb("s_pt", [P, 2, T, P])
        o_sb = sb("s_o", [P, NC, G, T * LQ])
        om = sb("s_om", [P, NC * G, T, LQ])
        o_pair = sb("s_opair", [P, NC * G, 2, LQ])
        o_t = sb("s_ot", [P, 2, NC, P])
        xr = sb("xr", [P, 2, D])
        x2 = sb("x2", [P, 2, D])
        st2, mv2, var2, root2, half2 = sb("st2", [P, 6]), sb("mv2", [P, 2]), sb("var2", [P, 1]), sb("root2", [P, 1]), sb("half2", [P, 1])
        xn2, xt2 = sb("xn2", [P, 2, D]), sb("xt2", [P, 2, NC, P])
        r_top, r_exp, r_den, r_w = sb("r_top", [P, 1]), sb("r_exp", [P, E]), sb("r_den", [P, 1]), sb("r_w", [P, 1])
        r_max, r_sel, r_best, gate = sb("r_max", [P, 1]), sb("r_sel", [P, E]), sb("r_best", [P, 1]), sb("gate", [P, 2, E])
        gate_t = sb("gate_t", [E, P])
        acc = sb("acc", [P, 2, D])

        a_ps = ps("a_ps", [P, 512])
        qk_ps = ps("qk_ps", [P, 512])
        s_ps = ps("ss_ps", [P, 2, 512])
        c_ps = ps("c_ps", [P, 512])
        o_ps = ps("so_ps", [P, 512])
        e_ps = ps("e_ps", [P, 2, 512])

        w_in, e_in, consts, biases, row_made = sem("s_win"), sem("s_ein"), sem("s_consts"), sem("s_biases"), sem("s_rowmade")
        ln1, var1_made, root1_made = sem("ln1"), sem("var1_made"), sem("root1_made")
        dve_waited = sem("s_waited")
        normed1, turned1, kept1 = sem("normed1"), sem("turned1"), sem("kept1")
        qk_made, qk_kept, v_made, v_kept, bd_made = (sem(f"s_{n}") for n in ("qk_made", "qk_kept", "v_made", "v_kept", "bd_made"))
        s_made, masked, softmax, exp_made, probs_made = (sem(f"s_{n}") for n in ("s_made", "masked", "softmax", "exp_made", "probs_made"))
        p_turned, p_kept, o_made, o_copied = (sem(f"s_{n}") for n in ("p_turned", "p_kept", "o_made", "o_copied"))
        o_masked, o_paired, o_kept = (sem(f"s_{n}") for n in ("o_masked", "o_paired", "o_kept"))
        xr_made, y_made, x2_made = sem("xr_made"), sem("s_y_made"), sem("x2_made")
        dve_second, dve_route, dve_total, var2_made, root2_made, normed2, turned2, kept2 = (sem(n) for n in (
            "dve_second", "dve_route", "dve_total", "var2_made", "root2_made", "normed2", "turned2", "kept2"))
        l_made, r_top_made, r_exp_made, gate_made, gate_turned, gate_kept, eb_made, eb_taken = (sem(n) for n in (
            "l_made", "r_top_made", "r_exp_made", "gate_made", "gate_turned", "gate_kept", "eb_made", "eb_taken"))
        e_made, e_taken, stored = sem("e_made"), sem("e_taken"), [sem("stored0"), sem("stored1")]

        def steps(e, step):
            peeled = lambda c: step(Tile(0, c, 2), *(0 <= c + d < NG for d in (2, 1, 0, -1, -2)))
            for c in range(-2, 4):
                peeled(c)
            with e.Fori(0, (NG - 6) // 2) as i:
                for c in (4, 5):
                    step(Tile(i, c, 2), True, True, True, True, True)
            for c in range(NG - 2, NG + 2):
                peeled(c)

        def head_mask(n):
            return quad_mask[:, :].unsqueeze(1).unsqueeze(3).to_broadcast([P, n, T, LQ])

        with nc.Block() as block:
            @block.sync
            def _(sp):
                for t, name in ((w_qkv, "w_qkv"), (w_proj, "w_proj"), (b_qk, "b_qk"), (b_v, "b_v2"), (b_proj, "b_proj"),
                                (b_exp, "b_exp"), (w_rt, "w_rt"), (b_rt, "b_rt"), (causal, "causal"), (rank, "rank"), (batch_mask, "batch_mask")):
                    sp.dma_start(t[:], a[name]).then_inc(w_in, 16)
                sp.dma_start(w_exp[:, :, :], a["w_exp"]).then_inc(e_in, 16)

                def store(g, par):
                    sp.wait_ge(e_taken, g * 4 + 4)
                    sp.dma_start(out[:, bass.ds(g, 1), :].rearrange("p o d -> p (o d)"), acc[:, par, :]).then_inc(stored[par], 16)
                with sp.Fori(0, NG // 2) as i:
                    store(i * 2, 0)
                    store(i * 2 + 1, 1)
                sp.wait_ge(stored[0], NG // 2 * 16)
                sp.wait_ge(stored[1], NG // 2 * 16)

            @block.gpsimd
            def _(pool):
                nc.gpsimd.memset(ones[:, :], 1.0).then_inc(consts, 1)
                nc.gpsimd.memset(power[:, :], -0.5).then_inc(consts, 1)
                pool.wait_ge(consts, 2)
                pool.wait_ge(var1_made, 1)
                nc.gpsimd.tensor_tensor(root1[:, :], var1[:, :], power[:, :], ALU.pow).then_inc(root1_made, 1)

                def root_of(g):
                    pool.wait_ge(var2_made, g.n + 1)
                    nc.gpsimd.tensor_tensor(root2[:, :], var2[:, :], power[:, 0:1], ALU.pow).then_inc(root2_made, 1)

                def block_diagonal(g):
                    pool.wait_ge(qk_kept, g.n + 1)
                    if g.from_two():
                        pool.wait_ge(s_made, g.n - 1)
                    for c in range(NC):
                        qv = q_t[:, g.c % 2, c, :].rearrange("p (b q) -> p b q", b=G).unsqueeze(2).to_broadcast([P, G, T, LQ])
                        ins = nc.gpsimd.tensor_tensor(q_bd[:, g.c % 2, c].rearrange("p b (j q) -> p b j q", j=T), qv,
                                                      head_mask(G), ALU.mult)
                    ins.then_inc(bd_made, 1)

                def residual_input(g):
                    if g.from_two():
                        pool.wait_ge(x2_made, g.n - 1)
                    else:
                        pool.wait_ge(row_made, 2)
                    xt = x_sb[:, bass.ds(g.n, 1), :].rearrange("p o d -> p (o d)")
                    nc.gpsimd.tensor_tensor(xr[:, g.c % 2, :], xt, row[:, :], ALU.add).then_inc(xr_made, 1)

                def gather_output(g, c):
                    n = g.n * 2 + c
                    half = slice(c * G, (c + 1) * G)
                    pool.wait_ge(o_copied, n + 1)
                    nc.gpsimd.tensor_tensor(om[:, half, :, :], o_sb[:, c].rearrange("p b (j q) -> p b j q", j=T),
                                            head_mask(G), ALU.mult).then_inc(o_masked, 1)
                    pool.wait_ge(o_masked, n + 1)
                    nc.gpsimd.tensor_tensor(o_pair[:, half, :, :], om[:, half, 0:2, :], om[:, half, 2:4, :], ALU.add
                                            ).then_inc(o_paired, 1)
                    pool.wait_ge(o_paired, n + 1)
                    if c == 0 and g.from_two():
                        pool.wait_ge(y_made, g.n - 1)
                    nc.gpsimd.tensor_tensor(o_t[:, g.c % 2, c].rearrange("p (b q) -> p b q", b=G), o_pair[:, half, 0, :],
                                            o_pair[:, half, 1, :], ALU.add).then_inc(o_kept, 1)
                    pool.wait_ge(o_kept, n + 1)

                def step(k, prepares, projects, attends, leads, ends):
                    if attends:
                        residual_input(k)
                    if leads:
                        root_of(k.plus(-1))
                    if projects:
                        block_diagonal(k.plus(1))
                    if attends:
                        gather_output(k, 0)
                        gather_output(k, 1)
                steps(pool, step)

            @block.tensor
            def _(pe):
                pe.wait_ge(w_in, 11 * 16)
                pe.wait_ge(consts, 2)
                pe.wait_ge(biases, 1)
                for c in range(NC):
                    nc.tensor.matmul(c_ps[:, 0:D], b_vb[:, c, :], w_proj[:, c, :], start=(c == 0), stop=False)
                nc.tensor.matmul(c_ps[:, 0:D], ones[:, :], b_proj[:, :], start=False, stop=True).then_inc(row_made, 1)

                def turn_first(g):
                    pe.wait_ge(normed1, g.n + 1)
                    if g.c:
                        pe.wait_ge(v_kept, g.n)
                    for c in range(NC):
                        mm = nc.tensor.transpose(a_ps[:, c * P:(c + 1) * P], xn1[:, g.c % 2, c * P:(c + 1) * P], ident[:, :])
                    mm.then_inc(turned1, 1)

                def project_in(g):
                    pe.wait_ge(kept1, g.n + 1)
                    if g.c:
                        pe.wait_ge(qk_kept, g.n)
                    for m in range(4):
                        for c in range(NC):
                            mm = nc.tensor.matmul(qk_ps[:, m * P:(m + 1) * P], w_qkv[:, c, m * P:(m + 1) * P], xt1[:, g.c % 2, c, :],
                                                  start=(c == 0), stop=(c == NC - 1))
                    mm.then_inc(qk_made, 1)
                    for c in range(NC):
                        mm = nc.tensor.matmul(a_ps[:, D:2 * D], xt1[:, g.c % 2, c, :], w_qkv[:, c, 2 * D:3 * D],
                                              start=(c == 0), stop=(c == NC - 1))
                    mm.then_inc(v_made, 1)

                def scores(g):
                    pe.wait_ge(bd_made, g.n + 1)
                    pe.wait_ge(qk_kept, g.n + 1)
                    if g.c:
                        pe.wait_ge(p_kept, g.n)
                    for t in range(T):
                        h = slice(64 * (t % 2), 64 * (t % 2) + 64)
                        for b in range(G):
                            at = (t // 2 * G + b) * LQ
                            mm = nc.tensor.matmul(s_ps[:, t % 2, at:at + LQ], q_bd[h, g.c % 2, t // 2, b, :],
                                                  k_t[h, g.c % 2, t // 2, b * LQ:(b + 1) * LQ], start=True, stop=True)
                    mm.then_inc(s_made, 1)

                def turn_probs(g):
                    pe.wait_ge(probs_made, g.n + 1)
                    for t in range(T):
                        mm = nc.tensor.transpose(s_ps[:, t % 2, t // 2 * P:(t // 2 + 1) * P],
                                                 s_sb[:, g.c % 2, t * G:(t + 1) * G, :].rearrange("p b k -> p (b k)"), ident[:, :])
                    mm.then_inc(p_turned, 1)

                def attend(g, c):
                    pe.wait_ge(p_kept, g.n + 1)
                    pe.wait_ge(v_kept, g.n + 1)
                    if g.c or c:
                        pe.wait_ge(o_copied, g.n * 2 + c)
                    for t in (2 * c, 2 * c + 1):
                        for b in range(G):
                            mm = nc.tensor.matmul(o_ps[64 * (t % 2):64 * (t % 2) + 64, b * P:(b + 1) * P],
                                                  v_sb[:, g.c % 2, b, 64 * t:64 * t + 64], p_t[:, g.c % 2, t, :],
                                                  start=True, stop=True)
                    mm.then_inc(o_made, 1)

                def project_out(g):
                    pe.wait_ge(o_kept, g.n * 2 + 2)
                    pe.wait_ge(row_made, 2)
                    if g.c:
                        pe.wait_ge(r_exp_made, g.n)
                    for c in range(NC):
                        mm = nc.tensor.matmul(c_ps[:, 0:D], o_t[:, g.c % 2, c, :], w_proj[:, c, :], start=(c == 0), stop=(c == NC - 1))
                    mm.then_inc(y_made, 1)

                def turn_second(g):
                    pe.wait_ge(normed2, g.n + 1)
                    if g.c:
                        pe.wait_ge(eb_taken, g.n)
                    for c in range(NC):
                        mm = nc.tensor.transpose(c_ps[:, D + c * P:D + (c + 1) * P], xn2[:, g.c % 2, c * P:(c + 1) * P], ident[:, :])
                    mm.then_inc(turned2, 1)

                def route(g):
                    pe.wait_ge(kept2, g.n + 1)
                    for c in range(NC):
                        nc.tensor.matmul(c_ps[:, D:D + E], xt2[:, g.c % 2, c, :], w_rt[:, c, :], start=(c == 0), stop=False)
                    nc.tensor.matmul(c_ps[:, D:D + E], ones[:, :], b_rt[:, :], start=False, stop=True).then_inc(l_made, 1)

                def turn_gates(g, leads):
                    if leads:
                        pe.wait_ge(x2_made, g.n + 2)
                    else:
                        pe.wait_ge(r_exp_made, g.n + 1)
                    pe.wait_ge(gate_made, g.n + 1)
                    nc.tensor.transpose(c_ps[0:E, D:D + P], gate[:, g.c % 2, :], ident[:, :]).then_inc(gate_turned, 1)

                def gate_biases(g):
                    pe.wait_ge(gate_kept, g.n + 1)
                    nc.tensor.matmul(c_ps[:, 0:D], gate_t[:, :], b_exp[:, :], start=True, stop=True).then_inc(eb_made, 1)

                def experts(g, p):
                    if g.c < 2:
                        pe.wait_ge(e_in, 16)
                    if not (g.c == 0 and p < 2):
                        pe.wait_ge(e_taken, g.n * 4 + (p - 1))
                    for c in range(NC):
                        mm = nc.tensor.matmul(e_ps[:, p % 2, :], xt2[:, g.c % 2, c, :], w_exp[:, c, p * 512:(p + 1) * 512],
                                              start=(c == 0), stop=(c == NC - 1))
                    mm.then_inc(e_made, 1)

                def step(k, prepares, projects, attends, leads, ends):
                    nxt, last, done = k.plus(1), k.plus(-1), k.plus(-2)
                    if attends:
                        scores(k)
                    if projects:
                        turn_first(nxt)
                    if ends:
                        experts(done, 0)
                    if leads:
                        project_out(last)
                    if ends:
                        experts(done, 1)
                    if projects:
                        project_in(nxt)
                    if ends:
                        turn_gates(done, leads)
                    if attends:
                        turn_probs(k)
                    if ends:
                        gate_biases(done)
                        experts(done, 2)
                    if attends:
                        attend(k, 0)
                    if leads:
                        turn_second(last)
                    if ends:
                        experts(done, 3)
                    if attends:
                        attend(k, 1)
                    if leads:
                        route(last)
                steps(pe, step)

            @block.scalar
            def _(act):
                act.wait_ge(biases, 2)

                def keep_output(g, c):
                    act.wait_ge(o_made, g.n * 2 + (c + 1))
                    if g.c:
                        act.wait_ge(o_masked, g.n * 2 + (c - 1))
                    nc.scalar.activation(o_sb[:, c].rearrange("p b n -> p (b n)"), o_ps[:, :], ACT.Copy).then_inc(o_copied, 1)

                def keep_projections(g):
                    act.wait_ge(qk_made, g.n + 1)
                    if g.from_two():
                        act.wait_ge(bd_made, g.n - 1)
                        act.wait_ge(s_made, g.n - 1)
                    for m in range(NC):
                        nc.scalar.activation(q_t[:, g.c % 2, m, :], qk_ps[:, m * P:(m + 1) * P], ACT.Identity,
                                             bias=b_qs[:, m:m + 1], scale=SCALE)
                        ins = nc.scalar.activation(k_t[:, g.c % 2, m, :], qk_ps[:, D + m * P:D + (m + 1) * P], ACT.Identity,
                                                   bias=b_qk[:, 2 + m:3 + m])
                    ins.then_inc(qk_kept, 1)

                def keep_values(g):
                    act.wait_ge(v_made, g.n + 1)
                    if g.from_two():
                        act.wait_ge(o_made, g.n * 2 - 2)
                    for b in range(G):
                        ins = nc.scalar.activation(v_sb[:, g.c % 2, b, :], a_ps[:, D:2 * D], ACT.Copy,
                                                   scale=batch_mask[:, b:b + 1])
                    ins.then_inc(v_kept, 1)

                def step(k, prepares, projects, attends, leads, ends):
                    nxt, last, done = k.plus(1), k.plus(-1), k.plus(-2)
                    if projects:
                        act.wait_ge(turned1, nxt.n + 1)
                        nc.scalar.activation(xt1[:, nxt.c % 2].rearrange("p c n -> p (c n)"), a_ps[:, 0:D], ACT.Copy).then_inc(kept1, 1)
                    if attends:
                        act.wait_ge(masked, k.n + 1)
                        sv = s_sb[:, k.c % 2].rearrange("p r k -> p (r k)")
                        nc.scalar.activation(sv, sv, ACT.Exp).then_inc(exp_made, 1)
                    if projects:
                        keep_projections(nxt)
                    if ends:
                        act.wait_ge(gate_turned, done.n + 1)
                        nc.scalar.activation(gate_t[:, :], c_ps[0:E, D:D + P], ACT.Copy).then_inc(gate_kept, 1)
                    if attends:
                        act.wait_ge(p_turned, k.n + 1)
                        for u in range(2):
                            ins = nc.scalar.activation(p_t[:, k.c % 2, u::2, :],
                                                       s_ps[:, u, 0:2 * P].rearrange("p (t n) -> p t n", t=2), ACT.Copy)
                        ins.then_inc(p_kept, 1)
                    if projects:
                        keep_values(nxt)
                    if attends:
                        keep_output(k, 0)
                    if leads:
                        act.wait_ge(turned2, last.n + 1)
                        nc.scalar.activation(xt2[:, last.c % 2].rearrange("p c n -> p (c n)"), c_ps[:, D:2 * D], ACT.Copy
                                             ).then_inc(kept2, 1)
                    if attends:
                        keep_output(k, 1)
                    if leads:
                        act.wait_ge(r_top_made, last.n + 1)
                        nc.scalar.activation(r_exp[:, :], c_ps[:, D:D + E], ACT.Exp, bias=r_top[:, :], accum_out=r_den[:, :]
                                             ).then_inc(r_exp_made, 1)
                steps(act, step)

            @block.vector
            def _(dve):
                v = nc.vector
                for g in range(NG):
                    ins = v.bn_stats(stats[:, g, :], x_sb[:, g, :])
                ins.then_inc(ln1, 1)
                dve.wait_ge(ln1, 1)
                for g in range(NG):
                    ins = v.bn_aggr(mv[:, g, :], stats[:, g, :])
                ins.then_inc(ln1, 1)
                dve.wait_ge(ln1, 2)
                v.tensor_scalar(var1[:, :], mv[:, :, 1], EPS, None, ALU.add).then_inc(var1_made, 1)
                dve.wait_ge(w_in, 11 * 16)
                for c in range(NC):
                    ins = v.tensor_copy(b_vb[:, c, :], b_v[:, c:c + 1].to_broadcast([P, P]))
                ins.then_inc(biases, 1)
                v.tensor_scalar(b_qs[:, :], b_qk[:, 0:2], SCALE, None, ALU.mult).then_inc(biases, 1)
                dve.wait_ge(var1_made, 1)
                dve.wait_ge(root1_made, 1)
                v.tensor_tensor(half1[:, :], root1[:, :], root1[:, :], ALU.mult).then_inc(ln1, 1)
                dve.wait_ge(ln1, 3)
                v.tensor_tensor(half1[:, :], half1[:, :], var1[:, :], ALU.mult).then_inc(ln1, 1)
                dve.wait_ge(ln1, 4)
                v.tensor_scalar(half1[:, :], half1[:, :], -0.5, 1.5, ALU.mult, ALU.add).then_inc(ln1, 1)
                dve.wait_ge(ln1, 5)
                v.tensor_tensor(root1[:, :], root1[:, :], half1[:, :], ALU.mult).then_inc(ln1, 1)
                dve.wait_ge(ln1, 6)
                dve.wait_ge(row_made, 1)
                v.tensor_copy(row[:, :], c_ps[:, 0:D]).then_inc(row_made, 1)

                class Chain:

                    def __init__(self, semaphore, per):
                        self.sem, self.per = semaphore, per

                    def start(self, g):
                        self.g, self.n = g, 0

                    def __call__(self, ins):
                        self.n += 1
                        ins.then_inc(self.sem, 1)
                        dve.wait_ge(self.sem, self.g.n * self.per + self.n)

                    def end(self):
                        assert self.n == self.per, self.n

                soft, second, route, total = Chain(softmax, 4), Chain(dve_second, 6), Chain(dve_route, 4), Chain(dve_total, 4)

                def normalise_first(g):
                    if g.from_two():
                        dve.wait_ge(turned1, g.n - 1)
                    if isinstance(g.n, int):
                        xt, mean, root = x_sb[:, g.n, :], mv[:, g.n, 0:1], root1[:, g.n:g.n + 1]
                    else:
                        xt = x_sb[:, bass.ds(g.n, 1), :].rearrange("p o d -> p (o d)")
                        mean = mv[:, bass.ds(g.n, 1), 0:1].rearrange("p o d -> p (o d)")
                        root = root1[:, bass.ds(g.n, 1)]
                    v.tensor_scalar(xn1[:, g.c % 2, :], xt, mean, root, ALU.subtract, ALU.mult).then_inc(normed1, 1)

                def residual(g):
                    second.start(g)
                    x2t = x2[:, g.c % 2, :]
                    dve.wait_ge(y_made, g.n + 1)
                    dve.wait_ge(xr_made, g.n + 1)
                    v.tensor_tensor(x2t, c_ps[:, 0:D], xr[:, g.c % 2, :], ALU.add).then_inc(x2_made, 1)
                    dve.wait_ge(x2_made, g.n + 1)
                    second(v.bn_stats(st2[:, :], x2t))
                    dve.sem_inc(dve_waited, 1)
                    second(v.bn_aggr(mv2[:, :], st2[:, :]))
                    v.tensor_scalar(var2[:, :], mv2[:, 1:2], EPS, None, ALU.add).then_inc(var2_made, 1)
                    dve.wait_ge(var2_made, g.n + 1)

                def normalise_second(g):
                    dve.wait_ge(root2_made, g.n + 1)
                    second(v.tensor_tensor(half2[:, :], root2[:, :], root2[:, :], ALU.mult))
                    second(v.tensor_tensor(half2[:, :], half2[:, :], var2[:, :], ALU.mult))
                    second(v.tensor_scalar(half2[:, :], half2[:, :], -0.5, 1.5, ALU.mult, ALU.add))
                    second(v.tensor_tensor(half2[:, :], half2[:, :], root2[:, :], ALU.mult))
                    second.end()
                    if g.from_two():
                        dve.wait_ge(turned2, g.n - 1)
                    v.tensor_scalar(xn2[:, g.c % 2, :], x2[:, g.c % 2, :], mv2[:, 0:1], half2[:, 0:1], ALU.subtract, ALU.mult
                                    ).then_inc(normed2, 1)

                def mask_scores(g):
                    soft.start(g)
                    dve.wait_ge(s_made, g.n + 1)
                    sv = s_sb[:, g.c % 2]
                    for u in range(2):
                        for w in range(2):
                            t = 2 * w + u
                            ins = v.tensor_tensor(sv[:, t * G:(t + 1) * G, :],
                                                  s_ps[:, u, w * P:(w + 1) * P].rearrange("p (b k) -> p b k", k=LQ),
                                                  causal[:, :].unsqueeze(1).to_broadcast([P, G, LQ]), ALU.add)
                    soft(ins)
                    soft(v.tensor_reduce(top[:, :], sv, AX.X, ALU.max))
                    v.tensor_tensor(sv, sv, top[:, :].unsqueeze(2).to_broadcast([P, T * G, LQ]), ALU.subtract).then_inc(masked, 1)

                def normalise_probs(g):
                    dve.wait_ge(exp_made, g.n + 1)
                    sv = s_sb[:, g.c % 2]
                    soft(v.tensor_reduce(den[:, :], sv, AX.X, ALU.add))
                    soft(v.reciprocal(inv[:, :], den[:, :]))
                    v.tensor_tensor(sv, sv, inv[:, :].unsqueeze(2).to_broadcast([P, T * G, LQ]), ALU.mult).then_inc(probs_made, 1)

                def likeliest(g):
                    dve.wait_ge(l_made, g.n + 1)
                    v.tensor_reduce(r_top[:, :], c_ps[:, D:D + E], AX.X, ALU.max, negate=True).then_inc(r_top_made, 1)

                def gates(g):
                    route.start(g)
                    dve.wait_ge(r_exp_made, g.n + 1)
                    route(v.reciprocal(r_w[:, :], r_den[:, :]))
                    route(v.tensor_reduce(r_max[:, :], r_exp[:, :], AX.X, ALU.max))
                    route(v.scalar_tensor_tensor(r_sel[:, :], r_exp[:, :], r_max[:, 0:1], rank[:, :], ALU.is_ge, ALU.mult))
                    route(v.tensor_reduce(r_best[:, :], r_sel[:, :], AX.X, ALU.max))
                    if g.from_two():
                        dve.wait_ge(gate_turned, g.n - 1)
                    v.tensor_scalar(gate[:, g.c % 2, :], r_sel[:, :], r_best[:, 0:1], r_w[:, 0:1], ALU.is_ge, ALU.mult
                                    ).then_inc(gate_made, 1)
                    dve.wait_ge(gate_made, g.n + 1)
                    route.end()

                def combine(g, p):
                    at = acc[:, g.c % 2, :]
                    if p == 0:
                        total.start(g)
                        if g.from_two():
                            dve.wait_ge(stored[g.c % 2], g.half * 16)
                    dve.wait_ge(e_made, g.n * 4 + (p + 1))
                    for e in (2 * p, 2 * p + 1):
                        ins = v.scalar_tensor_tensor(at, e_ps[:, p % 2, (e % 2) * D:(e % 2 + 1) * D], gate[:, g.c % 2, e:e + 1],
                                                     x2[:, g.c % 2, :] if e == 0 else at, ALU.mult, ALU.add)
                        if e % 2 == 0:
                            total(ins)
                    ins.then_inc(e_taken, 1)
                    dve.wait_ge(e_taken, g.n * 4 + (p + 1))

                def add_biases(g):
                    dve.wait_ge(eb_made, g.n + 1)
                    at = acc[:, g.c % 2, :]
                    v.tensor_tensor(at, c_ps[:, 0:D], at, ALU.add).then_inc(eb_taken, 1)
                    dve.wait_ge(eb_taken, g.n + 1)

                def step(k, prepares, projects, attends, leads, ends):
                    last, done = k.plus(-1), k.plus(-2)
                    if attends:
                        mask_scores(k)
                    if ends:
                        gates(done)
                        combine(done, 0)
                    if attends:
                        normalise_probs(k)
                    if leads:
                        residual(last)
                    if ends:
                        combine(done, 1)
                    if leads:
                        normalise_second(last)
                    if ends:
                        add_biases(done)
                        combine(done, 2)
                    if prepares:
                        normalise_first(k.plus(2))
                    if ends:
                        combine(done, 3)
                        total.end()
                    if leads:
                        likeliest(last)
                steps(dve, step)


def kernel(**inputs):
    import numpy as np
    import concourse.bacc as bacc
    from concourse.bass_utils import run_bass_kernel_spmd

    arrays = lay_out(**inputs)
    nc = bacc.Bacc("TRN2", target_bir_lowering=False, num_devices=1, dynamic_dma_scratch_size=1024)
    aps = {n: nc.dram_tensor(f"in_{n}", v.shape, F32, kind="ExternalInput").ap() for n, v in arrays.items()}
    out = nc.dram_tensor("out_x", (P, NG, D), F32, kind="ExternalOutput").ap()
    build(nc, aps, out)
    r = run_bass_kernel_spmd(nc, [{f"in_{n}": v for n, v in arrays.items()}], core_ids=[0])
    got = r.results[0]["out_x"]
    return np.ascontiguousarray(got.transpose(1, 0, 2)).reshape(B, LQ, D)


def lay_out(**inputs):
    import numpy as np

    i = {k: np.asarray(v) for k, v in inputs.items()}
    chunks = lambda w: w.reshape(NC, P, -1).transpose(1, 0, 2)
    column = lambda v: v.reshape(-1, P).T
    c = i["ctx_1024"]
    ctx_t = c.transpose(0, 2, 1).reshape(NG, G, NC, P, LK).transpose(0, 3, 1, 2, 4)
    channel = np.arange(P)
    arrays = {
        "x": i["x"].reshape(NG, P, D).transpose(1, 0, 2),
        "ctx_t": ctx_t,
        "ctx_last": c[:, LM, :].T.reshape(NC, P, B).transpose(1, 0, 2),
        "wq": chunks(i["L0_xattn_Wq"]), "wk": chunks(i["L0_xattn_Wk"]), "wv": chunks(i["L0_xattn_Wv"]),
        "wo": chunks(i["L0_xattn_Wo"]),
        "bq": column(i["L0_xattn_bq"]), "bk": column(i["L0_xattn_bk"]), "bv": column(i["L0_xattn_bv"]),
        "bo": i["L0_xattn_bo"].reshape(1, D),
        "w_qkv": chunks(i["L0_attn_W_attn"].T), "w_proj": chunks(i["L0_attn_W_proj"].T),
        "b_qk": column(i["L0_attn_b_attn"][:2 * D]), "b_v2": column(i["L0_attn_b_attn"][2 * D:]),
        "b_proj": i["L0_attn_b_proj"].reshape(1, D),
        "w_exp": chunks(i["L0_ffn_expert_w"].transpose(2, 0, 1).reshape(D, E * D)), "b_exp": i["L0_ffn_expert_b"],
        "w_rt": chunks(i["L0_ffn_router_w"].T), "b_rt": i["L0_ffn_router_b"].reshape(1, E),
        "causal": np.where(np.arange(LQ)[None, :] <= (channel % LQ)[:, None], 0.0, -1e30).astype(np.float32),
        "batch_mask": (channel[:, None] // LQ == np.arange(G)[None, :]).astype(np.float32),
        "rank": np.tile(E - np.arange(E, dtype=np.float32), (P, 1)),
        "ident": np.eye(P, dtype=np.float32),
        "quad_mask": (channel[:, None] % 64 // DH == np.arange(T)[None, :]).astype(np.float32),
    }
    return {n: np.ascontiguousarray(v) for n, v in arrays.items()}
```

```python
from contextlib import ExitStack

import concourse.bass as bass
from concourse import mybir

F32 = mybir.dt.float32
BF16 = mybir.dt.bfloat16
I32 = mybir.dt.int32
ALU = mybir.AluOpType
ACT = mybir.ActivationFunctionType
AX = mybir.AxisListType

P = 128
B, LQ, D = 64, 32, 256
LK = 257
LM = 256
H, DH = 16, 16
E = 8
NC = D // P
G = 4
NG = B // G
T = 4
ROWS = G * T
W = LK + 1
SCALE = 0.25
EPS = 1e-5
SHIFT = 8.0
ROUND = 1.5 * 2.0 ** 23
TOL = 2e-5
GUESS = (-0.0292, -0.0017, -0.1859, 0.264)
ACT_ROWS = (range(4), range(4, 7), range(7, 10))
DVE_ROWS = range(10, ROWS)
BUFFERS = 4
BESIDE_LAST = 7
JUNK = 4
SLOW_STEPS = 40


class Tile:

    def __init__(self, i, c, per=4):
        self.i, self.c, self.per = i, c, per
        self.n, self.half = i * per + c, i * (per // 2) + c // 2

    def plus(self, d):
        return Tile(self.i, self.c + d, self.per)

    def from_two(self):
        return not (isinstance(self.n, int) and self.c < 2)


def queries(nc, a, x_sb, ident, quad_mask, wk, wv, wo, bk, q_t, vl_dram, row, ctx_sb, ctx_in):
    with ExitStack() as ctx:
        sb = lambda name, shape, dt=F32: ctx.enter_context(nc.sbuf_tensor(name, shape, dt))
        sem = lambda name: ctx.enter_context(nc.semaphore(name))
        ps = lambda name, shape: ctx.enter_context(nc.psum_tensor(name, shape, F32))
        wq = sb("wq", [P, NC, D])
        bq, bq_s, bv = sb("bq", [P, NC]), sb("bq_s", [P, NC]), sb("bv", [P, NC])
        bv_b = sb("bv_b", [P, NC, P])
        bo = sb("bo", [1, D])
        ones = sb("ones", [1, P])
        last = sb("last", [P, NC, B])
        x_nt = sb("x_nt", [P, NC, B * LQ])
        vl_wide = sb("vl_wide", [B, T, D])
        stats, mv = sb("ln_stats", [P, NG, 6]), sb("ln_mv", [P, NG, 2])
        var, inv, root = sb("ln_var", [P, NG]), sb("ln_inv", [P, NG]), sb("ln_root", [P, NG])
        x_n = sb("ln_x", [P, BUFFERS, D])
        turned_ps = ps("ln_ps", [P, BUFFERS, 512])
        q_ps = ps("q_ps", [P, 2, 512])
        row_ps = ps("row_ps", [P, 512])
        last_ps = ps("last_ps", [B, 512])
        x_in = [sem(f"x_in{i}") for i in range(4)]
        wq_in, w_in, c_in = sem("wq_in"), sem("w_in"), sem("c_in")
        inv_made, root_made, dve_ln = sem("ln_inv_made"), sem("ln_root_made"), sem("dve_ln")
        normed, turned, kept = sem("ln_normed"), sem("ln_turned"), sem("ln_kept")
        q_made, q_kept = sem("q_made"), sem("q_kept")
        prepared, last_made, row_made, row_added = sem("prepared"), sem("last_made"), sem("row_made"), sem("row_added")
        widened, vl_out = sem("widened"), sem("vl_out")
        weights = ((wv, "wv"), (wo, "wo"), (wk, "wk"), (bq, "bq"), (bk, "bk"), (bv, "bv"), (bo, "bo"),
                   (last, "ctx_last"))

        def projected_after(g):
            return [g // 4 - 1] if g > 4 and g % 4 == 1 else [NG // 4 - 1] if g == NG - 1 else []

        with nc.Block() as block:
            @block.sync
            def _(sp):
                for i in range(4):
                    sp.dma_start(x_sb[:, 4 * i:4 * i + 4, :], a["x"][:, 4 * i:4 * i + 4, :]).then_inc(x_in[i], 16)
                sp.wait_ge(w_in, len(weights) * 16)
                for i in range(2):
                    sp.dma_start(ctx_sb[:, i], a["ctx_t"][i]).then_inc(ctx_in[i], 16)
                sp.wait_ge(widened, 1)
                sp.dma_start(vl_dram, vl_wide[:, :, :]).then_inc(vl_out, 16)
                sp.wait_ge(vl_out, 16)
                sp.wait_ge(c_in, 32)

            @block.gpsimd
            def _(pool):
                nc.gpsimd.memset(vl_wide[:, :, :], 0.0).then_inc(prepared, 1)
                nc.gpsimd.memset(ones[:, :], 1.0).then_inc(prepared, 1)

            @block.vector
            def _(dve):
                v = nc.vector
                for g in range(NG):
                    if g % 4 == 0:
                        dve.wait_ge(x_in[g // 4], 16)
                    ins = v.bn_stats(stats[:, g, :], x_sb[:, g, :])
                ins.then_inc(dve_ln, 1)
                dve.wait_ge(dve_ln, 1)
                for g in range(NG):
                    ins = v.bn_aggr(mv[:, g, :], stats[:, g, :])
                ins.then_inc(dve_ln, 1)
                dve.wait_ge(dve_ln, 2)
                v.tensor_scalar(var[:, :], mv[:, :, 1], EPS, None, ALU.add).then_inc(dve_ln, 1)
                dve.wait_ge(dve_ln, 3)
                v.reciprocal(inv[:, :], var[:, :]).then_inc(inv_made, 1)
                dve.wait_ge(root_made, 1)
                dve.wait_ge(inv_made, 1)
                v.tensor_tensor(inv[:, :], root[:, :], root[:, :], ALU.mult).then_inc(dve_ln, 1)
                dve.wait_ge(dve_ln, 4)
                v.tensor_tensor(inv[:, :], inv[:, :], var[:, :], ALU.mult).then_inc(dve_ln, 1)
                dve.wait_ge(dve_ln, 5)
                v.tensor_scalar(inv[:, :], inv[:, :], -0.5, 1.5, ALU.mult, ALU.add).then_inc(dve_ln, 1)
                dve.wait_ge(dve_ln, 6)
                v.tensor_tensor(root[:, :], root[:, :], inv[:, :], ALU.mult).then_inc(dve_ln, 1)
                dve.wait_ge(dve_ln, 7)
                for g in range(NG):
                    if g >= BUFFERS:
                        dve.wait_ge(turned, g - BUFFERS + 1)
                    v.tensor_scalar(x_n[:, g % BUFFERS, :], x_sb[:, g, :], mv[:, g, 0:1], root[:, g:g + 1],
                                    ALU.subtract, ALU.mult).then_inc(normed, 1)
                    if g == BUFFERS:
                        dve.wait_ge(w_in, len(weights) * 16)
                        v.tensor_scalar(bq_s[:, :], bq[:, :], SCALE, None, ALU.mult).then_inc(prepared, 1)
                        for c in range(NC):
                            ins = v.tensor_copy(bv_b[:, c, :], bv[:, c:c + 1].to_broadcast([P, P]))
                        ins.then_inc(prepared, 1)
                dve.wait_ge(prepared, 4)
                dve.wait_ge(last_made, 1)
                for t in range(T):
                    ins = v.tensor_copy(vl_wide[:, t, 64 * t:64 * t + 64], last_ps[:, 64 * t:64 * t + 64])
                ins.then_inc(widened, 1)
                dve.wait_ge(row_made, 1)
                v.tensor_copy(row[:, :], row_ps[:, 0:D]).then_inc(row_added, 1)
                dve.wait_ge(row_added, 1)
                dve.wait_ge(normed, NG)
                v.tensor_tensor(x_sb[:, :, :], x_sb[:, :, :], row[:, :].unsqueeze(1).to_broadcast([P, NG, D]), ALU.add
                                ).then_inc(row_added, 1)
                dve.wait_ge(row_added, 2)

            @block.scalar
            def _(act):
                act.dma_start(ident[:, :], a["ident"]).then_inc(c_in, 16)
                act.dma_start(quad_mask[:, :], a["quad_mask"]).then_inc(c_in, 16)
                act.dma_start(wq[:, :, :], a["wq"]).then_inc(wq_in, 16)
                for t, name in weights:
                    act.dma_start(t[:], a[name]).then_inc(w_in, 16)
                act.wait_ge(inv_made, 1)
                nc.scalar.activation(root[:, :], inv[:, :], ACT.Sqrt).then_inc(root_made, 1)
                for g in range(NG):
                    act.wait_ge(turned, g + 1)
                    nc.scalar.activation(x_nt[:, :, g * P:(g + 1) * P],
                                         turned_ps[:, g % BUFFERS, 0:2 * P].rearrange("p (c n) -> p c n", c=NC),
                                         ACT.Copy).then_inc(kept, 1)
                    for n in projected_after(g):
                        act.wait_ge(prepared, 4)
                        for m in range(NC):
                            act.wait_ge(q_made, 2 * n + m + 1)
                            nc.scalar.activation(q_t[:, m, n * 512:(n + 1) * 512], q_ps[:, m, :], ACT.Identity,
                                                 bias=bq_s[:, m:m + 1], scale=SCALE).then_inc(q_kept, 1)

            @block.tensor
            def _(pe):
                pe.wait_ge(c_in, 32)
                for g in range(NG):
                    pe.wait_ge(normed, g + 1)
                    if g >= BUFFERS:
                        pe.wait_ge(kept, g - BUFFERS + 1)
                    for c in range(NC):
                        mm = nc.tensor.transpose(turned_ps[:, g % BUFFERS, c * P:(c + 1) * P], x_n[:, g % BUFFERS, c * P:(c + 1) * P],
                                                 ident[:, :])
                    mm.then_inc(turned, 1)
                    for n in projected_after(g):
                        pe.wait_ge(wq_in, 16)
                        pe.wait_ge(kept, 4 * n + 4)
                        for m in range(NC):
                            if n:
                                pe.wait_ge(q_kept, 2 * n + m - 1)
                            for c in range(NC):
                                mm = nc.tensor.matmul(q_ps[:, m, :], wq[:, c, m * P:(m + 1) * P], x_nt[:, c, n * 512:(n + 1) * 512],
                                                      start=(c == 0), stop=(c == NC - 1))
                            mm.then_inc(q_made, 1)
                    if g == NG // 2:
                        pe.wait_ge(w_in, len(weights) * 16)
                        for c in range(NC):
                            mm = nc.tensor.matmul(last_ps[:, 0:D], last[:, c, :], wv[:, c, :], start=(c == 0), stop=(c == NC - 1))
                        mm.then_inc(last_made, 1)
                        pe.wait_ge(prepared, 4)
                        for c in range(NC):
                            nc.tensor.matmul(row_ps[:, 0:D], bv_b[:, c, :], wo[:, c, :], start=(c == 0), stop=False)
                        nc.tensor.matmul(row_ps[:, 0:D], ones[:, :], bo[:, :], start=False, stop=True).then_inc(row_made, 1)


def build(nc, a, out):
    with ExitStack() as kernel_ctx:
        keep = lambda name, shape, dt=F32: kernel_ctx.enter_context(nc.sbuf_tensor(name, shape, dt))
        x_sb = keep("x_sb", [P, NG, D])
        ident = keep("ident", [P, P])
        quad_mask = keep("quad_mask", [P, T])
        miss = keep("miss", [P, ROWS])
        flag = keep("flag", [1, 1], I32)
        ctx_sb = keep("ctx_sb", [P, 2, G, NC, LK])
        later, later_in = later_inputs(ctx_sb), kernel_ctx.enter_context(nc.semaphore("later_in"))
        cross_attention(nc, a, x_sb, ident, quad_mask, miss, flag, ctx_sb, later, later_in)
        attention_and_experts(nc, a, x_sb, ident, quad_mask, out, later, later_in)


def later_inputs(ctx_sb):
    flat = ctx_sb[:, :, :, :, :].rearrange("p s b c l -> p (s b c l)")
    views, at = {}, 0
    for name, partitions, columns, chunks in (
            ("w_qkv", P, NC * 3 * D, NC), ("w_proj", P, NC * D, NC), ("w_rt", P, NC * E, NC), ("b_qk", P, 4, 1), ("b_v2", P, NC, 1),
            ("b_proj", 1, D, 1), ("b_exp", E, D, 1), ("b_rt", 1, E, 1), ("causal", P, LQ, 1), ("rank", P, E, 1),
            ("batch_mask", P, G, 1)):
        view = flat[0:partitions, at:at + columns]
        views[name] = view.rearrange("p (c n) -> p c n", c=chunks) if chunks > 1 else view
        at += columns
    assert at <= 2 * G * NC * LK
    return views


def cross_attention(nc, a, x_sb, ident, quad_mask, miss, flag, ctx_sb, later, later_in):
    with ExitStack() as ctx:
        sb = lambda name, shape, dt=F32: ctx.enter_context(nc.sbuf_tensor(name, shape, dt))
        sem = lambda name: ctx.enter_context(nc.semaphore(name))
        wk = sb("wk", [P, NC, D])
        wv = sb("wv", [P, NC, D])
        wo = sb("wo", [P, NC, D])
        bk = sb("bk", [P, NC])
        q_t = sb("q_t", [P, NC, B * LQ])
        vl_dram = nc.dram_tensor("last_values", [B, T, D], F32, kind="Internal").ap()
        row = sb("row", [P, D])
        ctx_in = [sem("ctx_in0"), sem("ctx_in1")]
        queries(nc, a, x_sb, ident, quad_mask, wk, wv, wo, bk, q_t, vl_dram, row, ctx_sb, ctx_in)
        fast_cross_attention(nc, a, x_sb, ident, quad_mask, miss, wk, wv, wo, bk, q_t, vl_dram, ctx_sb, ctx_in, later, later_in)
        raise_flag(nc, ident, miss, flag)
        general_cross_attention(nc, a, x_sb, ident, quad_mask, flag, wk, wv, wo, bk, q_t, vl_dram, row)


def fast_cross_attention(nc, a, x_sb, ident, quad_mask, miss, wk, wv, wo, bk, q_t, vl_dram, ctx_sb, ctx_in, later, later_in):
    with ExitStack() as ctx:
        sb = lambda name, shape, dt=F32: ctx.enter_context(nc.sbuf_tensor(name, shape, dt))
        sem = lambda name: ctx.enter_context(nc.semaphore(name))

        k_t = sb("k_t", [P, 2, NC, W])
        q_bd = sb("q_bd", [P, 2, NC, P])
        v_sb = sb("v_sb", [P, 4, G, 2, D])
        s_sb = sb("s_sb", [P, 4, G, T, W])
        sh_sb = sb("sh_sb", [P, 2, G, T, W])
        a_t = sb("a_t", [P, 2, 2, T * P])
        al_t = sb("al_t", [T, 2, P])
        vl = sb("vl", [T, 2, G, D])
        om = sb("om", [P, 2, NC, T, LQ])
        pair_sum = sb("pair_sum", [P, NC, 2, LQ])
        o_sb = sb("o_sb", [P, 2, NC * P])
        y_sb = sb("y_sb", [P, D])
        o_t = sb("o_t", [P, 2, NC, P])
        junk_v = sb("junk_v", [P, JUNK, LK], BF16)
        junk_x = sb("junk_x", [P, 2, LK], BF16)
        zero, one = sb("zero", [P, 1]), sb("one", [P, 1])
        junk_a = sb("junk_a", [P, JUNK, LK], BF16)
        small = lambda name, n=1, dt=F32: sb(name, [P, n, ROWS], dt)
        top = sb("top", [P, ROWS, 8])
        top_sum, above, per_mean, lin = small("top_sum"), small("above"), small("per_mean"), small("lin")
        tau = small("tau")
        low = small("low")
        total, ratio, inv = small("total"), small("ratio"), small("inv")
        count = small("count")
        step_ = small("step_")
        neg4, inv4 = small("neg4", 2), small("inv4", 2)
        f4, d4 = small("f4"), small("d4")
        neg5 = small("neg5", 2)
        weight_sum = small("weight_sum", 2)
        off = small("off")

        ps = lambda name, shape: ctx.enter_context(nc.psum_tensor(name, shape, F32))
        k_ps = ps("k_ps", [P, 2, 512])
        v_ps = ps("v_ps", [P, 512])
        s_ps = ps("s_ps", [P, 2, 512])
        t_ps = ps("t_ps", [P, 1024])
        o_ps = ps("o_ps", [P, 512])

        vl_in = [sem("vl_in0"), sem("vl_in1")]
        k_made, k_kept = sem("k_made"), sem("k_kept")
        v_made, v_kept = sem("v_made"), sem("v_kept")
        s_made, s_kept, sh_kept = sem("s_made"), sem("s_kept"), sem("sh_kept")
        bd_made = sem("bd_made")
        tau4_made, f4_made, tau5_made = sem("tau4_made"), sem("f4_made"), sem("tau5_made")
        weights_made, a_turned, a_kept = sem("weights_made"), sem("a_turned"), sem("a_kept")
        o_made, o_copied, o_masked = sem("o_made"), sem("o_copied"), sem("o_masked")
        o_paired, o_kept = sem("o_paired"), sem("o_kept")
        y_made, y_copied, y_kept = sem("y_made"), sem("y_copied"), sem("y_kept")
        top_made, dve_first, d4_made = sem("top_made"), sem("dve_first"), sem("d4_made")
        pool_first = sem("pool_first")
        dve_waited = sem("dve_waited")
        dve_newton, dve_guess, dve_exact, checked = (sem(n) for n in ("dve_newton", "dve_guess", "dve_exact", "checked"))

        def steps(e, step):
            peeled = lambda c: step(Tile(0, c), *(0 <= c + d < NG for d in (1, 0, -1, -2, -3)))
            for c in range(-1, 3):
                peeled(c)
            with e.Fori(0, (NG - 4) // 4) as i:
                for c in range(3, 7):
                    step(Tile(i, c), True, True, True, True, True)
            for c in range(NG - 1, NG + 3):
                peeled(c)

        def turned(b, spare):
            if spare:
                main = k_ps[:, :, :].rearrange("p m n -> p (m n)") if b % 2 else t_ps[:, :]
                return main, s_ps[0:T, b % 2, 0:P]
            return t_ps[:, :], o_ps[0:T, D:D + P]

        with nc.Block() as block:
            @block.sync
            def _(sp):
                def load_ctx(g):
                    sp.dma_start(ctx_sb[:, g.c % 2], a["ctx_t"][bass.ds(g.n, 1)].rearrange("o p b c l -> (o p) b c l")
                                 ).then_inc(ctx_in[g.c % 2], 16)

                def load_vl(g):
                    with nc.allow_non_contiguous_dma(reason="one row of 1 KiB for each quad"):
                        sp.dma_start(vl[:, g.c % 2], vl_dram[bass.ds(g.n * G, G)].rearrange("b t n -> t b n")
                                     ).then_inc(vl_in[g.c % 2], 16)

                def reload_ctx(g):
                    sp.wait_ge(v_made, (g.n - 1) * G)
                    load_ctx(g)

                def reload_vl(g):
                    sp.wait_ge(o_made, (g.n - 1) * G)
                    load_vl(g)

                for c in range(2):
                    load_vl(Tile(0, c))
                for c in range(2, 5):
                    reload_ctx(Tile(0, c))
                with sp.Fori(0, (NG - 6) // 2) as i:
                    for c in (5, 6):
                        reload_ctx(Tile(i, c, 2))
                        reload_vl(Tile(i, c - 3, 2))
                reload_ctx(Tile(0, NG - 1))
                reload_vl(Tile(0, NG - 4))
                sp.wait_ge(v_made, NG * G)
                for name, view in later.items():
                    sp.dma_start(view, a[name]).then_inc(later_in, 16)
                for c in range(NG - 3, NG):
                    reload_vl(Tile(0, c))

            @block.gpsimd
            def _(pool):
                def block_diagonal(n, par, first):
                    if not first:
                        pool.wait_ge(s_made, n * 2 - 2)
                    qv = q_t[:, :, bass.ds(n * LQ, LQ)].unsqueeze(2).to_broadcast([P, NC, T, LQ])
                    mv = quad_mask[:, :].unsqueeze(1).unsqueeze(3).to_broadcast([P, NC, T, LQ])
                    nc.gpsimd.tensor_tensor(q_bd[:, par].rearrange("p c (j q) -> p c j q", j=T), qv, mv,
                                            ALU.mult).then_inc(bd_made, 1)

                def gather_output(g, b):
                    n = g.n * G + b
                    pool.wait_ge(o_copied, n + 1)
                    mv = quad_mask[:, :].unsqueeze(1).unsqueeze(3).to_broadcast([P, NC, T, LQ])
                    nc.gpsimd.tensor_tensor(om[:, b % 2], o_sb[:, b % 2].rearrange("p (c j q) -> p c j q", c=NC, j=T), mv,
                                            ALU.mult).then_inc(o_masked, 1)
                    pool.wait_ge(o_masked, n + 1)
                    nc.gpsimd.tensor_tensor(pair_sum[:, :, :, :], om[:, b % 2, :, 0:2, :], om[:, b % 2, :, 2:4, :],
                                            ALU.add).then_inc(o_paired, 1)
                    pool.wait_ge(o_paired, n + 1)
                    if b == 0 and not (g.c < 2 and isinstance(g.n, int)):
                        pool.wait_ge(y_made, g.n - 1)
                    nc.gpsimd.tensor_tensor(o_t[:, g.c % 2, :, b * LQ:(b + 1) * LQ], pair_sum[:, :, 0, :], pair_sum[:, :, 1, :],
                                            ALU.add).then_inc(o_kept, 1)
                    pool.wait_ge(o_kept, n + 1)

                def residual(g):
                    pool.wait_ge(y_copied, g.n + 1)
                    xt = x_sb[:, bass.ds(g.n, 1), :].rearrange("p o d -> p (o d)")
                    nc.gpsimd.tensor_tensor(xt, y_sb[:, :], xt, ALU.add).then_inc(y_kept, 1)

                def refine(g):
                    pool.wait_ge(f4_made, (g.n + 1) * DVE_ROWS[0])
                    pool.wait_ge(dve_exact, (g.n + 1) * len(DVE_ROWS))
                    pool.wait_ge(tau4_made, g.n + 1)
                    nc.gpsimd.tensor_tensor(d4[:, 0, :], f4[:, 0, :], one[:, 0:1].to_broadcast([P, ROWS]), ALU.subtract
                                            ).then_inc(d4_made, 1)
                    pool.wait_ge(d4_made, g.n * 2 + 1)
                    nc.gpsimd.tensor_tensor(d4[:, 0, :], d4[:, 0, :], inv4[:, g.c % 2, :], ALU.mult).then_inc(d4_made, 1)
                    pool.wait_ge(d4_made, g.n * 2 + 2)
                    if g.from_two():
                        pool.wait_ge(weights_made, (g.n - 1) * G)
                    nc.gpsimd.tensor_tensor(neg5[:, g.c % 2, :], neg4[:, g.c % 2, :], d4[:, 0, :], ALU.subtract).then_inc(tau5_made, 1)

                def check_sums(g):
                    at = g.n * 3
                    pool.wait_ge(weights_made, g.n * G + G)
                    nc.gpsimd.tensor_tensor(off[:, 0, :], weight_sum[:, g.c % 2, :], one[:, 0:1].to_broadcast([P, ROWS]), ALU.subtract
                                            ).then_inc(checked, 1)
                    pool.wait_ge(checked, at + 1)
                    nc.gpsimd.tensor_tensor(off[:, 0, :], off[:, 0, :], off[:, 0, :], ALU.mult).then_inc(checked, 1)
                    pool.wait_ge(checked, at + 2)
                    nc.gpsimd.tensor_tensor(miss[:, :], off[:, 0, :], miss[:, :], ALU.add).then_inc(checked, 1)
                    pool.wait_ge(checked, at + 3)

                def step(k, loads, search, refines, outputs, projects):
                    nxt, last, old = k.plus(1), k.plus(-1), k.plus(-2)
                    for b in range(G):
                        if loads:
                            block_diagonal(nxt.n * G + b, b % 2, nxt.c == 0 and b < 2)
                        if outputs:
                            gather_output(old, b)
                        if b == 0 and projects:
                            residual(k.plus(-3))
                        if b == (2 if search else 1) and refines:
                            refine(last)
                        if b == 3 and outputs:
                            check_sums(old)
                nc.gpsimd.memset(miss[:, :], 0.0)
                nc.gpsimd.memset(one[:, :], 1.0).then_inc(pool_first, 1)
                pool.wait_ge(pool_first, 1)
                steps(pool, step)

            @block.tensor
            def _(pe):
                def keys(g, b):
                    n = g.n * G + b
                    if b == 0:
                        pe.wait_ge(ctx_in[g.c % 2], (g.half + 1) * 16)
                    for m in range(NC):
                        if not (g.c == 0 and b == 0):
                            pe.wait_ge(k_kept, n * 2 + (m - 1))
                        for c in range(NC):
                            mm = nc.tensor.matmul(k_ps[:, m, 0:LK], wk[:, c, m * P:(m + 1) * P],
                                                  ctx_sb[:, g.c % 2, b, c, :], start=(c == 0), stop=(c == NC - 1))
                        mm.then_inc(k_made, 1)

                def values(g, b):
                    n = g.n * G + b
                    if not (g.c == 0 and b == 0):
                        pe.wait_ge(v_kept, n)
                    for j in range(2):
                        for c in range(NC):
                            mm = nc.tensor.matmul(v_ps[:, j * D:(j + 1) * D], ctx_sb[:, g.c % 2, b, c, j * P:(j + 1) * P],
                                                  wv[:, c, :], start=(c == 0), stop=(c == NC - 1))
                    mm.then_inc(v_made, 1)

                def scores(g, b, pair):
                    n = g.n * G + b
                    pe.wait_ge(k_kept, n * 2 + 2)
                    pe.wait_ge(bd_made, n + 1)
                    if not (g.c == 0 and b == 0 and pair == 0):
                        pe.wait_ge(sh_kept, n * 2 + pair)
                    for u in range(2):
                        h = slice(64 * u, 64 * u + 64)
                        mm = nc.tensor.matmul(s_ps[:, u, 0:W], q_bd[h, b % 2, pair, :], k_t[h, b % 2, pair, :],
                                              start=True, stop=True)
                    mm.then_inc(s_made, 1)

                def turn(g, b, spare):
                    n = g.n * G + b
                    pe.wait_ge(weights_made, n + 1)
                    if spare:
                        pe.wait_ge(a_kept, n - 1)
                        if b < 2:
                            pe.wait_ge(k_kept, NG * G * 2)
                            pe.wait_ge(sh_kept, NG * G * 2)
                    else:
                        if not (g.c == 0 and b == 0):
                            pe.wait_ge(a_kept, n)
                            pe.wait_ge(o_copied, n)
                        if b == 1 and not g.c == 0:
                            pe.wait_ge(y_copied, g.n)
                    main, last_token = turned(b, spare)
                    for t in range(T):
                        for j in range(2):
                            nc.tensor.transpose(main[:, (j * T + t) * P:(j * T + t + 1) * P],
                                                s_sb[:, g.c % 4, b, t, j * P:(j + 1) * P], ident[:, :])
                    nc.tensor.transpose(last_token, s_sb[:, g.c % 4, b, :, LM], ident[:, :]).then_inc(a_turned, 1)

                def output(g, b, spare):
                    n = g.n * G + b
                    pe.wait_ge(a_kept, n + 1)
                    pe.wait_ge(v_kept, n + 1)
                    if spare:
                        pe.wait_ge(o_copied, n)
                        if b == 1:
                            pe.wait_ge(y_copied, g.n)
                    if b == 0:
                        pe.wait_ge(vl_in[g.c % 2], (g.half + 1) * 16)
                    for c in range(NC):
                        cols = slice(c * P, (c + 1) * P)
                        nc.tensor.matmul(o_ps[:, cols], vl[:, g.c % 2, b, cols], al_t[:, b % 2, :],
                                         start=True, stop=False, skip_group_check=True)
                        for t in (2 * c, 2 * c + 1):
                            for j in range(2):
                                mm = nc.tensor.matmul(
                                    o_ps[64 * (t % 2):64 * (t % 2) + 64, cols], v_sb[:, g.c % 4, b, j, 64 * t:64 * t + 64],
                                    a_t[:, b % 2, j, t * P:(t + 1) * P], start=False, stop=(j == 1), skip_group_check=True)
                    mm.then_inc(o_made, 1)

                def project(g, outputs):
                    pe.wait_ge(o_kept, g.n * G + G)
                    pe.wait_ge(o_copied, g.n * G + G)
                    if outputs:
                        pe.wait_ge(a_kept, g.n * G + G + 1)
                    for c in range(NC):
                        mm = nc.tensor.matmul(o_ps[:, D:2 * D], o_t[:, g.c % 2, c, :], wo[:, c, :],
                                              start=(c == 0), stop=(c == NC - 1))
                    mm.then_inc(y_made, 1)

                def step(k, loads, search, refines, outputs, projects):
                    nxt, old = k.plus(1), k.plus(-2)
                    spare = not search
                    for b in range(G):
                        if loads:
                            keys(nxt, b)
                        if b and loads:
                            scores(nxt, b - 1, 1)
                        if b == 0 and search:
                            scores(k, G - 1, 1)
                        if outputs and (b == 0 or not spare):
                            turn(old, b, spare)
                        if outputs and spare and b < G - 1:
                            turn(old, b + 1, spare)
                        if loads:
                            values(nxt, b)
                        if b == 0 and projects:
                            project(k.plus(-3), outputs)
                        if outputs:
                            output(old, b, spare)
                        if loads:
                            scores(nxt, b, 0)
                steps(pe, step)

            @block.scalar
            def _(act):
                def keep_keys(g, b):
                    n = g.n * G + b
                    for m in range(NC):
                        act.wait_ge(k_made, n * 2 + (m + 1))
                        if not (g.c == 0 and b < 2):
                            act.wait_ge(s_made, n * 2 - 2)
                        nc.scalar.activation(k_t[:, b % 2, m, 0:LK], k_ps[:, m, 0:LK], ACT.Identity, bias=bk[:, m:m + 1],
                                             accum_out=k_t[:, b % 2, m, LK:W]).then_inc(k_kept, 1)

                def keep_values(g, b):
                    n = g.n * G + b
                    act.wait_ge(v_made, n + 1)
                    if b == 0 and not (g.c < 4 and isinstance(g.n, int)):
                        act.wait_ge(o_made, g.n * G - 12)
                    nc.scalar.activation(v_sb[:, g.c % 4, b].rearrange("p j n -> p (j n)"), v_ps[:, :], ACT.Copy
                                         ).then_inc(v_kept, 1)

                def keep_output(g, b):
                    n = g.n * G + b
                    act.wait_ge(o_made, n + 1)
                    if not (g.c == 0 and b < 2):
                        act.wait_ge(o_masked, n - 1)
                    nc.scalar.activation(o_sb[:, b % 2, :], o_ps[:, 0:D], ACT.Copy).then_inc(o_copied, 1)

                def keep_projected(g, outputs):
                    act.wait_ge(y_made, g.n + 1)
                    if outputs:
                        act.wait_ge(o_made, g.n * G + G + 1)
                    if not g.c == 0:
                        act.wait_ge(y_kept, g.n)
                    nc.scalar.activation(y_sb[:, :], o_ps[:, D:2 * D], ACT.Copy).then_inc(y_copied, 1)

                def keep_scores(g, b, pair):
                    n = g.n * G + b
                    act.wait_ge(s_made, n * 2 + (pair + 1))
                    if b == 0 and pair == 0 and g.from_two():
                        act.wait_ge(tau4_made, g.n - 1)
                    nc.scalar.activation(s_sb[:, g.c % 4, b, 2 * pair:2 * pair + 2, :], s_ps[:, :, 0:W], ACT.Copy
                                         ).then_inc(s_kept, 1)
                    nc.scalar.activation(sh_sb[:, g.c % 2, b, 2 * pair:2 * pair + 2, :], s_ps[:, :, 0:W], ACT.Copy,
                                         bias=SHIFT).then_inc(sh_kept, 1)

                len_act = DVE_ROWS[0]
                half = len_act // 2

                def exact_excess(g, rows):
                    for r in rows:
                        if r == 0:
                            act.wait_ge(tau4_made, g.n + 1)
                        if r >= JUNK:
                            act.wait_ge(f4_made, g.n * len_act + (r - JUNK + 1))
                        nc.scalar.activation(junk_a[:, r % JUNK, :], s_sb[:, g.c % 4, r // T, r % T, 0:LK], ACT.Relu,
                                             bias=neg4[:, g.c % 2, r:r + 1], accum_out=f4[:, 0, r:r + 1]).then_inc(f4_made, 1)

                def weights(g, b):
                    if b == 0:
                        act.wait_ge(tau5_made, g.n + 1)
                    for t in range(T):
                        row, r = s_sb[:, g.c % 4, b, t, 0:LK], b * T + t
                        ins = nc.scalar.activation(row, row, ACT.Relu, bias=neg5[:, g.c % 2, r:r + 1],
                                                   accum_out=weight_sum[:, g.c % 2, r:r + 1])
                    ins.then_inc(weights_made, 1)

                def keep_turned(g, b, spare):
                    n = g.n * G + b
                    act.wait_ge(a_turned, n + 1)
                    if not (g.c == 0 and b < 2):
                        act.wait_ge(o_made, n - 1)
                    main, last_token = turned(b, spare)
                    nc.scalar.activation(al_t[:, b % 2, :], last_token, ACT.Copy)
                    nc.scalar.activation(a_t[:, b % 2].rearrange("p j n -> p (j n)"), main, ACT.Copy
                                         ).then_inc(a_kept, 1)

                def step(k, loads, search, refines, outputs, projects):
                    nxt, last, old = k.plus(1), k.plus(-1), k.plus(-2)
                    spare = not search
                    ahead = 2 if spare else 1
                    for b in range(G):
                        if loads:
                            keep_keys(nxt, b)
                        if outputs:
                            keep_turned(old, b, spare)
                        if b and loads:
                            keep_scores(nxt, b - 1, 1)
                        if b == 0 and search:
                            keep_scores(k, G - 1, 1)
                        if refines and spare and b < 2:
                            exact_excess(last, range(b * half, (b + 1) * half))
                        if outputs and b + ahead < G:
                            weights(old, b + ahead)
                        if outputs:
                            keep_output(old, b)
                        if b == 0 and projects:
                            keep_projected(k.plus(-3), outputs)
                        if loads:
                            keep_values(nxt, b)
                            keep_scores(nxt, b, 0)
                        if refines and not spare and b < 3:
                            exact_excess(last, ACT_ROWS[b])
                        if refines and b + ahead >= G:
                            weights(last, b + ahead - G)
                    if refines and search and not loads:
                        weights(last, 1)
                steps(act, step)

            @block.vector
            def _(dve):
                class Chain:

                    def __init__(self, semaphore, per):
                        self.sem, self.per = semaphore, per

                    def start(self, g):
                        self.g, self.n = g, 0

                    def __call__(self, ins, meanwhile=None):
                        self.n += 1
                        ins.then_inc(self.sem, 1)
                        if meanwhile:
                            meanwhile()
                        dve.wait_ge(self.sem, self.g.n * self.per + self.n)

                    def post(self, ins):
                        self.n += 1
                        ins.then_inc(self.sem, 1)

                    def settle(self, open_=0):
                        dve.wait_ge(self.sem, self.g.n * self.per + (self.n - open_))

                    def end(self):
                        assert self.n == self.per, self.n

                newton, guess, exact = Chain(dve_newton, 3 * ROWS + 30), Chain(dve_guess, 9), Chain(dve_exact, len(DVE_ROWS))
                v = nc.vector

                def largest(g, rows):
                    for r in rows:
                        if r % T == 0:
                            dve.wait_ge(s_kept, (g.n * G + r // T) * 2 + 2)
                            dve.sem_inc(dve_waited, 1)
                        ins = v.max(top[:, r, :], s_sb[:, g.c % 4, r // T, r % T, 0:LK])
                        if r == ROWS - 1:
                            ins.then_inc(top_made, 1)

                def first_guess(g):
                    guess.start(g)
                    eighth, largest_ = top[:, :, 7], top[:, :, 0]
                    guess.post(v.tensor_reduce(top_sum[:, 0, :], top[:, :, :], AX.X, ALU.add))
                    guess.post(v.scalar_tensor_tensor(per_mean[:, 0, :].rearrange("p (b t) -> p b t", t=T), s_sb[:, g.c % 4, :, :, LK], -1.0 / LK,
                                                      eighth.rearrange("p (b t) -> p b t", t=T), ALU.mult, ALU.add))
                    guess.settle(1)
                    guess.post(v.scalar_tensor_tensor(above[:, 0, :], eighth, -8.0, top_sum[:, 0, :], ALU.mult, ALU.add))
                    guess.settle(1)
                    guess.post(v.tensor_scalar(lin[:, 0, :], per_mean[:, 0, :], GUESS[3], GUESS[1], ALU.mult, ALU.add))
                    guess.post(v.tensor_scalar(low[:, 0, :], top_sum[:, 0, :], 8 * SHIFT - 1, 0.125, ALU.add, ALU.mult))
                    guess.settle(1)
                    guess.post(v.tensor_tensor(above[:, 0, :], lin[:, 0, :], above[:, 0, :], ALU.mult))
                    guess.settle(1)
                    guess.post(v.scalar_tensor_tensor(low[:, 0, :], largest_, SHIFT - 1, low[:, 0, :], ALU.add, ALU.max))
                    guess.settle(1)
                    guess.post(v.scalar_tensor_tensor(lin[:, 0, :], per_mean[:, 0, :], GUESS[2], above[:, 0, :], ALU.mult, ALU.add))
                    guess.settle()
                    guess(v.scalar_tensor_tensor(tau[:, 0, :], lin[:, 0, :], GUESS[0] + SHIFT, eighth, ALU.add, ALU.add))
                    guess.end()

                def sums_above(g, t):
                    for r in range(ROWS):
                        row = sh_sb[:, g.c % 2, r // T, r % T, 0:LK]
                        if r >= JUNK:
                            newton.settle(JUNK - 1)
                        newton.post(v.scalar_tensor_tensor(junk_v[:, r % JUNK, :], row, t[:, 0, r:r + 1], row, ALU.is_gt,
                                                           ALU.mult, accum_out=total[:, 0, r:r + 1]))
                    newton.settle()

                def newton_round(t, fast, inverse, meanwhile):
                    other = lambda j: lambda: meanwhile(j)
                    newton(v.reciprocal(inv[:, 0, :], t[:, 0, :]), other(0))
                    newton(v.tensor_tensor(ratio[:, 0, :], total[:, 0, :], inv[:, 0, :], ALU.mult), other(1))
                    newton(v.tensor_scalar(count[:, 0, :], ratio[:, 0, :], -0.45, ROUND, ALU.add, ALU.add), other(2))
                    newton(v.tensor_scalar(count[:, 0, :], count[:, 0, :], -ROUND, 1.0, ALU.add, ALU.max), other(3))
                    newton(v.reciprocal(inverse, count[:, 0, :]), other(4))
                    newton(v.scalar_tensor_tensor(ratio[:, 0, :], total[:, 0, :], -1.0, inverse, ALU.add, ALU.mult), other(5))
                    if fast:
                        newton.post(v.tensor_tensor(step_[:, 0, :], ratio[:, 0, :], tau[:, 0, :], ALU.subtract))
                        newton.post(v.tensor_tensor(low[:, 0, :], low[:, 0, :], ratio[:, 0, :], ALU.max))
                        meanwhile(6)
                        newton.settle(1)
                        newton(v.scalar_tensor_tensor(inv[:, 0, :], step_[:, 0, :], 0.25, count[:, 0, :], ALU.mult, ALU.mult), other(7))
                        newton(v.tensor_tensor(inv[:, 0, :], inv[:, 0, :], step_[:, 0, :], ALU.mult), other(8))
                        newton(v.tensor_tensor(tau[:, 0, :], inv[:, 0, :], ratio[:, 0, :], ALU.add), other(9))
                    else:
                        newton(v.tensor_tensor(low[:, 0, :], low[:, 0, :], ratio[:, 0, :], ALU.max), other(6))

                def exact_excess(g, rows):
                    for r in rows:
                        if r == DVE_ROWS[0]:
                            exact.start(g)
                            dve.wait_ge(tau4_made, g.n + 1)
                            if not g.c == 0:
                                dve.wait_ge(tau5_made, g.n)
                        if r >= DVE_ROWS[0] + 2:
                            exact.settle(1)
                        exact.post(v.scalar_tensor_tensor(junk_x[:, r % 2, :], s_sb[:, g.c % 4, r // T, r % T, 0:LK],
                                                          neg4[:, g.c % 2, r:r + 1], zero[:, 0:1].to_broadcast([P, LK]), ALU.add,
                                                          ALU.max, accum_out=f4[:, 0, r:r + 1]))

                def step(k, loads, search, refines, outputs, projects):
                    nxt, last, old = k.plus(1), k.plus(-1), k.plus(-2)
                    if search:
                        largest(k, range(3 * T, ROWS))
                        dve.wait_ge(top_made, k.n + 1)
                        first_guess(k)
                        newton.start(k)
                        dve.wait_ge(sh_kept, (k.n + 1) * (2 * G))
                        newton(v.tensor_tensor(tau[:, 0, :], tau[:, 0, :], low[:, 0, :], ALU.max))
                        sums_above(k, tau)
                        newton_round(tau, True, inv[:, 0, :], lambda j: exact_excess(last, DVE_ROWS[j:j + 1]) if refines else None)
                        sums_above(k, tau)
                        newton_round(tau, True, inv[:, 0, :], lambda j: largest(nxt, (j,)) if loads and j < T else None)
                        sums_above(k, low)
                    else:
                        if refines:
                            exact_excess(last, DVE_ROWS)
                        if loads:
                            largest(nxt, range(T))
                    if search:
                        newton_round(low, False, inv4[:, k.c % 2, :], lambda j: largest(nxt, (T + j,)) if loads and j < BESIDE_LAST else None)
                        v.tensor_scalar(neg4[:, k.c % 2, :], low[:, 0, :], -1.0, SHIFT, ALU.mult, ALU.add).then_inc(tau4_made, 1)
                        newton.end()
                    elif loads:
                        largest(nxt, range(T, T + BESIDE_LAST))
                    if loads:
                        largest(nxt, range(T + BESIDE_LAST, 3 * T))
                v.memset(zero[:, :], 0.0).then_inc(dve_first, 1)
                dve.wait_ge(dve_first, 1)
                steps(dve, step)


def raise_flag(nc, ident, miss, flag):
    with ExitStack() as ctx:
        sb = lambda name, shape, dt=F32: ctx.enter_context(nc.sbuf_tensor(name, shape, dt))
        sem = lambda name: ctx.enter_context(nc.semaphore(name))
        ok, ok_made = sb("ok", [P, ROWS]), sem("ok_made")
        least, least_all = sb("least", [P, 1]), sb("least_all", [1, 1])
        turned = ctx.enter_context(nc.psum_tensor("flag_ps", [P, 512], F32))
        least_made, flag_turned, flag_made = sem("least_made"), sem("flag_turned"), sem("flag_made")
        with nc.Block() as block:
            @block.vector
            def _(dve):
                nc.vector.tensor_scalar(ok[:, :], miss[:, :], TOL * TOL, None, ALU.is_le).then_inc(ok_made, 1)
                dve.wait_ge(ok_made, 1)
                nc.vector.tensor_reduce(least[:, :], ok[:, :], AX.X, ALU.min).then_inc(least_made, 1)
                dve.wait_ge(flag_turned, 1)
                nc.vector.tensor_reduce(least_all[:, :], turned[0:1, 0:P], AX.X, ALU.min).then_inc(flag_made, 1)
                dve.wait_ge(flag_made, 1)
                nc.vector.tensor_copy(flag[:, :], least_all[:, :]).then_inc(flag_made, 1)
                dve.wait_ge(flag_made, 2)

            @block.tensor
            def _(pe):
                pe.wait_ge(least_made, 1)
                nc.tensor.transpose(turned[0:1, 0:P], least[:, :], ident[:, :]).then_inc(flag_turned, 1)
                pe.wait_ge(flag_turned, 1)


def general_cross_attention(nc, a, x_sb, ident, quad_mask, flag, wk, wv, wo, bk, q_t, vl_dram, row):
    with ExitStack() as ctx:
        sb = lambda name, shape, dt=F32: ctx.enter_context(nc.sbuf_tensor(name, shape, dt))
        sem = lambda name: ctx.enter_context(nc.semaphore(name))
        ps = lambda name, shape: ctx.enter_context(nc.psum_tensor(name, shape, F32))
        ctx_sb = sb("g_ctx", [P, G, NC, LK])
        vl = sb("g_vl", [T, G, D])
        k_t = sb("g_k", [P, NC, LK])
        q_bd = sb("g_bd", [P, NC, P])
        v_sb = sb("g_v", [P, 2, D])
        s_sb = sb("g_s", [P, T, LK])
        zeros = sb("g_zeros", [P, LK])
        junk = sb("g_junk", [P, 2, T, LK])
        low, excess, count, inv, neg = (sb(f"g_{n}", [P, T]) for n in ("low", "excess", "count", "inv", "neg"))
        a_t = sb("g_at", [P, 2, T * P])
        al_t = sb("g_alt", [T, P])
        om = sb("g_om", [P, NC, T, LQ])
        o_t = sb("g_ot", [P, NC, P])
        kv_ps = ps("g_kvps", [P, 2, 512])
        s_ps = ps("g_sps", [P, T, 512])
        t_ps = s_ps[:, 0:2, :]
        o_ps = ps("g_ops", [P, 512])
        y_ps = ps("g_yps", [P, 512])
        zeroed, row_in, row_added, loaded, vl_loaded = (sem(f"g_{n}") for n in (
            "zeroed", "row_in", "row_added", "loaded", "vl_loaded"))
        k_made, k_kept, bd_made, s_made, s_kept = (sem(f"g_{n}") for n in ("k_made", "k_kept", "bd_made", "s_made", "s_kept"))
        dve_waited = sem("g_waited")
        v_made, v_kept, newton, stepped, w_made, turned, a_kept = (sem(f"g_{n}") for n in (
            "v_made", "v_kept", "newton", "stepped", "w_made", "turned", "a_kept"))
        o_made, o_masked, o_kept, y_made, y_kept = (sem(f"g_{n}") for n in ("o_made", "o_masked", "o_kept", "y_made", "y_kept"))
        START, EACH = 3, 4

        with nc.Block() as block:
            def needed(e):
                return e.If(e.value_load(flag[0:1, 0:1], min_val=0, max_val=1) < 1)

            @block.sync
            def _(sp):
                with needed(sp):
                    sp.dma_start(x_sb[:, :, :], a["x"]).then_inc(row_in, 16)
                    with sp.Fori(0, NG) as g:
                        sp.wait_ge(v_made, g * G)
                        sp.dma_start(ctx_sb[:, :, :, :], a["ctx_t"][bass.ds(g, 1)].rearrange("o p b c l -> (o p) b c l")
                                     ).then_inc(loaded, 16)
                        sp.wait_ge(o_made, g * G)
                        with nc.allow_non_contiguous_dma(reason="one row of 1 KiB for each quad"):
                            sp.dma_start(vl[:, :, :], vl_dram[bass.ds(g * G, G)].rearrange("b t n -> t b n")
                                         ).then_inc(vl_loaded, 16)
                sp.nop()

            @block.gpsimd
            def _(pool):
                with needed(pool):
                    with pool.Fori(0, B) as n:
                        pool.wait_ge(s_made, n)
                        qv = q_t[:, :, bass.ds(n * LQ, LQ)].unsqueeze(2).to_broadcast([P, NC, T, LQ])
                        mv = quad_mask[:, :].unsqueeze(1).unsqueeze(3).to_broadcast([P, NC, T, LQ])
                        nc.gpsimd.tensor_tensor(q_bd[:, :, :].rearrange("p c (j q) -> p c j q", j=T), qv, mv, ALU.mult
                                                ).then_inc(bd_made, 1)
                pool.nop()

            @block.tensor
            def _(pe):
                with needed(pe):
                    with pe.Fori(0, NG) as g:
                        pe.wait_ge(loaded, g * 16 + 16)
                        pe.wait_ge(vl_loaded, g * 16 + 16)
                        for b in range(G):
                            n = g * G + b
                            pe.wait_ge(v_kept, n)
                            for m in range(NC):
                                for c in range(NC):
                                    mm = nc.tensor.matmul(kv_ps[:, m, 0:LK], wk[:, c, m * P:(m + 1) * P], ctx_sb[:, b, c, :],
                                                          start=(c == 0), stop=(c == NC - 1))
                            mm.then_inc(k_made, 1)
                            pe.wait_ge(k_kept, n + 1)
                            pe.wait_ge(bd_made, n + 1)
                            pe.wait_ge(a_kept, n)
                            for t in range(T):
                                h = slice(64 * (t % 2), 64 * (t % 2) + 64)
                                mm = nc.tensor.matmul(s_ps[:, t, 0:LK], q_bd[h, t // 2, :], k_t[h, t // 2, :],
                                                      start=True, stop=True)
                            mm.then_inc(s_made, 1)
                            for j in range(2):
                                for c in range(NC):
                                    mm = nc.tensor.matmul(kv_ps[:, j, 0:D], ctx_sb[:, b, c, j * P:(j + 1) * P], wv[:, c, :],
                                                          start=(c == 0), stop=(c == NC - 1))
                            mm.then_inc(v_made, 1)
                            pe.wait_ge(w_made, n + 1)
                            pe.wait_ge(s_kept, n + 1)
                            pe.wait_ge(o_kept, n)
                            for t in range(T):
                                for j in range(2):
                                    nc.tensor.transpose(t_ps[:, j, t * P:(t + 1) * P], s_sb[:, t, j * P:(j + 1) * P], ident[:, :])
                            nc.tensor.transpose(o_ps[0:T, D:D + P], s_sb[:, :, LM], ident[:, :]).then_inc(turned, 1)
                            pe.wait_ge(a_kept, n + 1)
                            pe.wait_ge(v_kept, n + 1)
                            for c in range(NC):
                                cols = slice(c * P, (c + 1) * P)
                                nc.tensor.matmul(o_ps[:, cols], vl[:, b, cols], al_t[:, :], start=True, stop=False,
                                                 skip_group_check=True)
                                for t in (2 * c, 2 * c + 1):
                                    for j in range(2):
                                        mm = nc.tensor.matmul(
                                            o_ps[64 * (t % 2):64 * (t % 2) + 64, cols], v_sb[:, j, 64 * t:64 * t + 64],
                                            a_t[:, j, t * P:(t + 1) * P], start=False, stop=(j == 1), skip_group_check=True)
                            mm.then_inc(o_made, 1)
                        pe.wait_ge(o_kept, g * G + G)
                        pe.wait_ge(y_kept, g)
                        for c in range(NC):
                            mm = nc.tensor.matmul(y_ps[:, 0:D], o_t[:, c, :], wo[:, c, :], start=(c == 0), stop=(c == NC - 1))
                        mm.then_inc(y_made, 1)
                pe.nop()

            @block.scalar
            def _(act):
                with needed(act):
                    with act.Fori(0, B) as n:
                        act.wait_ge(k_made, n + 1)
                        for m in range(NC):
                            ins = nc.scalar.activation(k_t[:, m, :], kv_ps[:, m, 0:LK], ACT.Identity, bias=bk[:, m:m + 1])
                        ins.then_inc(k_kept, 1)
                        act.wait_ge(s_made, n + 1)
                        nc.scalar.activation(s_sb[:, :, :], s_ps[:, :, 0:LK], ACT.Copy).then_inc(s_kept, 1)
                        act.wait_ge(v_made, n + 1)
                        nc.scalar.activation(v_sb[:, :, :], kv_ps[:, :, 0:D], ACT.Copy).then_inc(v_kept, 1)
                        act.wait_ge(turned, n + 1)
                        nc.scalar.activation(al_t[:, :], o_ps[0:T, D:D + P], ACT.Copy)
                        nc.scalar.activation(a_t[:, :, :], t_ps, ACT.Copy).then_inc(a_kept, 1)
                act.nop()

            @block.vector
            def _(dve):
                v = nc.vector
                with needed(dve):
                    v.memset(zeros[:, :], 0.0).then_inc(zeroed, 1)
                    dve.wait_ge(zeroed, 1)
                    dve.wait_ge(row_in, 16)
                    v.tensor_tensor(x_sb[:, :, :], x_sb[:, :, :], row[:, :].unsqueeze(1).to_broadcast([P, NG, D]), ALU.add
                                    ).then_inc(row_added, 1)
                    dve.wait_ge(row_added, 1)
                    with dve.Fori(0, NG) as g:
                        for b in range(G):
                            n = g * G + b
                            done = n * (START + EACH * SLOW_STEPS)
                            dve.wait_ge(s_kept, n + 1)
                            v.tensor_reduce(low[:, :], s_sb[:, :, :], AX.X, ALU.max).then_inc(newton, 1)
                            dve.wait_ge(newton, done + 1)
                            v.tensor_scalar(low[:, :], low[:, :], -1.0, None, ALU.add).then_inc(newton, 1)
                            dve.wait_ge(newton, done + 2)
                            dve.sem_inc(dve_waited, 1)
                            with dve.Fori(0, SLOW_STEPS) as k:
                                at = done + k * EACH + 2
                                for t in range(T):
                                    v.scalar_tensor_tensor(junk[:, 0, t, :], s_sb[:, t, :], low[:, t:t + 1], zeros[:, :],
                                                           ALU.subtract, ALU.max, accum_out=excess[:, t:t + 1])
                                    ins = v.tensor_scalar(junk[:, 1, t, :], s_sb[:, t, :], low[:, t:t + 1], None, ALU.is_gt,
                                                          ALU.add, accum_out=count[:, t:t + 1])
                                ins.then_inc(newton, 1)
                                dve.wait_ge(newton, at + 1)
                                v.tensor_scalar(count[:, :], count[:, :], 1.0, None, ALU.max).then_inc(newton, 1)
                                dve.wait_ge(newton, at + 2)
                                v.reciprocal(inv[:, :], count[:, :]).then_inc(newton, 1)
                                dve.wait_ge(newton, at + 3)
                                v.scalar_tensor_tensor(inv[:, :], excess[:, :], -1.0, inv[:, :], ALU.add, ALU.mult
                                                       ).then_inc(newton, 1)
                                dve.wait_ge(newton, at + 4)
                                v.scalar_tensor_tensor(low[:, :], inv[:, :], 0.0, low[:, :], ALU.max, ALU.add
                                                       ).then_inc(stepped, 1)
                                dve.wait_ge(stepped, n * SLOW_STEPS + k + 1)
                            v.tensor_scalar(neg[:, :], low[:, :], -1.0, None, ALU.mult).then_inc(newton, 1)
                            dve.wait_ge(newton, done + START + EACH * SLOW_STEPS)
                            for t in range(T):
                                ins = v.tensor_scalar(s_sb[:, t, :], s_sb[:, t, :], neg[:, t:t + 1], 0.0, ALU.add, ALU.max)
                            ins.then_inc(w_made, 1)
                            dve.wait_ge(o_made, n + 1)
                            ov = o_ps[:, 0:D].rearrange("p (c j q) -> p c j q", c=NC, j=T)
                            mv = quad_mask[:, :].unsqueeze(1).unsqueeze(3).to_broadcast([P, NC, T, LQ])
                            v.tensor_tensor(om[:, :, :, :], ov, mv, ALU.mult).then_inc(o_masked, 1)
                            dve.wait_ge(o_masked, n + 1)
                            v.tensor_reduce(o_t[:, :, b * LQ:(b + 1) * LQ], om[:, :, :, :].rearrange("p c j q -> p c q j"),
                                            AX.X, ALU.add).then_inc(o_kept, 1)
                            dve.wait_ge(o_kept, n + 1)
                        dve.wait_ge(y_made, g + 1)
                        xt = x_sb[:, bass.ds(g, 1), :].rearrange("p o d -> p (o d)")
                        v.tensor_tensor(xt, y_ps[:, 0:D], xt, ALU.add).then_inc(y_kept, 1)
                        dve.wait_ge(y_kept, g + 1)
                dve.nop()


def attention_and_experts(nc, a, x_sb, ident, quad_mask, out, later, later_in):
    with ExitStack() as ctx:
        sb = lambda name, shape, dt=F32: ctx.enter_context(nc.sbuf_tensor(name, shape, dt))
        sem = lambda name: ctx.enter_context(nc.semaphore(name))
        ps = lambda name, shape: ctx.enter_context(nc.psum_tensor(name, shape, F32))
        w_qkv, w_proj, w_rt, b_qk, b_v, b_proj, b_exp, b_rt, causal, rank, batch_mask = (later[n] for n in (
            "w_qkv", "w_proj", "w_rt", "b_qk", "b_v2", "b_proj", "b_exp", "b_rt", "causal", "rank", "batch_mask"))
        b_qs = sb("b_qs", [P, NC])
        b_vb = sb("b_vb", [P, NC, P])
        w_exp = sb("w_exp", [P, NC, E * D])
        ones = sb("s_ones", [1, P])
        power = sb("power", [P, 1])
        row = sb("s_row", [P, D])

        st1, mv1, var1, root1, half1 = sb("st1", [P, 6]), sb("mv1", [P, 2]), sb("var1", [P, 1]), sb("root1", [P, 1]), sb("half1", [P, 1])
        xn1, xt1 = sb("xn1", [P, 2, D]), sb("xt1", [P, 2, NC, P])
        q_t, k_t = sb("s_q", [P, 2, NC, P]), sb("s_k", [P, 2, NC, P])
        v_sb = sb("s_v", [P, 2, G, D])
        q_bd = sb("s_bd", [P, 2, NC, G, T * LQ])
        s_sb = sb("s_s", [P, 2, T * G, LQ])
        top, den, inv = sb("s_top", [P, T * G]), sb("s_den", [P, T * G]), sb("s_inv", [P, T * G])
        p_t = sb("s_pt", [P, 2, T, P])
        o_sb = sb("s_o", [P, NC, G, T * LQ])
        om = sb("s_om", [P, NC * G, T, LQ])
        o_pair = sb("s_opair", [P, NC * G, 2, LQ])
        o_t = sb("s_ot", [P, 2, NC, P])
        xr = sb("xr", [P, 2, D])
        x2 = sb("x2", [P, 2, D])
        st2, mv2, var2, root2, half2 = sb("st2", [P, 6]), sb("mv2", [P, 2]), sb("var2", [P, 1]), sb("root2", [P, 1]), sb("half2", [P, 1])
        xn2, xt2 = sb("xn2", [P, 2, D]), sb("xt2", [P, 2, NC, P])
        r_top, r_exp, r_den, r_w = sb("r_top", [P, 1]), sb("r_exp", [P, E]), sb("r_den", [P, 1]), sb("r_w", [P, 1])
        r_max, r_sel, r_best, gate = sb("r_max", [P, 1]), sb("r_sel", [P, E]), sb("r_best", [P, 1]), sb("gate", [P, 2, E])
        gate_t = sb("gate_t", [E, P])
        acc = sb("acc", [P, 2, D])

        a_ps = ps("a_ps", [P, 512])
        qk_ps = ps("qk_ps", [P, 512])
        s_ps = ps("ss_ps", [P, 2, 512])
        c_ps = ps("c_ps", [P, 512])
        o_ps = ps("so_ps", [P, 512])
        e_ps = ps("e_ps", [P, 2, 512])

        e_in, consts, biases, row_made = sem("s_ein"), sem("s_consts"), sem("s_biases"), sem("s_rowmade")
        dve_first, var1_made, root1_made = sem("s_first"), sem("var1_made"), sem("root1_made")
        dve_waited = sem("s_waited")
        normed1, turned1, kept1 = sem("normed1"), sem("turned1"), sem("kept1")
        qk_made, qk_kept, v_made, v_kept, bd_made = (sem(f"s_{n}") for n in ("qk_made", "qk_kept", "v_made", "v_kept", "bd_made"))
        s_made, masked, softmax, exp_made, probs_made = (sem(f"s_{n}") for n in ("s_made", "masked", "softmax", "exp_made", "probs_made"))
        p_turned, p_kept, o_made, o_copied = (sem(f"s_{n}") for n in ("p_turned", "p_kept", "o_made", "o_copied"))
        o_masked, o_paired, o_kept = (sem(f"s_{n}") for n in ("o_masked", "o_paired", "o_kept"))
        xr_made, y_made, x2_made = sem("xr_made"), sem("s_y_made"), sem("x2_made")
        dve_second, dve_route, dve_total, var2_made, root2_made, normed2, turned2, kept2 = (sem(n) for n in (
            "dve_second", "dve_route", "dve_total", "var2_made", "root2_made", "normed2", "turned2", "kept2"))
        l_made, r_top_made, r_exp_made, gate_made, gate_turned, gate_kept, eb_made, eb_taken = (sem(n) for n in (
            "l_made", "r_top_made", "r_exp_made", "gate_made", "gate_turned", "gate_kept", "eb_made", "eb_taken"))
        e_made, e_taken, stored = sem("e_made"), sem("e_taken"), [sem("stored0"), sem("stored1")]

        def steps(e, step):
            peeled = lambda c: step(Tile(0, c, 2), *(0 <= c + d < NG for d in (2, 1, 0, -1, -2)))
            for c in range(-2, 4):
                peeled(c)
            with e.Fori(0, (NG - 6) // 2) as i:
                for c in (4, 5):
                    step(Tile(i, c, 2), True, True, True, True, True)
            for c in range(NG - 2, NG + 2):
                peeled(c)

        def head_mask(n):
            return quad_mask[:, :].unsqueeze(1).unsqueeze(3).to_broadcast([P, n, T, LQ])

        with nc.Block() as block:
            @block.sync
            def _(sp):
                sp.dma_start(w_exp[:, :, :], a["w_exp"]).then_inc(e_in, 16)

                def store(g, par):
                    sp.wait_ge(e_taken, g * 4 + 4)
                    sp.dma_start(out[:, bass.ds(g, 1), :].rearrange("p o d -> p (o d)"), acc[:, par, :]).then_inc(stored[par], 16)
                with sp.Fori(0, NG // 2) as i:
                    store(i * 2, 0)
                    store(i * 2 + 1, 1)
                sp.wait_ge(stored[0], NG // 2 * 16)
                sp.wait_ge(stored[1], NG // 2 * 16)

            @block.gpsimd
            def _(pool):
                nc.gpsimd.memset(ones[:, :], 1.0).then_inc(consts, 1)
                nc.gpsimd.memset(power[:, :], -0.5).then_inc(consts, 1)
                pool.wait_ge(consts, 2)

                def root_of_first(g):
                    pool.wait_ge(var1_made, g.n + 1)
                    nc.gpsimd.tensor_tensor(root1[:, :], var1[:, :], power[:, 0:1], ALU.pow).then_inc(root1_made, 1)

                def root_of(g):
                    pool.wait_ge(var2_made, g.n + 1)
                    nc.gpsimd.tensor_tensor(root2[:, :], var2[:, :], power[:, 0:1], ALU.pow).then_inc(root2_made, 1)

                def block_diagonal(g):
                    pool.wait_ge(qk_kept, g.n + 1)
                    if g.from_two():
                        pool.wait_ge(s_made, g.n - 1)
                    for c in range(NC):
                        qv = q_t[:, g.c % 2, c, :].rearrange("p (b q) -> p b q", b=G).unsqueeze(2).to_broadcast([P, G, T, LQ])
                        ins = nc.gpsimd.tensor_tensor(q_bd[:, g.c % 2, c].rearrange("p b (j q) -> p b j q", j=T), qv,
                                                      head_mask(G), ALU.mult)
                    ins.then_inc(bd_made, 1)

                def residual_input(g):
                    if g.from_two():
                        pool.wait_ge(x2_made, g.n - 1)
                    else:
                        pool.wait_ge(row_made, 2)
                    xt = x_sb[:, bass.ds(g.n, 1), :].rearrange("p o d -> p (o d)")
                    nc.gpsimd.tensor_tensor(xr[:, g.c % 2, :], xt, row[:, :], ALU.add).then_inc(xr_made, 1)

                def gather_output(g, c):
                    n = g.n * 2 + c
                    half = slice(c * G, (c + 1) * G)
                    pool.wait_ge(o_copied, n + 1)
                    nc.gpsimd.tensor_tensor(om[:, half, :, :], o_sb[:, c].rearrange("p b (j q) -> p b j q", j=T),
                                            head_mask(G), ALU.mult).then_inc(o_masked, 1)
                    pool.wait_ge(o_masked, n + 1)
                    nc.gpsimd.tensor_tensor(o_pair[:, half, :, :], om[:, half, 0:2, :], om[:, half, 2:4, :], ALU.add
                                            ).then_inc(o_paired, 1)
                    pool.wait_ge(o_paired, n + 1)
                    if c == 0 and g.from_two():
                        pool.wait_ge(y_made, g.n - 1)
                    nc.gpsimd.tensor_tensor(o_t[:, g.c % 2, c].rearrange("p (b q) -> p b q", b=G), o_pair[:, half, 0, :],
                                            o_pair[:, half, 1, :], ALU.add).then_inc(o_kept, 1)
                    pool.wait_ge(o_kept, n + 1)

                def step(k, prepares, projects, attends, leads, ends):
                    if attends:
                        residual_input(k)
                    if prepares:
                        root_of_first(k.plus(2))
                    if leads:
                        root_of(k.plus(-1))
                    if projects:
                        block_diagonal(k.plus(1))
                    if attends:
                        gather_output(k, 0)
                        gather_output(k, 1)
                steps(pool, step)

            @block.tensor
            def _(pe):
                pe.wait_ge(later_in, len(later) * 16)
                pe.wait_ge(consts, 2)
                pe.wait_ge(biases, 1)
                for c in range(NC):
                    nc.tensor.matmul(c_ps[:, 0:D], b_vb[:, c, :], w_proj[:, c, :], start=(c == 0), stop=False)
                nc.tensor.matmul(c_ps[:, 0:D], ones[:, :], b_proj[:, :], start=False, stop=True).then_inc(row_made, 1)

                def turn_first(g):
                    pe.wait_ge(normed1, g.n + 1)
                    if g.c:
                        pe.wait_ge(v_kept, g.n)
                    for c in range(NC):
                        mm = nc.tensor.transpose(a_ps[:, c * P:(c + 1) * P], xn1[:, g.c % 2, c * P:(c + 1) * P], ident[:, :])
                    mm.then_inc(turned1, 1)

                def project_in(g):
                    pe.wait_ge(kept1, g.n + 1)
                    if g.c:
                        pe.wait_ge(qk_kept, g.n)
                    for m in range(4):
                        for c in range(NC):
                            mm = nc.tensor.matmul(qk_ps[:, m * P:(m + 1) * P], w_qkv[:, c, m * P:(m + 1) * P], xt1[:, g.c % 2, c, :],
                                                  start=(c == 0), stop=(c == NC - 1))
                    mm.then_inc(qk_made, 1)
                    for c in range(NC):
                        mm = nc.tensor.matmul(a_ps[:, D:2 * D], xt1[:, g.c % 2, c, :], w_qkv[:, c, 2 * D:3 * D],
                                              start=(c == 0), stop=(c == NC - 1))
                    mm.then_inc(v_made, 1)

                def scores(g):
                    pe.wait_ge(bd_made, g.n + 1)
                    pe.wait_ge(qk_kept, g.n + 1)
                    if g.c:
                        pe.wait_ge(p_kept, g.n)
                    for t in range(T):
                        h = slice(64 * (t % 2), 64 * (t % 2) + 64)
                        for b in range(G):
                            at = (t // 2 * G + b) * LQ
                            mm = nc.tensor.matmul(s_ps[:, t % 2, at:at + LQ], q_bd[h, g.c % 2, t // 2, b, :],
                                                  k_t[h, g.c % 2, t // 2, b * LQ:(b + 1) * LQ], start=True, stop=True)
                    mm.then_inc(s_made, 1)

                def turn_probs(g):
                    pe.wait_ge(probs_made, g.n + 1)
                    for t in range(T):
                        mm = nc.tensor.transpose(s_ps[:, t % 2, t // 2 * P:(t // 2 + 1) * P],
                                                 s_sb[:, g.c % 2, t * G:(t + 1) * G, :].rearrange("p b k -> p (b k)"), ident[:, :])
                    mm.then_inc(p_turned, 1)

                def attend(g, c):
                    pe.wait_ge(p_kept, g.n + 1)
                    pe.wait_ge(v_kept, g.n + 1)
                    if g.c or c:
                        pe.wait_ge(o_copied, g.n * 2 + c)
                    for t in (2 * c, 2 * c + 1):
                        for b in range(G):
                            mm = nc.tensor.matmul(o_ps[64 * (t % 2):64 * (t % 2) + 64, b * P:(b + 1) * P],
                                                  v_sb[:, g.c % 2, b, 64 * t:64 * t + 64], p_t[:, g.c % 2, t, :],
                                                  start=True, stop=True)
                    mm.then_inc(o_made, 1)

                def project_out(g):
                    pe.wait_ge(o_kept, g.n * 2 + 2)
                    pe.wait_ge(row_made, 2)
                    if g.c:
                        pe.wait_ge(r_exp_made, g.n)
                    for c in range(NC):
                        mm = nc.tensor.matmul(c_ps[:, 0:D], o_t[:, g.c % 2, c, :], w_proj[:, c, :], start=(c == 0), stop=(c == NC - 1))
                    mm.then_inc(y_made, 1)

                def turn_second(g):
                    pe.wait_ge(normed2, g.n + 1)
                    if g.c:
                        pe.wait_ge(eb_taken, g.n)
                    for c in range(NC):
                        mm = nc.tensor.transpose(c_ps[:, D + c * P:D + (c + 1) * P], xn2[:, g.c % 2, c * P:(c + 1) * P], ident[:, :])
                    mm.then_inc(turned2, 1)

                def route(g):
                    pe.wait_ge(kept2, g.n + 1)
                    for c in range(NC):
                        nc.tensor.matmul(c_ps[:, D:D + E], xt2[:, g.c % 2, c, :], w_rt[:, c, :], start=(c == 0), stop=False)
                    nc.tensor.matmul(c_ps[:, D:D + E], ones[:, :], b_rt[:, :], start=False, stop=True).then_inc(l_made, 1)

                def turn_gates(g, leads):
                    if leads:
                        pe.wait_ge(x2_made, g.n + 2)
                    else:
                        pe.wait_ge(r_exp_made, g.n + 1)
                    pe.wait_ge(gate_made, g.n + 1)
                    nc.tensor.transpose(c_ps[0:E, D:D + P], gate[:, g.c % 2, :], ident[:, :]).then_inc(gate_turned, 1)

                def gate_biases(g):
                    pe.wait_ge(gate_kept, g.n + 1)
                    nc.tensor.matmul(c_ps[:, 0:D], gate_t[:, :], b_exp[:, :], start=True, stop=True).then_inc(eb_made, 1)

                def experts(g, p):
                    if g.c < 2:
                        pe.wait_ge(e_in, 16)
                    if not (g.c == 0 and p < 2):
                        pe.wait_ge(e_taken, g.n * 4 + (p - 1))
                    for c in range(NC):
                        mm = nc.tensor.matmul(e_ps[:, p % 2, :], xt2[:, g.c % 2, c, :], w_exp[:, c, p * 512:(p + 1) * 512],
                                              start=(c == 0), stop=(c == NC - 1))
                    mm.then_inc(e_made, 1)

                def step(k, prepares, projects, attends, leads, ends):
                    nxt, last, done = k.plus(1), k.plus(-1), k.plus(-2)
                    if attends:
                        scores(k)
                    if projects:
                        turn_first(nxt)
                    if ends:
                        experts(done, 0)
                    if leads:
                        project_out(last)
                    if ends:
                        experts(done, 1)
                    if projects:
                        project_in(nxt)
                    if ends:
                        turn_gates(done, leads)
                    if attends:
                        turn_probs(k)
                    if ends:
                        gate_biases(done)
                        experts(done, 2)
                    if attends:
                        attend(k, 0)
                    if leads:
                        turn_second(last)
                    if ends:
                        experts(done, 3)
                    if attends:
                        attend(k, 1)
                    if leads:
                        route(last)
                steps(pe, step)

            @block.scalar
            def _(act):
                act.wait_ge(biases, 2)

                def keep_output(g, c):
                    act.wait_ge(o_made, g.n * 2 + (c + 1))
                    if g.c:
                        act.wait_ge(o_masked, g.n * 2 + (c - 1))
                    nc.scalar.activation(o_sb[:, c].rearrange("p b n -> p (b n)"), o_ps[:, :], ACT.Copy).then_inc(o_copied, 1)

                def keep_projections(g):
                    act.wait_ge(qk_made, g.n + 1)
                    if g.from_two():
                        act.wait_ge(bd_made, g.n - 1)
                        act.wait_ge(s_made, g.n - 1)
                    for m in range(NC):
                        nc.scalar.activation(q_t[:, g.c % 2, m, :], qk_ps[:, m * P:(m + 1) * P], ACT.Identity,
                                             bias=b_qs[:, m:m + 1], scale=SCALE)
                        ins = nc.scalar.activation(k_t[:, g.c % 2, m, :], qk_ps[:, D + m * P:D + (m + 1) * P], ACT.Identity,
                                                   bias=b_qk[:, 2 + m:3 + m])
                    ins.then_inc(qk_kept, 1)

                def keep_values(g):
                    act.wait_ge(v_made, g.n + 1)
                    if g.from_two():
                        act.wait_ge(o_made, g.n * 2 - 2)
                    for b in range(G):
                        ins = nc.scalar.activation(v_sb[:, g.c % 2, b, :], a_ps[:, D:2 * D], ACT.Copy,
                                                   scale=batch_mask[:, b:b + 1])
                    ins.then_inc(v_kept, 1)

                def step(k, prepares, projects, attends, leads, ends):
                    nxt, last, done = k.plus(1), k.plus(-1), k.plus(-2)
                    if projects:
                        act.wait_ge(turned1, nxt.n + 1)
                        nc.scalar.activation(xt1[:, nxt.c % 2].rearrange("p c n -> p (c n)"), a_ps[:, 0:D], ACT.Copy).then_inc(kept1, 1)
                    if attends:
                        act.wait_ge(masked, k.n + 1)
                        sv = s_sb[:, k.c % 2].rearrange("p r k -> p (r k)")
                        nc.scalar.activation(sv, sv, ACT.Exp).then_inc(exp_made, 1)
                    if projects:
                        keep_projections(nxt)
                    if ends:
                        act.wait_ge(gate_turned, done.n + 1)
                        nc.scalar.activation(gate_t[:, :], c_ps[0:E, D:D + P], ACT.Copy).then_inc(gate_kept, 1)
                    if attends:
                        act.wait_ge(p_turned, k.n + 1)
                        for u in range(2):
                            ins = nc.scalar.activation(p_t[:, k.c % 2, u::2, :],
                                                       s_ps[:, u, 0:2 * P].rearrange("p (t n) -> p t n", t=2), ACT.Copy)
                        ins.then_inc(p_kept, 1)
                    if projects:
                        keep_values(nxt)
                    if attends:
                        keep_output(k, 0)
                    if leads:
                        act.wait_ge(turned2, last.n + 1)
                        nc.scalar.activation(xt2[:, last.c % 2].rearrange("p c n -> p (c n)"), c_ps[:, D:2 * D], ACT.Copy
                                             ).then_inc(kept2, 1)
                    if attends:
                        keep_output(k, 1)
                    if leads:
                        act.wait_ge(r_top_made, last.n + 1)
                        nc.scalar.activation(r_exp[:, :], c_ps[:, D:D + E], ACT.Exp, bias=r_top[:, :], accum_out=r_den[:, :]
                                             ).then_inc(r_exp_made, 1)
                steps(act, step)

            @block.vector
            def _(dve):
                v = nc.vector
                dve.wait_ge(later_in, len(later) * 16)
                for c in range(NC):
                    ins = v.tensor_copy(b_vb[:, c, :], b_v[:, c:c + 1].to_broadcast([P, P]))
                ins.then_inc(biases, 1)
                v.tensor_scalar(b_qs[:, :], b_qk[:, 0:2], SCALE, None, ALU.mult).then_inc(biases, 1)

                class Chain:

                    def __init__(self, semaphore, per):
                        self.sem, self.per = semaphore, per

                    def start(self, g):
                        self.g, self.n = g, 0

                    def __call__(self, ins):
                        self.n += 1
                        ins.then_inc(self.sem, 1)
                        dve.wait_ge(self.sem, self.g.n * self.per + self.n)

                    def end(self):
                        assert self.n == self.per, self.n

                soft, first, second, route, total = Chain(softmax, 4), Chain(dve_first, 6), Chain(dve_second, 6), Chain(dve_route, 4), Chain(dve_total, 4)

                def tile_of_x(g):
                    return x_sb[:, g.n, :] if isinstance(g.n, int) else x_sb[:, bass.ds(g.n, 1), :].rearrange("p o d -> p (o d)")

                def first_statistics(g):
                    first.start(g)
                    first(v.bn_stats(st1[:, :], tile_of_x(g)))
                    dve.sem_inc(dve_waited, 1)
                    first(v.bn_aggr(mv1[:, :], st1[:, :]))
                    v.tensor_scalar(var1[:, :], mv1[:, 1:2], EPS, None, ALU.add).then_inc(var1_made, 1)
                    dve.wait_ge(var1_made, g.n + 1)

                def normalise_first(g):
                    dve.wait_ge(root1_made, g.n + 1)
                    first(v.tensor_tensor(half1[:, :], root1[:, :], root1[:, :], ALU.mult))
                    first(v.tensor_tensor(half1[:, :], half1[:, :], var1[:, :], ALU.mult))
                    first(v.tensor_scalar(half1[:, :], half1[:, :], -0.5, 1.5, ALU.mult, ALU.add))
                    first(v.tensor_tensor(half1[:, :], half1[:, :], root1[:, :], ALU.mult))
                    first.end()
                    if g.from_two():
                        dve.wait_ge(turned1, g.n - 1)
                    v.tensor_scalar(xn1[:, g.c % 2, :], tile_of_x(g), mv1[:, 0:1], half1[:, 0:1], ALU.subtract, ALU.mult
                                    ).then_inc(normed1, 1)

                def residual(g):
                    second.start(g)
                    x2t = x2[:, g.c % 2, :]
                    dve.wait_ge(y_made, g.n + 1)
                    dve.wait_ge(xr_made, g.n + 1)
                    v.tensor_tensor(x2t, c_ps[:, 0:D], xr[:, g.c % 2, :], ALU.add).then_inc(x2_made, 1)
                    dve.wait_ge(x2_made, g.n + 1)
                    second(v.bn_stats(st2[:, :], x2t))
                    dve.sem_inc(dve_waited, 1)
                    second(v.bn_aggr(mv2[:, :], st2[:, :]))
                    v.tensor_scalar(var2[:, :], mv2[:, 1:2], EPS, None, ALU.add).then_inc(var2_made, 1)
                    dve.wait_ge(var2_made, g.n + 1)

                def normalise_second(g):
                    dve.wait_ge(root2_made, g.n + 1)
                    second(v.tensor_tensor(half2[:, :], root2[:, :], root2[:, :], ALU.mult))
                    second(v.tensor_tensor(half2[:, :], half2[:, :], var2[:, :], ALU.mult))
                    second(v.tensor_scalar(half2[:, :], half2[:, :], -0.5, 1.5, ALU.mult, ALU.add))
                    second(v.tensor_tensor(half2[:, :], half2[:, :], root2[:, :], ALU.mult))
                    second.end()
                    if g.from_two():
                        dve.wait_ge(turned2, g.n - 1)
                    v.tensor_scalar(xn2[:, g.c % 2, :], x2[:, g.c % 2, :], mv2[:, 0:1], half2[:, 0:1], ALU.subtract, ALU.mult
                                    ).then_inc(normed2, 1)

                def mask_scores(g):
                    soft.start(g)
                    dve.wait_ge(s_made, g.n + 1)
                    sv = s_sb[:, g.c % 2]
                    for u in range(2):
                        for w in range(2):
                            t = 2 * w + u
                            ins = v.tensor_tensor(sv[:, t * G:(t + 1) * G, :],
                                                  s_ps[:, u, w * P:(w + 1) * P].rearrange("p (b k) -> p b k", k=LQ),
                                                  causal[:, :].unsqueeze(1).to_broadcast([P, G, LQ]), ALU.add)
                    soft(ins)
                    soft(v.tensor_reduce(top[:, :], sv, AX.X, ALU.max))
                    v.tensor_tensor(sv, sv, top[:, :].unsqueeze(2).to_broadcast([P, T * G, LQ]), ALU.subtract).then_inc(masked, 1)

                def normalise_probs(g):
                    dve.wait_ge(exp_made, g.n + 1)
                    sv = s_sb[:, g.c % 2]
                    soft(v.tensor_reduce(den[:, :], sv, AX.X, ALU.add))
                    soft(v.reciprocal(inv[:, :], den[:, :]))
                    v.tensor_tensor(sv, sv, inv[:, :].unsqueeze(2).to_broadcast([P, T * G, LQ]), ALU.mult).then_inc(probs_made, 1)

                def likeliest(g):
                    dve.wait_ge(l_made, g.n + 1)
                    v.tensor_reduce(r_top[:, :], c_ps[:, D:D + E], AX.X, ALU.max, negate=True).then_inc(r_top_made, 1)

                def gates(g):
                    route.start(g)
                    dve.wait_ge(r_exp_made, g.n + 1)
                    route(v.reciprocal(r_w[:, :], r_den[:, :]))
                    route(v.tensor_reduce(r_max[:, :], r_exp[:, :], AX.X, ALU.max))
                    route(v.scalar_tensor_tensor(r_sel[:, :], r_exp[:, :], r_max[:, 0:1], rank[:, :], ALU.is_ge, ALU.mult))
                    route(v.tensor_reduce(r_best[:, :], r_sel[:, :], AX.X, ALU.max))
                    if g.from_two():
                        dve.wait_ge(gate_turned, g.n - 1)
                    v.tensor_scalar(gate[:, g.c % 2, :], r_sel[:, :], r_best[:, 0:1], r_w[:, 0:1], ALU.is_ge, ALU.mult
                                    ).then_inc(gate_made, 1)
                    dve.wait_ge(gate_made, g.n + 1)
                    route.end()

                def combine(g, p):
                    at = acc[:, g.c % 2, :]
                    if p == 0:
                        total.start(g)
                        if g.from_two():
                            dve.wait_ge(stored[g.c % 2], g.half * 16)
                    dve.wait_ge(e_made, g.n * 4 + (p + 1))
                    for e in (2 * p, 2 * p + 1):
                        ins = v.scalar_tensor_tensor(at, e_ps[:, p % 2, (e % 2) * D:(e % 2 + 1) * D], gate[:, g.c % 2, e:e + 1],
                                                     x2[:, g.c % 2, :] if e == 0 else at, ALU.mult, ALU.add)
                        if e % 2 == 0:
                            total(ins)
                    ins.then_inc(e_taken, 1)
                    dve.wait_ge(e_taken, g.n * 4 + (p + 1))

                def add_biases(g):
                    dve.wait_ge(eb_made, g.n + 1)
                    at = acc[:, g.c % 2, :]
                    v.tensor_tensor(at, c_ps[:, 0:D], at, ALU.add).then_inc(eb_taken, 1)
                    dve.wait_ge(eb_taken, g.n + 1)

                def step(k, prepares, projects, attends, leads, ends):
                    last, done = k.plus(-1), k.plus(-2)
                    if attends:
                        mask_scores(k)
                    if ends:
                        gates(done)
                        combine(done, 0)
                    if attends:
                        normalise_probs(k)
                    if prepares:
                        first_statistics(k.plus(2))
                    if leads:
                        residual(last)
                    if ends:
                        combine(done, 1)
                    if leads:
                        normalise_second(last)
                    if ends:
                        add_biases(done)
                        combine(done, 2)
                    if prepares:
                        normalise_first(k.plus(2))
                    if k.c == -1:
                        dve.wait_ge(row_made, 1)
                        v.tensor_copy(row[:, :], c_ps[:, 0:D]).then_inc(row_made, 1)
                    if ends:
                        combine(done, 3)
                        total.end()
                    if leads:
                        likeliest(last)
                steps(dve, step)


def kernel(**inputs):
    import numpy as np
    import concourse.bacc as bacc
    from concourse.bass_utils import run_bass_kernel_spmd

    arrays = lay_out(**inputs)
    nc = bacc.Bacc("TRN2", target_bir_lowering=False, num_devices=1, dynamic_dma_scratch_size=1024)
    aps = {n: nc.dram_tensor(f"in_{n}", v.shape, F32, kind="ExternalInput").ap() for n, v in arrays.items()}
    out = nc.dram_tensor("out_x", (P, NG, D), F32, kind="ExternalOutput").ap()
    build(nc, aps, out)
    r = run_bass_kernel_spmd(nc, [{f"in_{n}": v for n, v in arrays.items()}], core_ids=[0])
    got = r.results[0]["out_x"]
    return np.ascontiguousarray(got.transpose(1, 0, 2)).reshape(B, LQ, D)


def lay_out(**inputs):
    import numpy as np

    i = {k: np.asarray(v) for k, v in inputs.items()}
    chunks = lambda w: w.reshape(NC, P, -1).transpose(1, 0, 2)
    column = lambda v: v.reshape(-1, P).T
    c = i["ctx_1024"]
    ctx_t = c.transpose(0, 2, 1).reshape(NG, G, NC, P, LK).transpose(0, 3, 1, 2, 4)
    channel = np.arange(P)
    arrays = {
        "x": i["x"].reshape(NG, P, D).transpose(1, 0, 2),
        "ctx_t": ctx_t,
        "ctx_last": c[:, LM, :].T.reshape(NC, P, B).transpose(1, 0, 2),
        "wq": chunks(i["L0_xattn_Wq"]), "wk": chunks(i["L0_xattn_Wk"]), "wv": chunks(i["L0_xattn_Wv"]),
        "wo": chunks(i["L0_xattn_Wo"]),
        "bq": column(i["L0_xattn_bq"]), "bk": column(i["L0_xattn_bk"]), "bv": column(i["L0_xattn_bv"]),
        "bo": i["L0_xattn_bo"].reshape(1, D),
        "w_qkv": chunks(i["L0_attn_W_attn"].T), "w_proj": chunks(i["L0_attn_W_proj"].T),
        "b_qk": column(i["L0_attn_b_attn"][:2 * D]), "b_v2": column(i["L0_attn_b_attn"][2 * D:]),
        "b_proj": i["L0_attn_b_proj"].reshape(1, D),
        "w_exp": chunks(i["L0_ffn_expert_w"].transpose(2, 0, 1).reshape(D, E * D)), "b_exp": i["L0_ffn_expert_b"],
        "w_rt": chunks(i["L0_ffn_router_w"].T), "b_rt": i["L0_ffn_router_b"].reshape(1, E),
        "causal": np.where(np.arange(LQ)[None, :] <= (channel % LQ)[:, None], 0.0, -1e30).astype(np.float32),
        "batch_mask": (channel[:, None] // LQ == np.arange(G)[None, :]).astype(np.float32),
        "rank": np.tile(E - np.arange(E, dtype=np.float32), (P, 1)),
        "ident": np.eye(P, dtype=np.float32),
        "quad_mask": (channel[:, None] % 64 // DH == np.arange(T)[None, :]).astype(np.float32),
    }
    return {n: np.ascontiguousarray(v) for n, v in arrays.items()}
```
